# Optimizing a Trainium2 kernel written in Bass

```python
import numpy as np
import jax
import jax.numpy as jnp

def _softmax(x, axis=-1):
    return jax.nn.softmax(x, axis=axis)

def _gelu(x):
    return jax.nn.gelu(x, approximate=True)

def _silu(x):
    return jax.nn.silu(x)

def _sigmoid(x):
    return jax.nn.sigmoid(x)

def _layernorm(x, axis=-1, eps=1e-05):
    m = jnp.mean(x, axis=axis, keepdims=True)
    v = jnp.var(x, axis=axis, keepdims=True)
    return (x - m) / jnp.sqrt(v + eps)

def _scatter_add(tgt, idx, src, axis=0):
    return tgt.at[idx].add(src)

def _segment_sum(src, seg, n):
    return jax.ops.segment_sum(src, seg, n)
kernel_name = 'mk_adaln_ffn_d2_seqx_r8_d753e0'

def setup_inputs(seed: int=0):
    np.random.seed(seed)
    _w = jnp.asarray

    def _rec_inputs():
        import jax
        import jax.numpy as jnp
        _rk = jax.random.key(seed)
        x = -0.003407 + 1.001 * jax.random.normal(jax.random.fold_in(_rk, 1), (4, 256, 256), jnp.float32)
        _lenS = 256 - jax.random.randint(jax.random.fold_in(_rk, 7), (4,), 0, max(1, 256 // 4) + 1, jnp.int32)
        _lenS2 = 256 - jax.random.randint(jax.random.fold_in(_rk, 8), (4,), 0, max(1, 256 // 4) + 1, jnp.int32)
        itok_Bx257_0_4111 = jax.random.randint(jax.random.fold_in(_rk, 11), (4, 257), 0, 514, jnp.int32)
        itok_B_37_3939 = jax.random.randint(jax.random.fold_in(_rk, 12), (4,), 37, 3940, jnp.int32)
        itok_B_0_6 = jax.random.randint(jax.random.fold_in(_rk, 13), (4,), 0, 7, jnp.int32)
        return (x, itok_Bx257_0_4111, itok_B_37_3939, itok_B_0_6)
    x, itok_Bx257_0_4111, itok_B_37_3939, itok_B_0_6 = _rec_inputs()

    def _L0_cond_setup():
        import jax, jax.numpy as jnp
        import numpy as np
        H, G, HD = (8, 4, 32)
        GSZ = H // G
        BLOCK = 16
        WINDOW = 128
        SCALE = 256.0 ** (-0.5)
        EPS = 1e-06
        THETA = 10000.0
        B, T, D = (16, 4, 256)
        NBLK = 257

        def _rms(x, scale):
            var = jnp.mean(x * x, axis=-1, keepdims=True)
            return x * jax.lax.rsqrt(var + EPS) * (1.0 + scale)

        def _rope(x, pos):
            half = HD // 2
            inv = 1.0 / THETA ** (jnp.arange(half, dtype=jnp.float32) / half)
            ang = pos[:, :, None].astype(jnp.float32) * inv
            cos = jnp.cos(ang)[:, None, :, :]
            sin = jnp.sin(ang)[:, None, :, :]
            x1, x2 = (x[..., :half], x[..., half:])
            return jnp.concatenate([x1 * cos - x2 * sin, x2 * cos + x1 * sin], axis=-1)
        key = jax.random.key(seed)
        ks = jax.random.split(key, 10)
        inv_d = 1.0 / np.sqrt(D)
        return {'x': jax.random.normal(ks[0], (B, T, D), jnp.float32), 'Wq': jax.random.normal(ks[1], (H * HD, D), jnp.float32) * inv_d, 'Wk': jax.random.normal(ks[2], (G * HD, D), jnp.float32) * inv_d, 'Wv': jax.random.normal(ks[3], (G * HD, D), jnp.float32) * inv_d, 'Wo': jax.random.normal(ks[4], (D, H * HD), jnp.float32) * inv_d, 'q_norm_scale': jax.random.normal(ks[5], (HD,), jnp.float32) * 0.02, 'k_norm_scale': jax.random.normal(ks[6], (HD,), jnp.float32) * 0.02, 'k_blocks': jax.random.normal(ks[7], (B * NBLK, G, BLOCK, HD), jnp.float32), 'v_blocks': jax.random.normal(ks[8], (B * NBLK, G, BLOCK, HD), jnp.float32), 'block_tables': jnp.arange(B * NBLK, dtype=jnp.int32).reshape(B, NBLK), 'kv_lens': jax.random.randint(ks[9], (B,), 0, 512, dtype=jnp.int32)}
    _L0_cond_all = _L0_cond_setup()
    _L0_cond_in = {k: v for k, v in _L0_cond_all.items() if k in ('Wq', 'Wk', 'Wv', 'Wo', 'q_norm_scale', 'k_norm_scale', 'k_blocks', 'v_blocks')}
    del _L0_cond_all

    def _L0_ffn_setup():
        import jax, jax.numpy as jnp
        import numpy as np
        QMAX = 127.0
        QMIN = -128.0
        key = jax.random.key(seed)
        k1, k2, k3 = jax.random.split(key, 3)
        B, N, D, O = (4, 512, 256, 256)
        x = jax.random.normal(k1, (B, N, D), dtype=jnp.float32)
        weight = jax.random.normal(k2, (O, D), dtype=jnp.float32)
        bias = jax.random.normal(k3, (O,), dtype=jnp.float32)
        return {'x': x, 'weight': weight, 'bias': bias}
    _L0_ffn_all = _L0_ffn_setup()
    _L0_ffn_in = {k: v for k, v in _L0_ffn_all.items() if k in ('weight', 'bias')}
    del _L0_ffn_all

    def _L1_cond_setup():
        import jax, jax.numpy as jnp
        import numpy as np
        B, T, D_IN, D_OUT = (16, 256, 256, 256)
        N_ADAPTERS, RANK = (8, 16)
        key = jax.random.key(seed)
        k_x, k_w, k_a, k_b, k_s, k_idx = jax.random.split(key, 6)
        x = jax.random.normal(k_x, (B, T, D_IN), dtype=jnp.float32)
        W = jax.random.normal(k_w, (D_OUT, D_IN), dtype=jnp.float32) * (1.0 / np.sqrt(D_IN))
        A = jax.random.normal(k_a, (N_ADAPTERS, RANK, D_IN), dtype=jnp.float32) * 0.02
        Bm = jax.random.normal(k_b, (N_ADAPTERS, D_OUT, RANK), dtype=jnp.float32) * 0.02
        scalings = jnp.ones((N_ADAPTERS,), dtype=jnp.float32)
        adapter_idx = jax.random.randint(k_idx, (B,), 0, N_ADAPTERS, dtype=jnp.int32)
        return {'x': x, 'W': W, 'A': A, 'Bm': Bm, 'scalings': scalings, 'adapter_idx': adapter_idx}
    _L1_cond_all = _L1_cond_setup()
    _L1_cond_in = {k: v for k, v in _L1_cond_all.items() if k in ('W', 'A', 'Bm', 'scalings')}
    del _L1_cond_all

    def _L1_ffn_setup():
        import jax, jax.numpy as jnp
        import numpy as np
        DIM = 256
        N_EXPERTS = 8
        TOP_K = 2
        key = jax.random.key(seed)
        ks = jax.random.split(key, 5)
        x = jax.random.normal(ks[0], (4, 512, DIM), dtype=jnp.float32)
        W_up = jax.random.normal(ks[1], (DIM, DIM), dtype=jnp.float32) * (1.0 / np.sqrt(DIM))
        W_down = jax.random.normal(ks[2], (DIM, DIM), dtype=jnp.float32) * (1.0 / np.sqrt(DIM))
        W_gate = jax.random.normal(ks[3], (N_EXPERTS, DIM), dtype=jnp.float32) * (1.0 / np.sqrt(DIM))
        W_expert = jax.random.normal(ks[4], (DIM, DIM), dtype=jnp.float32) * (1.0 / np.sqrt(DIM))
        return {'x': x, 'W_up': W_up, 'W_down': W_down, 'W_gate': W_gate, 'W_expert': W_expert}
    _L1_ffn_all = _L1_ffn_setup()
    _L1_ffn_in = {k: v for k, v in _L1_ffn_all.items() if k in ('W_up', 'W_down', 'W_gate', 'W_expert')}
    del _L1_ffn_all
    return {'x': x, 'itok_Bx257_0_4111': itok_Bx257_0_4111, 'itok_B_37_3939': itok_B_37_3939, 'itok_B_0_6': itok_B_0_6, 'L0_cond_Wq': _L0_cond_in['Wq'], 'L0_cond_Wk': _L0_cond_in['Wk'], 'L0_cond_Wv': _L0_cond_in['Wv'], 'L0_cond_Wo': _L0_cond_in['Wo'], 'L0_cond_q_norm_scale': _L0_cond_in['q_norm_scale'], 'L0_cond_k_norm_scale': _L0_cond_in['k_norm_scale'], 'L0_cond_k_blocks': _L0_cond_in['k_blocks'], 'L0_cond_v_blocks': _L0_cond_in['v_blocks'], 'L0_ffn_weight': _L0_ffn_in['weight'], 'L0_ffn_bias': _L0_ffn_in['bias'], 'L1_cond_W': _L1_cond_in['W'], 'L1_cond_A': _L1_cond_in['A'], 'L1_cond_Bm': _L1_cond_in['Bm'], 'L1_cond_scalings': _L1_cond_in['scalings'], 'L1_ffn_W_up': _L1_ffn_in['W_up'], 'L1_ffn_W_down': _L1_ffn_in['W_down'], 'L1_ffn_W_gate': _L1_ffn_in['W_gate'], 'L1_ffn_W_expert': _L1_ffn_in['W_expert']}

def reference(x, itok_Bx257_0_4111, itok_B_37_3939, itok_B_0_6, L0_cond_Wq, L0_cond_Wk, L0_cond_Wv, L0_cond_Wo, L0_cond_q_norm_scale, L0_cond_k_norm_scale, L0_cond_k_blocks, L0_cond_v_blocks, L0_ffn_weight, L0_ffn_bias, L1_cond_W, L1_cond_A, L1_cond_Bm, L1_cond_scalings, L1_ffn_W_up, L1_ffn_W_down, L1_ffn_W_gate, L1_ffn_W_expert):
    import jax
    import jax.numpy as jnp

    def _L0_cond_ref(x, Wq, Wk, Wv, Wo, q_norm_scale, k_norm_scale, k_blocks, v_blocks, block_tables, kv_lens):
        import jax, jax.numpy as jnp
        import numpy as np
        H, G, HD = (8, 4, 32)
        GSZ = H // G
        BLOCK = 16
        WINDOW = 128
        SCALE = 256.0 ** (-0.5)
        EPS = 1e-06
        THETA = 10000.0
        B, T, D = (16, 4, 256)
        NBLK = 257

        def _rms(x, scale):
            var = jnp.mean(x * x, axis=-1, keepdims=True)
            return x * jax.lax.rsqrt(var + EPS) * (1.0 + scale)

        def _rope(x, pos):
            half = HD // 2
            inv = 1.0 / THETA ** (jnp.arange(half, dtype=jnp.float32) / half)
            ang = pos[:, :, None].astype(jnp.float32) * inv
            cos = jnp.cos(ang)[:, None, :, :]
            sin = jnp.sin(ang)[:, None, :, :]
            x1, x2 = (x[..., :half], x[..., half:])
            return jnp.concatenate([x1 * cos - x2 * sin, x2 * cos + x1 * sin], axis=-1)
        Bx, Tx, _ = x.shape
        q = jnp.einsum('btd,od->bto', x, Wq).reshape(Bx, Tx, H, HD).transpose(0, 2, 1, 3)
        k = jnp.einsum('btd,od->bto', x, Wk).reshape(Bx, Tx, G, HD).transpose(0, 2, 1, 3)
        v = jnp.einsum('btd,od->bto', x, Wv).reshape(Bx, Tx, G, HD).transpose(0, 2, 1, 3)
        q = _rms(q, q_norm_scale)
        k = _rms(k, k_norm_scale)
        pos = kv_lens[:, None] + jnp.arange(Tx, dtype=jnp.int32)
        q = _rope(q, pos)
        k = _rope(k, pos)
        slot = pos // BLOCK
        off = pos % BLOCK
        blk = jnp.take_along_axis(block_tables, slot, axis=1)
        k_blocks = k_blocks.at[blk, :, off, :].set(k.transpose(0, 2, 1, 3))
        v_blocks = v_blocks.at[blk, :, off, :].set(v.transpose(0, 2, 1, 3))
        k_all = k_blocks[block_tables].transpose(0, 2, 1, 3, 4).reshape(Bx, G, -1, HD)
        v_all = v_blocks[block_tables].transpose(0, 2, 1, 3, 4).reshape(Bx, G, -1, HD)
        S = k_all.shape[2]
        qg = q.reshape(Bx, G, GSZ, Tx, HD)
        scores = jnp.einsum('bghtd,bgsd->bghts', qg, k_all) * SCALE
        kpos = jnp.arange(S, dtype=jnp.int32)
        allowed = (kpos[None, None, :] <= pos[:, :, None]) & (kpos[None, None, :] > pos[:, :, None] - WINDOW)
        scores = jnp.where(allowed[:, None, None, :, :], scores, -jnp.inf)
        p = jax.nn.softmax(scores, axis=-1)
        o = jnp.einsum('bghts,bgsd->bghtd', p, v_all).reshape(Bx, H, Tx, HD)
        o = o.transpose(0, 2, 1, 3).reshape(Bx, Tx, H * HD)
        return jnp.einsum('bto,do->btd', o, Wo)

    def _L0_ffn_ref(x, weight, bias):
        import jax, jax.numpy as jnp
        import numpy as np
        QMAX = 127.0
        QMIN = -128.0
        w_max = jnp.clip(jnp.max(jnp.abs(weight), axis=1, keepdims=True), 1e-08, None)
        w_scale = w_max / QMAX
        w_q = jnp.clip(jnp.round(weight / w_scale), QMIN, QMAX).astype(jnp.int8)
        w_scale = w_scale.squeeze(1).astype(jnp.float32)
        x_max = jnp.max(jnp.abs(x), axis=2, keepdims=True)
        x_scale = jnp.maximum(x_max / QMAX, 1e-12)
        x_q = jnp.clip(jnp.round(x / x_scale), QMIN, QMAX).astype(jnp.int8)
        acc = jnp.einsum('bnd,od->bno', x_q.astype(jnp.int32), w_q.astype(jnp.int32))
        y = acc.astype(jnp.float32) * x_scale.astype(jnp.float32) * w_scale[None, None, :]
        y = y + bias
        return y.astype(x.dtype)

    def _L1_cond_ref(x, W, A, Bm, scalings, adapter_idx):
        import jax, jax.numpy as jnp
        import numpy as np
        B, T, D_IN, D_OUT = (16, 256, 256, 256)
        N_ADAPTERS, RANK = (8, 16)
        H = jnp.einsum('btd,od->bto', x, W)
        A_b = A[adapter_idx]
        B_b = Bm[adapter_idx]
        s_b = scalings[adapter_idx]
        xa = jnp.einsum('btd,brd->btr', x, A_b)
        delta = jnp.einsum('btr,bor->bto', xa, B_b)
        delta = jax.lax.stop_gradient(delta * s_b[:, None, None])
        return H + delta

    def _L1_ffn_ref(x, W_up, W_down, W_gate, W_expert):
        import jax, jax.numpy as jnp
        import numpy as np
        DIM = 256
        N_EXPERTS = 8
        TOP_K = 2
        logits = jnp.einsum('bsd,ed->bse', x, W_gate)
        routing_weights, selected_experts = jax.lax.top_k(logits, TOP_K)
        shared_out = jnp.einsum('bsd,od->bso', jax.nn.relu(jnp.einsum('bsd,od->bso', x, W_up)), W_down)
        rw = jax.nn.softmax(routing_weights, axis=-1)
        expert_out = jnp.einsum('bsd,do->bso', x, W_expert)
        moe_out = jnp.sum(rw, axis=-1, keepdims=True) * expert_out
        return shared_out + moe_out
    x = x + _L0_ffn_ref(_L0_cond_ref(x, L0_cond_Wq, L0_cond_Wk, L0_cond_Wv, L0_cond_Wo, L0_cond_q_norm_scale, L0_cond_k_norm_scale, L0_cond_k_blocks, L0_cond_v_blocks, itok_Bx257_0_4111, itok_B_37_3939), L0_ffn_weight, L0_ffn_bias)
    x = x + _L1_ffn_ref(_L1_cond_ref(x, L1_cond_W, L1_cond_A, L1_cond_Bm, L1_cond_scalings, itok_B_0_6), L1_ffn_W_up, L1_ffn_W_down, L1_ffn_W_gate, L1_ffn_W_expert)
    return x

_drawn_inputs = setup_inputs


def setup_inputs(seed=0):
    import zlib

    import numpy as np

    out = dict(_drawn_inputs(seed))
    spreads = {'L1_cond_scalings': (1.0, 0.6)}
    factors = {'L0_cond_q_norm_scale': 7.724,
     'L0_cond_k_norm_scale': 7.455,
     'L1_cond_A': 3.178,
     'L1_cond_Bm': 3.156,
     'L1_ffn_W_gate': 8.0}
    for name, (base, spread) in spreads.items():
        noise = np.random.default_rng([zlib.crc32(name.encode()), seed]).standard_normal(out[name].shape)
        drawn = base * np.exp(spread * noise) if base else spread * noise
        out[name] = jnp.asarray(drawn.astype(out[name].dtype))
    for name, factor in factors.items():
        out[name] = (out[name] * factor).astype(out[name].dtype)
    return out
```

```python
from contextlib import ExitStack

import concourse.bass as bass
from concourse import mybir

F32 = mybir.dt.float32
BF16 = mybir.dt.bfloat16
I32 = mybir.dt.int32
U32 = mybir.dt.uint32
ALU = mybir.AluOpType
ACT = mybir.ActivationFunctionType
AX = mybir.AxisListType

P = 128
B, T, D = 4, 256, 256
U = T // P
NT = B * U
DC = D // P
H, G, HD = 8, 4, 32
GS = H // G
HALF = HD // 2
BLOCK, WINDOW = 16, 128
NBLK = 257
S_ALL = NBLK * BLOCK
KC = (WINDOW + T) // P
RB = 32
W0 = WINDOW // BLOCK
NW = T // BLOCK + 1
HB = WINDOW // BLOCK + 1
HR = HB * BLOCK
NEW = B * T
N_ADAPT, RANK = 8, 16
N_EXP = 8
EPS = 1e-6
SCALE = 256.0 ** -0.5
QMAX = 127.0
MAGIC = 1.5 * 2.0 ** 23
TWO_PI_HI = 6.28125
TWO_PI_MID = 0.0019340515136718750
TWO_PI_LO = 1.2556659146170633e-06
INV_TWO_PI = 0.15915494309189535
PI = 3.1415925

C_IDENT = 0
C_OLD = C_IDENT + P
C_OLD_T = C_OLD + P
C_NEW_T = C_OLD_T + P
C_BMASK = C_NEW_T + P
C_JKEY = C_BMASK + B
C_FALL = C_JKEY + KC
C_INV = C_FALL + B
C_POS = C_INV + HALF
C_ROW16 = C_POS + U
C_ROWS = C_ROW16 + 1
C_TOFF = C_ROWS + 1
C_ROWS_H = C_TOFF + 1
C_ADAPT = C_ROWS_H + 1
C_IOTA = C_ADAPT + 1
NCONST = C_IOTA + KC * P


def build(nc, x, tables, lens, adapters, wq, wk, wv, wo, q_scale, k_scale, k_blocks, v_blocks,
          w_int, bias, w1, lora_a, lora_b, scalings, w_up, w_down, w_gate, w_expert, consts, out):
    with ExitStack() as ctx:
        def sb(name, shape, dt=F32):
            return ctx.enter_context(nc.sbuf_tensor(name, shape, dt))

        def sem(name):
            return ctx.enter_context(nc.semaphore(name))

        def dram_view(t, pattern, offset=0):
            return bass.AP(t.tensor, offset, pattern)

        kv_rows = nc.dram_tensor("kv_rows", [NEW + B * HR, 2 * P], F32, kind="Internal").ap()

        bank = [ctx.enter_context(nc.psum_tensor(f"bank{i}", [P, 512], F32)) for i in range(2)]
        ps_scores = ctx.enter_context(nc.psum_tensor("ps_scores", [P, G, GS * 2 * P], F32))
        ps_turn = ctx.enter_context(nc.psum_tensor("ps_turn", [P, H, P], F32))
        ps_a, ps_b = bank

        cst = sb("cst", [P, NCONST])
        ident = cst[:, C_IDENT:C_IDENT + P]
        x_tok = sb("x_tok", [P, NT, D])
        w_qkv = sb("w_qkv", [P, 4, D])
        w_o = sb("w_o", [P, DC, D])
        w_i = sb("w_i", [P, DC, D])
        w_1 = sb("w_1", [P, DC, D])
        w_u = sb("w_u", [P, DC, D])
        w_d = sb("w_d", [P, DC, D])
        w_e = sb("w_e", [P, DC, D])
        w_g = sb("w_g", [N_EXP, D])
        a_all = sb("a_all", [P, D])
        b_all = sb("b_all", [P, DC, P])
        bias_bc = sb("bias_bc", [P, D])
        qk_scale = sb("qk_scale", [P, 2, HD])
        s_row = sb("s_row", [P, 1])
        ad_bc = sb("ad_bc", [P, B], I32)
        len_h = sb("len_h", [P, 1], I32)
        len_r = sb("len_r", [P, 1], I32)
        len_bc = sb("len_bc", [P, B], I32)
        tab_h = sb("tab_h", [P, NBLK], I32)
        tab_r = sb("tab_r", [P, NBLK], I32)

        wT_qkv = sb("wT_qkv", [P, DC, 512])
        wT_o = sb("wT_o", [P, DC, D])
        wT_i = sb("wT_i", [P, DC, D], BF16)
        wT_1 = sb("wT_1", [P, DC, D])
        wT_u = sb("wT_u", [P, DC, D])
        wT_d = sb("wT_d", [P, DC, D])
        wT_g = sb("wT_g", [P, DC, N_EXP])
        bT = sb("bT", [P, D])
        a_sel = sb("a_sel", [P, B, D])
        w_eff = sb("w_eff", [P, B, DC, D])
        w_round = w_i
        w_max = sb("w_max", [P, DC])
        w_inv = sb("w_inv", [P, DC])
        w_scale = sb("w_scale", [P, DC])
        w_scale_bc = sb("w_scale_bc", [P, D])
        sel = sb("sel", [P, B])
        x_bias = sb("x_bias", [P, NT, D])

        xT = sb("xT", [P, DC, NT, P])
        k_raw = sb("k_raw", [P, NT, P])
        k_sq = sb("k_sq", [P, NT, P])
        q_raw = sb("q_raw", [P, NT, D])
        q_sq = sb("q_sq", [P, NT, D])
        kv_new = sb("kv_new", [P, NT, 2 * P])
        pos = sb("pos", [P, B, U])
        ang = sb("ang", [P, 2, NT, HALF])
        turns = sb("turns", [P, 2, NT, HALF])
        trig = sb("trig", [P, 2, NT, HALF])
        cos_k, sin_k = sb("cos_k", [P, NT, HD]), sb("sin_k", [P, NT, HD])
        cos_q, sin_q = sb("cos_q", [P, NT, HD]), sb("sin_q", [P, NT, HD])
        var = sb("var", [P, NT * (G + H)])
        std = sb("std", [P, NT * (G + H)])
        rstd = sb("rstd", [P, NT * (G + H)])
        newton = sb("newton", [P, NT * (G + H)])
        rot_a = sb("rot_a", [P, 2 * U, D])
        rot_b = sb("rot_b", [P, 2 * U, D])

        slot = sb("slot", [P, 4])
        slot_i = sb("slot_i", [P, 4], I32)
        picked = sb("picked", [P, NBLK])
        blk_h = sb("blk_h", [P, 1])
        idx_h = sb("idx_h", [P, 1], I32)
        row = sb("row", [P, 12])
        (R_LEN, R_SLOT, R_BLK, R_U, R_U15, R_V, R_JMIN, R_JMAX, R_LO, R_HI) = range(10)
        abe = sb("abe", [P, 3])
        j_row = sb("j_row", [P, KC * P])
        in_row = sb("in_row", [P, KC * P])
        v_diag = sb("v_diag", [P, B])
        abe_bc = sb("abe_bc", [P, 3, B * NW])
        lim = sb("lim", [P, 4, B])
        low_i = sb("low_i", [P, B], I32)
        j_key = sb("j_key", [P, KC, B])
        valid = sb("valid", [P, KC, B])
        rid = sb("rid", [P, KC * B])
        m_ge = sb("m_ge", [P, KC * B, B * NW])
        m_le = sb("m_le", [P, KC * B, B * NW])
        cand = sb("cand", [P, KC * B, B * NW])
        win = sb("win", [P, KC, B])
        idx_f = sb("idx_f", [P, KC, B])
        fall = sb("fall", [P, 4, B])
        idx = sb("idx", [P, KC, B], I32)
        turned = sb("turned", [P, 3, 2 * H * P])
        probs = sb("probs", [P, 2, H, P])
        old_k = turned[0:B * HB, 2, :]
        old_v = probs[0:B * HB, :, :, :].rearrange("s r h t -> s (r h t)")
        old_rows = turned[0:B * HB, 0:2, :].rearrange("s k (o c) -> s (k o) c", c=2 * P)

        def view(t, pattern, **dims):
            return t[:, :, :].rearrange("p a b -> p (a b)").rearrange(pattern.replace("(", "p (", 1), **dims)

        kv = sb("kv", [P, B, KC, 2 * P])
        kT = sb("kT", [P, B, KC * P])
        v_aug = sb("v_aug", [P, B, KC, G, HD + 1])
        qT = sb("qT", [P, B, GS, T])
        q_rot = q_sq
        folded = view(q_raw, "(r h t) -> p r h t", r=2, h=H)
        shifted = folded
        neg_max = sb("neg_max", [P, 2, H])
        pT_all, pT_old, pT_new = (turned[:, k, :].rearrange("p (r h t) -> p r h t", r=2, h=H) for k in range(3))
        rden = sb("rden", [P, 2, H])
        o_tok, y_round, z_tok = (kv_new[:, 2 * k:2 * k + 2, :] for k in range(3))
        oT = kv_new[:, 6:8, :].rearrange("p r (c t) -> p r c t", c=DC)

        y_scale = sb("y_scale", [P, 2, 3])
        yT = sb("yT", [P, 2, DC, P], BF16)
        x1 = xT[:, 0, :, :].rearrange("p n t -> p (n t)").rearrange("p (k d) -> p k d", k=4)
        x1T = view(k_raw, "(r c t) -> p r c t", r=2, c=DC)
        hT = view(k_sq, "(r c t) -> p r c t", r=2, c=DC)
        rT = view(rot_a, "(r c t) -> p r c t", r=2, c=DC)
        top = sb("top", [P, U, 8])
        top_d = sb("top_d", [P, U, 2])
        top_e = sb("top_e", [P, U, 2])
        top_w = sb("top_w", [P, U, 2])
        top_s = sb("top_s", [P, 2, U])
        moe = view(rot_b, "(r u d) -> p r u d", r=2, u=U)
        y_out = xT[:, 1, :, :].rearrange("p n t -> p (n t)").rearrange("p (r u d) -> p r u d", r=2, u=U)

        consts_in, len_in, scales_in = sem("consts_in"), sem("len_in"), sem("scales_in")
        wqkv_in = sem("wqkv_in")
        x_in = [sem(f"x_in{b}") for b in range(B)]
        weights_in = {n: sem(f"{n}_in") for n in ("wo", "wi", "w1", "wu", "wd", "we", "wg", "lora_a", "lora_b", "bias")}
        old_in, old_out, new_out = sem("old_in"), sem("old_out"), sem("new_out")
        kv_in = [sem(f"kv_in{b}") for b in range(B)]
        stored = [sem(f"stored{k}") for k in range(2)]

        pe_wqkv, act_wqkv = sem("pe_wqkv"), sem("act_wqkv")
        pe_xT, act_xT = sem("pe_xT"), sem("act_xT")
        pe_kv, act_kv = sem("pe_kv"), sem("act_kv")
        pe_q, act_q = sem("pe_q"), sem("act_q")
        dve_ang, act_trig = sem("dve_ang"), sem("act_trig")
        dve_var, act_std = sem("dve_var"), sem("act_std")
        dve_k, dve_q = sem("dve_k"), sem("dve_q")
        dve_idx_h, act_old, pool_old = sem("dve_idx_h"), sem("act_old"), sem("pool_old")
        dve_rows, pe_rows, dve_rid, pool_cand, dve_idx = (
            sem("dve_rows"), sem("pe_rows"), sem("dve_rid"), sem("pool_cand"), sem("dve_idx"))
        pe_wT, act_wT = sem("pe_wT"), sem("act_wT")
        dve_wround, dve_bc, pool_sel, dve_eff = sem("dve_wround"), sem("dve_bc"), sem("pool_sel"), sem("dve_eff")
        dve_sel, pool_xb = sem("dve_sel"), sem("pool_xb")
        pe_qT, act_qT = sem("pe_qT"), sem("act_qT")
        pe_kT, act_kT, pool_v = sem("pe_kT"), sem("act_kT"), sem("pool_v")
        pe_scores, act_fold, dve_fold, dve_max = sem("pe_scores"), sem("act_fold"), sem("dve_fold"), sem("dve_max")
        pool_shift, act_exp, pe_pT = sem("pool_shift"), sem("act_exp"), sem("pe_pT")
        act_pT, dve_pT, pool_pT = sem("act_pT"), sem("dve_pT"), sem("pool_pT")
        pe_pv, dve_o, pe_oT, act_oT, pe_y = sem("pe_pv"), sem("dve_o"), sem("pe_oT"), sem("act_oT"), sem("pe_y")
        dve_yround, pe_yT, act_yT, pe_z, dve_x1 = (
            sem("dve_yround"), sem("pe_yT"), sem("act_yT"), sem("pe_z"), sem("dve_x1"))
        pe_x1T, act_x1T, pe_h, act_h, pe_u, act_u = (
            sem("pe_x1T"), sem("act_x1T"), sem("pe_h"), sem("act_h"), sem("pe_u"), sem("act_u"))
        pe_out, dve_gate, act_gate, dve_out = sem("pe_out"), sem("dve_gate"), sem("act_gate"), sem("dve_out")
        dve_chain = sem("dve_chain")

        ps_turn_lo = ps_turn[:, 0:4, :].rearrange("p (c v) t -> p c (v t)", c=DC)
        ps_turn_hi = ps_turn[:, 4:8, :].rearrange("p (c v) t -> p c (v t)", c=DC)
        wT_jobs = [(wT_o[:, :, :].rearrange("p c d -> p (c d)"), ps_scores[:, 0, :]),
                   (wT_i, ps_scores[:, 1, :]),
                   (wT_1[:, :, :].rearrange("p c d -> p (c d)"), ps_scores[:, 2, :]),
                   (wT_u[:, :, :].rearrange("p c d -> p (c d)"), ps_scores[:, 3, :]),
                   (wT_d[:, :, :].rearrange("p c d -> p (c d)"), bank[1][:, :]),
                   (bT[:, :], ps_turn[:, 0:2, :].rearrange("p c t -> p (c t)")),
                   (wT_g[:, :, :], ps_turn[:, 4, 0:DC * N_EXP].rearrange("p (c e) -> p c e", c=DC))]
        N_WT = len(wT_jobs)

        block = ctx.enter_context(nc.Block())

        @block.sync
        def _(sp):
            sp.dma_start(len_h[0:B * HB, :], dram_view(lens, [[1, B], [0, HB], [1, 1]])).then_inc(len_in, 16)
            sp.dma_start(tab_h[0:B * HB, :], dram_view(tables, [[NBLK, B], [0, HB], [1, NBLK]])).then_inc(len_in, 16)
            sp.dma_start(cst[:, 0:C_IOTA], consts[:, 0:C_IOTA]).then_inc(consts_in, 16)
            sp.dma_start(cst[:, C_IOTA:], consts[:, C_IOTA:]).then_inc(consts_in, 16)
            sp.dma_start(len_r[:, :], dram_view(lens, [[1, B], [0, RB], [1, 1]])).then_inc(len_in, 16)
            sp.dma_start(len_bc[:, :], dram_view(lens, [[0, P], [1, B]])).then_inc(len_in, 16)
            sp.dma_start(tab_r[:, :], dram_view(tables, [[NBLK, B], [0, RB], [1, NBLK]])).then_inc(len_in, 16)
            for b in range(B):
                sp.dma_start(x_tok[:, U * b:U * b + U, :],
                             x[b].rearrange("(u p) d -> p u d", p=P)).then_inc(x_in[b], 16)
            sp.dma_start(qk_scale[:, 0, :], dram_view(q_scale, [[0, P], [1, HD]])).then_inc(scales_in, 16)
            sp.dma_start(qk_scale[:, 1, :], dram_view(k_scale, [[0, P], [1, HD]])).then_inc(scales_in, 16)
            for half in range(2):
                sp.wait_ge(dve_k, half + 1)
                sp.wait_ge(act_kv, 4 * half + 4)
                n0 = 2 * U * half
                sp.dma_start(kv_rows[n0 * P:(n0 + 2 * U) * P, :].rearrange("(n p) c -> p n c", p=P),
                             kv_new[:, n0:n0 + 2 * U, :]).then_inc(new_out, 16)
            for b in range(B):
                sp.wait_ge(dve_out, U * b + U)
                sp.dma_start(out[b].rearrange("(u p) d -> p u d", p=P), y_out[:, b % 2, :, :]).then_inc(stored[b % 2], 16)
            for k in range(2):
                sp.wait_ge(stored[k], 16 * (B // 2))

        @block.gpsimd
        def _(pool):
            pool.wait_ge(dve_idx_h, 1)
            for dst, cache in ((old_k, k_blocks), (old_v, v_blocks)):
                pool.indirect_dma_start(out=dst[:, :], out_offset=None, in_=cache.rearrange("n g o d -> n (g o d)"),
                                        in_offset=bass.IndirectOffsetOnAxis(ap=idx_h[0:B * HB, 0:1], axis=0)
                                        ).then_inc(old_in, 16)
            pool.wait_ge(dve_sel, 1)
            pool.wait_ge(weights_in["lora_a"], 48)
            for b in range(B):
                pool.tensor_scalar(a_sel[:, b, :], a_all[:, :], sel[:, b:b + 1], None, ALU.mult).then_inc(pool_sel, 1)
            pool.wait_ge(old_in, 32)
            pool.tensor_copy(old_rows[:, :, P:2 * P].rearrange("s o (g d) -> s o g d", g=G),
                             old_v[:, :].rearrange("s (g o d) -> s o g d", g=G, o=BLOCK)).then_inc(pool_old, 1)
            pool.wait_ge(pool_old, 1)
            pool.wait_ge(act_old, 1)
            pool.dma_start(kv_rows[NEW:, :].rearrange("(s o) c -> s (o c)", o=BLOCK),
                           old_rows[:, :, :].rearrange("s o c -> s (o c)")).then_inc(old_out, 16)
            pool.wait_ge(dve_rid, 1)
            pool.tensor_tensor(cand[:, :, :], rid[:, :].unsqueeze(2).to_broadcast([P, KC * B, B * NW]),
                               abe_bc[:, 2, :].unsqueeze(1).to_broadcast([P, KC * B, B * NW]),
                               ALU.add).then_inc(pool_cand, 1)
            pool.wait_ge(dve_idx, 1)
            pool.wait_ge(new_out, 32)
            pool.wait_ge(old_out, 16)
            for b in range(B):
                for c in range(KC):
                    pool.indirect_dma_start(out=kv[:, b, c, :], out_offset=None, in_=kv_rows[:, :],
                                            in_offset=bass.IndirectOffsetOnAxis(ap=idx[:, c, b:b + 1], axis=0)
                                            ).then_inc(kv_in[b], 16)
            for b in range(B):
                pool.wait_ge(weights_in["bias"], 16)
                pool.wait_ge(x_in[b], 16)
                pool.tensor_tensor(x_bias[:, U * b:U * b + U, :], x_tok[:, U * b:U * b + U, :],
                                   bias_bc[:, :].unsqueeze(1).to_broadcast([P, U, D]), ALU.add).then_inc(pool_xb, 1)

            def values(b):
                pool.wait_ge(kv_in[b], 16 * KC)
                for c in range(KC):
                    pool.tensor_tensor(v_aug[:, b, c, :, 0:HD],
                                       kv[:, b, c, P:2 * P].rearrange("p (g d) -> p g d", g=G),
                                       valid[:, c, b:b + 1].unsqueeze(2).to_broadcast([P, G, HD]),
                                       ALU.mult).then_inc(pool_v, 1)
                pool.tensor_copy(v_aug[:, b, :, :, HD],
                                 valid[:, :, b:b + 1].to_broadcast([P, KC, G])).then_inc(pool_v, 1)

            values(0)
            for n in range(NT + 1):
                if n < NT:
                    r = n % 2
                    pool.wait_ge(dve_max, n + 1)
                    if n >= 2:
                        pool.wait_ge(act_exp, n - 1)
                    pool.tensor_tensor(shifted[:, r, :, :], folded[:, r, :, :],
                                       neg_max[:, r, :].unsqueeze(2).to_broadcast([P, H, P]),
                                       ALU.add).then_inc(pool_shift, 1)
                if n >= 1:
                    m, r = n - 1, (n - 1) % 2
                    pool.wait_ge(act_pT, m + 1)
                    if m >= 2:
                        pool.wait_ge(pe_pv, m - 1)
                    pool.tensor_tensor(pT_new[:, r, :, :], pT_all[:, r, :, :],
                                       cst[:, C_NEW_T:C_NEW_T + P].unsqueeze(1).to_broadcast([P, H, P]),
                                       ALU.mult).then_inc(pool_pT, 1)
                if n < NT and n % 2 == 0 and n // 2 + 1 < B:
                    values(n // 2 + 1)

        @block.scalar
        def _(act):
            act.dma_start(w_qkv[:, 0:2, :], wq.rearrange("(c p) d -> p c d", p=P)).then_inc(wqkv_in, 16)
            act.dma_start(w_qkv[:, 2, :], wk).then_inc(wqkv_in, 16)
            act.dma_start(w_qkv[:, 3, :], wv).then_inc(wqkv_in, 16)
            act.dma_start(a_all[:, :], lora_a.rearrange("n r d -> (n r) d")).then_inc(weights_in["lora_a"], 16)
            act.dma_start(s_row[:, :], dram_view(scalings, [[1, N_ADAPT], [0, RANK], [1, 1]])
                          ).then_inc(weights_in["lora_a"], 16)
            act.dma_start(ad_bc[:, :], dram_view(adapters, [[0, P], [1, B]])).then_inc(weights_in["lora_a"], 16)
            for name, dst, src in (("wo", w_o, wo), ("wi", w_i, w_int), ("w1", w_1, w1), ("wu", w_u, w_up),
                                   ("wd", w_d, w_down), ("we", w_e, w_expert)):
                act.dma_start(dst[:, :, :], src.rearrange("(c p) d -> p c d", p=P)).then_inc(weights_in[name], 16)
            for c in range(DC):
                act.dma_start(b_all[:, c, :].rearrange("p (n r) -> p n r", n=N_ADAPT),
                              lora_b[:, c * P:(c + 1) * P, :].rearrange("n p r -> p n r")
                              ).then_inc(weights_in["lora_b"], 16)
            act.dma_start(w_g[:, :], w_gate).then_inc(weights_in["wg"], 16)
            act.dma_start(bias_bc[:, :], dram_view(bias, [[0, P], [1, D]])).then_inc(weights_in["bias"], 16)

            for c in range(DC):
                act.wait_ge(pe_wqkv, c + 1)
                nc.scalar.copy(wT_qkv[:, c, 0:D].rearrange("p (i g d) -> p i g d", i=GS, g=G),
                               ps_scores[:, c, 0:D].rearrange("p (g i d) -> p i g d", g=G, i=GS)
                               ).then_inc(act_wqkv, 1)
                nc.scalar.copy(wT_qkv[:, c, D:], ps_scores[:, c, D:]).then_inc(act_wqkv, 1)
            for b in range(B):
                act.wait_ge(pe_xT, b + 1)
                nc.scalar.copy(xT[:, :, U * b:U * b + U, :],
                               ps_scores[:, 2 + b % 2, :].rearrange("p (c u t) -> p c u t", c=DC, u=U)
                               ).then_inc(act_xT, 1)
                if b == 1:
                    act.wait_ge(dve_ang, 1)
                    nc.scalar.activation(trig[:, :, :, :], ang[:, :, :, :], ACT.Sin).then_inc(act_trig, 1)
            for b in range(B):
                act.wait_ge(pe_kv, b + 1)
                kv_ps = bank[b % 2][:, :].rearrange("p (u c) -> p u c", u=U)
                tiles = slice(U * b, U * b + U)
                nc.scalar.activation(k_sq[:, tiles, :], kv_ps[:, :, 0:P], ACT.Square)
                nc.scalar.copy(k_raw[:, tiles, :], kv_ps[:, :, 0:P]).then_inc(act_kv, 1)
                nc.scalar.copy(kv_new[:, tiles, P:2 * P], kv_ps[:, :, P:2 * P]).then_inc(act_kv, 1)
                if b % 2 == 1:
                    half = b // 2
                    act.wait_ge(dve_var, half + 1)
                    seg = slice(2 * U * G * half, 2 * U * G * (half + 1))
                    nc.scalar.activation(std[:, seg], var[:, seg], ACT.Sqrt).then_inc(act_std, 1)
            act.wait_ge(old_in, 32)
            nc.scalar.copy(old_rows[:, :, 0:P].rearrange("s o (g d) -> s o g d", g=G),
                           old_k[:, :].rearrange("s (g o d) -> s o g d", g=G, o=BLOCK)).then_inc(act_old, 1)
            for b in range(B):
                act.wait_ge(pe_q, b + 1)
                q_ps = ps_scores[:, b % 2, :].rearrange("p (u c) -> p u c", u=U)
                tiles = slice(U * b, U * b + U)
                nc.scalar.activation(q_sq[:, tiles, :], q_ps, ACT.Square)
                nc.scalar.copy(q_raw[:, tiles, :], q_ps).then_inc(act_q, 1)
                if b % 2 == 1:
                    half = b // 2
                    act.wait_ge(dve_var, half + 3)
                    seg = slice(NT * G + 2 * U * H * half, NT * G + 2 * U * H * (half + 1))
                    nc.scalar.activation(std[:, seg], var[:, seg], ACT.Sqrt).then_inc(act_std, 1)
            for k, (dst, src) in enumerate(wT_jobs):
                act.wait_ge(pe_wT, k + 1)
                if dst is wT_i:
                    nc.scalar.activation(dst[:, :, :].rearrange("p c d -> p (c d)"), src, ACT.Copy,
                                         bias=-MAGIC).then_inc(act_wT, 1)
                else:
                    nc.scalar.copy(dst, src).then_inc(act_wT, 1)
            for b in range(B):
                act.wait_ge(pe_qT, b + 1)
                nc.scalar.copy(qT[:, b, :, :].rearrange("p i t -> p (i t)"), bank[b % 2][:, :]).then_inc(act_qT, 1)

            def keys(b):
                act.wait_ge(pe_kT, b + 1)
                nc.scalar.copy(kT[:, b, :], ps_a[:, 0:KC * P]).then_inc(act_kT, 1)

            keys(0)
            for n in range(NT + 4):
                r = n % 2
                if 1 <= n <= NT:
                    m, q = n - 1, (n - 1) % 2
                    act.wait_ge(pe_pT, m + 1)
                    if m >= 2:
                        act.wait_ge(pool_pT, m - 1)
                        act.wait_ge(dve_pT, m - 1)
                    nc.scalar.copy(pT_all[:, q, :, :], ps_turn[:, :, :]).then_inc(act_pT, 1)
                if n < NT:
                    act.wait_ge(pe_scores, n + 1)
                    if n >= 2:
                        act.wait_ge(pool_shift, n - 1)
                        act.wait_ge(dve_max, n - 1)
                    nc.scalar.copy(folded[:, r, :, :],
                                   ps_scores[:, :, :].rearrange("p g (i k) -> p (g i) k", i=GS)[:, :, P:2 * P]
                                   ).then_inc(act_fold, 1)
                if n >= 4 and n % 2 == 0:
                    act.wait_ge(dve_gate, n // 2 - 1)
                    nc.scalar.activation(top_e[:, :, :], top_d[:, :, :], ACT.Exp).then_inc(act_gate, 1)
                if 2 <= n < NT + 2:
                    m = n - 2
                    act.wait_ge(pe_x1T, m + 1)
                    u, f = m % 2, (m // 2) % 2
                    if m >= 4:
                        act.wait_ge(pe_h, m // 2 - 1)
                    nc.scalar.copy(x1T[:, f, :, u * P:(u + 1) * P],
                                   ps_b[:, 0:D].rearrange("p (c t) -> p c t", c=DC)).then_inc(act_x1T, 1)
                if 1 <= n <= NT:
                    m, q = n - 1, (n - 1) % 2
                    act.wait_ge(pe_oT, m + 1)
                    if m >= 2:
                        act.wait_ge(pe_y, m - 1)
                    nc.scalar.copy(oT[:, q, :, :].rearrange("p c t -> p (c t)"), ps_a[:, 0:D]).then_inc(act_oT, 1)
                if 3 <= n < NT + 3 and n % 2 == 1:
                    b = (n - 3) // 2
                    act.wait_ge(pe_h, b + 1)
                    nc.scalar.copy(hT[:, b % 2, :, :], ps_turn_lo).then_inc(act_h, 1)
                if n < NT:
                    act.wait_ge(pool_shift, n + 1)
                    if n >= 2:
                        act.wait_ge(pe_pT, n - 1)
                    nc.scalar.activation(probs[:, r, :, :], shifted[:, r, :, :], ACT.Exp).then_inc(act_exp, 1)
                if 3 <= n < NT + 3 and n % 2 == 1:
                    b = (n - 3) // 2
                    act.wait_ge(pe_u, b + 1)
                    nc.scalar.activation(rT[:, b % 2, :, :], ps_turn_hi, ACT.Relu).then_inc(act_u, 1)
                if 1 <= n <= NT:
                    m, q = n - 1, (n - 1) % 2
                    act.wait_ge(pe_yT, m + 1)
                    if m >= 2:
                        act.wait_ge(pe_z, m - 1)
                    nc.scalar.activation(yT[:, q, :, :].rearrange("p c t -> p (c t)"), ps_b[:, D:2 * D], ACT.Copy,
                                         bias=-MAGIC).then_inc(act_yT, 1)
                if n < NT and n % 2 == 0 and n // 2 + 1 < B:
                    keys(n // 2 + 1)

        @block.vector
        def _(dve):
            chain = [0]

            def link(ins):
                chain[0] += 1
                ins.then_inc(dve_chain, 1)
                dve.wait_ge(dve_chain, chain[0])

            dve.wait_ge(len_in, 80)
            dve.wait_ge(consts_in, 32)
            hb = slice(0, B * HB)
            link(dve.tensor_scalar(slot_i[hb, 0:1], len_h[hb, :], 4, None, ALU.logical_shift_right))
            link(dve.tensor_scalar(slot[hb, 0:1], slot_i[hb, 0:1], cst[hb, C_ROWS_H:C_ROWS_H + 1], None, ALU.add))
            link(dve.scalar_tensor_tensor(picked[hb, :], cst[hb, C_IOTA:C_IOTA + NBLK], slot[hb, 0:1], tab_h[hb, :],
                                          ALU.is_equal, ALU.mult, accum_out=blk_h[hb, :]))
            dve.tensor_copy(idx_h[hb, :], blk_h[hb, :]).then_inc(dve_idx_h, 1)

            link(dve.tensor_copy(lim[:, 0, :], len_bc[:, :]))
            link(dve.tensor_tensor(pos[:, :, :], lim[:, 0, :].unsqueeze(2).to_broadcast([P, B, U]),
                                   cst[:, C_POS:C_POS + U].unsqueeze(1).to_broadcast([P, B, U]), ALU.add))
            pos_n = pos[:, :, :].rearrange("p b u -> p (b u)")
            for k in range(2):
                last = dve.tensor_tensor(ang[:, k, :, :], pos_n.unsqueeze(2).to_broadcast([P, NT, HALF]),
                                         cst[:, C_INV:C_INV + HALF].unsqueeze(1).to_broadcast([P, NT, HALF]), ALU.mult)
            link(last)
            dve.tensor_scalar(turns[:, 0, :, :], ang[:, 0, :, :], INV_TWO_PI, MAGIC, ALU.mult, ALU.add)
            link(dve.tensor_scalar(turns[:, 1, :, :], ang[:, 1, :, :], INV_TWO_PI, 0.25, ALU.mult, ALU.add))
            link(dve.tensor_scalar(turns[:, 1, :, :], turns[:, 1, :, :], MAGIC, None, ALU.add))
            link(dve.tensor_scalar(turns[:, :, :, :], turns[:, :, :, :], MAGIC, None, ALU.subtract))
            for part in (TWO_PI_HI, TWO_PI_MID, TWO_PI_LO):
                link(dve.scalar_tensor_tensor(ang[:, :, :, :].rearrange("p k n i -> p (k n i)"),
                                              turns[:, :, :, :].rearrange("p k n i -> p (k n i)"), -part,
                                              ang[:, :, :, :].rearrange("p k n i -> p (k n i)"), ALU.mult, ALU.add))
            link(dve.tensor_scalar(ang[:, 1, :, :], ang[:, 1, :, :], 0.5 * 3.141592653589793, None, ALU.add))
            dve.tensor_scalar(ang[:, :, :, :], ang[:, :, :, :], PI, -PI, ALU.min, ALU.max).then_inc(dve_ang, 1)

            link(dve.tensor_scalar(slot_i[:, 1:2], len_r[:, :], 4, None, ALU.logical_shift_right))
            link(dve.tensor_scalar(slot_i[:, 2:3], len_r[:, :], 15, None, ALU.bitwise_and))
            link(dve.tensor_scalar(row[:, R_SLOT:R_SLOT + 1], slot_i[:, 1:2], cst[:, C_ROWS:C_ROWS + 1], None, ALU.add))
            link(dve.tensor_copy(row[:, R_LEN:R_LEN + 1], len_r[:, :]))

            def col(k):
                return row[:, k:k + 1]

            dve.scalar_tensor_tensor(picked[:, :], cst[:, C_IOTA:C_IOTA + NBLK], col(R_SLOT), tab_r[:, :],
                                     ALU.is_equal, ALU.mult, accum_out=col(R_BLK))
            link(dve.tensor_scalar(col(R_U), slot_i[:, 2:3], -1.0, cst[:, C_ROW16:C_ROW16 + 1], ALU.mult, ALU.add))
            dve.tensor_scalar(col(R_JMIN), col(R_LEN), -1.0, float(WINDOW), ALU.mult, ALU.add)
            link(dve.tensor_scalar(col(R_JMAX), col(R_LEN), -1.0, float(S_ALL - 1 + WINDOW), ALU.mult, ALU.add))
            link(dve.scalar_tensor_tensor(col(R_V), col(R_BLK), float(BLOCK), col(R_U), ALU.mult, ALU.subtract))
            link(dve.tensor_scalar(col(R_U15), col(R_U), BLOCK - 1.0, None, ALU.add))
            dve.tensor_scalar(col(R_LO), col(R_U), float(WINDOW), None, ALU.max)
            link(dve.tensor_scalar(col(R_HI), col(R_U15), float(KC * P - 1), col(R_JMAX), ALU.min, ALU.min))
            dve.tensor_tensor(abe[:, 0:1], col(R_V), col(R_LO), ALU.add)
            dve.tensor_tensor(abe[:, 1:2], col(R_V), col(R_HI), ALU.add)
            dve.tensor_tensor(abe[:, 2:3], cst[:, C_TOFF:C_TOFF + 1], col(R_V), ALU.subtract).then_inc(dve_rows, 1)
            dve.tensor_scalar(v_diag[:, :], cst[:, C_BMASK:C_BMASK + B], col(R_V), None, ALU.mult).then_inc(dve_rows, 1)
            link(dve.tensor_scalar(j_row[:, :], cst[:, C_IOTA:C_IOTA + KC * P], col(R_JMIN), col(R_JMAX),
                                   ALU.max, ALU.min))
            link(dve.tensor_scalar(in_row[:, :], j_row[:, :], col(R_U), None, ALU.is_ge))
            dve.scalar_tensor_tensor(in_row[:, :], j_row[:, :], col(R_U15), in_row[:, :],
                                     ALU.is_le, ALU.mult).then_inc(dve_rows, 1)
            dve.tensor_scalar(lim[:, 1, :], lim[:, 0, :], -1.0, float(WINDOW), ALU.mult, ALU.add)
            dve.tensor_scalar(lim[:, 2, :], lim[:, 0, :], -1.0, float(S_ALL - 1 + WINDOW), ALU.mult, ALU.add)
            link(dve.tensor_scalar(low_i[:, :], len_bc[:, :], 15, None, ALU.bitwise_and))
            link(dve.tensor_copy(lim[:, 3, :], low_i[:, :]))
            j_own = cst[:, C_JKEY:C_JKEY + KC].unsqueeze(2).to_broadcast([P, KC, B])
            link(dve.tensor_tensor(j_key[:, :, :], j_own, lim[:, 1, :].unsqueeze(1).to_broadcast([P, KC, B]), ALU.max))
            link(dve.tensor_tensor(j_key[:, :, :], j_key[:, :, :],
                                   lim[:, 2, :].unsqueeze(1).to_broadcast([P, KC, B]), ALU.min))
            link(dve.tensor_tensor(valid[:, :, :], j_own, j_key[:, :, :], ALU.is_equal))

            dve.wait_ge(scales_in, 32)
            link(dve.tensor_scalar(qk_scale[:, :, :], qk_scale[:, :, :], 1.0, None, ALU.add))
            link(dve.tensor_scalar(qk_scale[:, 0, :], qk_scale[:, 0, :], SCALE, None, ALU.mult))
            dve.wait_ge(act_trig, 1)

            def tables_of(which, cos_t, sin_t):
                for h in range(2):
                    sc = qk_scale[:, which, h * HALF:(h + 1) * HALF].unsqueeze(1).to_broadcast([P, NT, HALF])
                    other = slice((1 - h) * HALF, (2 - h) * HALF)
                    dve.tensor_tensor(cos_t[:, :, h * HALF:(h + 1) * HALF], trig[:, 1, :, :], sc, ALU.mult)
                    last = dve.tensor_tensor(sin_t[:, :, other], trig[:, 0, :, :], sc, ALU.mult)
                link(last)
                link(dve.tensor_scalar(sin_t[:, :, 0:HALF], sin_t[:, :, 0:HALF], -1.0, None, ALU.mult))

            tables_of(1, cos_k, sin_k)

            def norm_rope(raw, sq, heads, seg0, done, cos_t, sin_t, half, dst, signal):
                n0, nt = 2 * U * half, 2 * U
                m = nt * heads
                seg = slice(seg0 + m * half, seg0 + m * (half + 1))
                v4 = raw[:, n0:n0 + nt, :].rearrange("p n (h d) -> p n h d", d=HD)
                s4 = sq[:, n0:n0 + nt, :].rearrange("p n (h d) -> p (n h) d", d=HD)
                link(dve.tensor_reduce(var[:, seg], s4, AX.X, ALU.add))
                dve.tensor_scalar(var[:, seg], var[:, seg], 1.0 / HD, EPS, ALU.mult, ALU.add).then_inc(dve_var, 1)
                dve.wait_ge(act_std, done)
                link(dve.reciprocal(rstd[:, seg], std[:, seg]))
                link(dve.tensor_tensor(newton[:, seg], rstd[:, seg], rstd[:, seg], ALU.mult))
                link(dve.tensor_tensor(newton[:, seg], newton[:, seg], var[:, seg], ALU.mult))
                link(dve.tensor_scalar(newton[:, seg], newton[:, seg], -0.5, 1.5, ALU.mult, ALU.add))
                link(dve.tensor_tensor(rstd[:, seg], rstd[:, seg], newton[:, seg], ALU.mult))
                a4 = rot_a[:, :, 0:heads * HD].rearrange("p n (h d) -> p n h d", d=HD)
                b4 = rot_b[:, :, 0:heads * HD].rearrange("p n (h d) -> p n h d", d=HD)
                for n in range(nt):
                    rs = rstd[:, seg.start + n * heads:seg.start + (n + 1) * heads]
                    last = dve.tensor_tensor(a4[:, n], v4[:, n], rs.unsqueeze(2).to_broadcast([P, heads, HD]), ALU.mult)
                link(last)
                cs = cos_t[:, n0:n0 + nt, :].unsqueeze(2).to_broadcast([P, nt, heads, HD])
                for h in range(2):
                    here, there = slice(h * HALF, (h + 1) * HALF), slice((1 - h) * HALF, (2 - h) * HALF)
                    sn = sin_t[:, n0:n0 + nt, here].unsqueeze(2).to_broadcast([P, nt, heads, HALF])
                    last = dve.tensor_tensor(b4[:, :, :, here], a4[:, :, :, there], sn, ALU.mult)
                link(last)
                link(dve.tensor_tensor(a4, a4, cs, ALU.mult))
                out4 = dst[:, n0:n0 + nt, 0:heads * HD].rearrange("p n (h d) -> p n h d", d=HD)
                dve.tensor_tensor(out4, a4, b4, ALU.add).then_inc(signal, 1)
                dve.wait_ge(signal, half + 1)

            dve.wait_ge(weights_in["lora_a"], 48)
            dve.tensor_scalar(sel[:, :], ad_bc[:, :], cst[:, C_ADAPT:C_ADAPT + 1], s_row[:, 0:1],
                              ALU.is_equal, ALU.mult).then_inc(dve_sel, 1)

            for half in range(2):
                dve.wait_ge(act_kv, 4 * half + 4)
                norm_rope(k_raw, k_sq, G, 0, half + 1, cos_k, sin_k, half, kv_new, dve_k)

            dve.wait_ge(pe_rows, 2)
            dve.tensor_copy(abe_bc[:, :, :].rearrange("p k (b w) -> p k b w", b=B),
                            ps_turn[:, 0:3, :].rearrange("p k (b w) -> p k b w", b=B)[:, :, :, W0:W0 + NW])
            dve.tensor_tensor(rid[:, :], ps_turn[:, 4, 0:KC * B], j_key[:, :, :].rearrange("p c b -> p (c b)"),
                              ALU.add).then_inc(dve_rid, 1)
            dve.wait_ge(dve_rid, 1)
            rid_w = rid[:, :].unsqueeze(2).to_broadcast([P, KC * B, B * NW])
            dve.tensor_tensor(m_ge[:, :, :], rid_w, abe_bc[:, 0, :].unsqueeze(1).to_broadcast([P, KC * B, B * NW]),
                              ALU.is_ge)
            link(dve.tensor_tensor(m_le[:, :, :], rid_w,
                                   abe_bc[:, 1, :].unsqueeze(1).to_broadcast([P, KC * B, B * NW]), ALU.is_le))
            link(dve.tensor_tensor(m_ge[:, :, :], m_ge[:, :, :], m_le[:, :, :], ALU.mult))
            dve.wait_ge(pool_cand, 1)
            link(dve.tensor_tensor(m_ge[:, :, :], m_ge[:, :, :], cand[:, :, :], ALU.mult))
            link(dve.tensor_reduce(win[:, :, :].rearrange("p c b -> p (c b)"), m_ge[:, :, :], AX.X, ALU.max))
            link(dve.tensor_scalar(idx_f[:, :, :], win[:, :, :], -1.0, None, ALU.add))
            dve.tensor_tensor(fall[:, 0, :], j_key[:, 0, :], lim[:, 3, :], ALU.add)
            link(dve.tensor_scalar(fall[:, 1, :], win[:, 0, :], 0.0, None, ALU.is_gt))
            link(dve.tensor_tensor(fall[:, 0, :], fall[:, 0, :], cst[:, C_FALL:C_FALL + B], ALU.add))
            link(dve.tensor_tensor(fall[:, 2, :], idx_f[:, 0, :], fall[:, 0, :], ALU.subtract))
            link(dve.tensor_tensor(fall[:, 2, :], fall[:, 2, :], fall[:, 1, :], ALU.mult))
            link(dve.tensor_tensor(idx_f[:, 0, :], fall[:, 2, :], fall[:, 0, :], ALU.add))
            dve.tensor_copy(idx[:, :, :], idx_f[:, :, :]).then_inc(dve_idx, 1)

            dve.wait_ge(weights_in["wi"], 16)
            link(dve.tensor_reduce(w_max[:, :], w_i[:, :, :], AX.X, ALU.max, apply_absolute_value=True))
            link(dve.tensor_scalar(w_scale[:, :], w_max[:, :], 1e-8, 1.0 / QMAX, ALU.max, ALU.mult))
            link(dve.reciprocal(w_inv[:, :], w_scale[:, :]))
            for c in range(DC):
                last = dve.tensor_scalar(w_round[:, c, :], w_i[:, c, :], w_inv[:, c:c + 1], MAGIC, ALU.mult, ALU.add)
            link(last)
            dve.tensor_scalar(w_round[:, :, :], w_round[:, :, :], MAGIC + QMAX, MAGIC - QMAX - 1,
                              ALU.min, ALU.max).then_inc(dve_wround, 1)

            tables_of(0, cos_q, sin_q)
            for half in range(2):
                dve.wait_ge(act_q, 2 * half + 2)
                norm_rope(q_raw, q_sq, H, NT * G, half + 3, cos_q, sin_q, half, q_rot, dve_q)

            dve.wait_ge(pe_wT, N_WT + 1)
            dve.tensor_copy(w_scale_bc[:, :], ps_a[:, 0:D]).then_inc(dve_bc, 1)
            for b in range(B):
                dve.wait_ge(pe_wT, N_WT + 2 + b)
                dve.wait_ge(act_wT, N_WT)
                dve.tensor_tensor(w_eff[:, b, :, :], ps_scores[:, b, :].rearrange("p (c d) -> p c d", c=DC),
                                  wT_1[:, :, :], ALU.add).then_inc(dve_eff, 1)

            for n in range(NT + 4):
                r = n % 2
                if 1 <= n <= NT:
                    m, q = n - 1, (n - 1) % 2
                    dve.wait_ge(act_pT, m + 1)
                    if m >= 2:
                        dve.wait_ge(pe_pv, m - 1)
                    dve.tensor_tensor(pT_old[:, q, :, :], pT_all[:, q, :, :],
                                      cst[:, C_OLD_T:C_OLD_T + P].unsqueeze(1).to_broadcast([P, H, P]),
                                      ALU.mult).then_inc(dve_pT, 1)
                if n < NT:
                    dve.wait_ge(act_fold, n + 1)
                    dve.copy_predicated(folded[:, r, :, :],
                                        cst[:, C_OLD:C_OLD + P].bitcast(U32).unsqueeze(1).to_broadcast([P, H, P]),
                                        ps_scores[:, :, :].rearrange("p g (i k) -> p (g i) k", i=GS)[:, :, 0:P]
                                        ).then_inc(dve_fold, 1)
                    dve.wait_ge(dve_fold, n + 1)
                    if n >= 2:
                        dve.wait_ge(pool_shift, n - 1)
                    dve.tensor_reduce(neg_max[:, r, :], folded[:, r, :, :], AX.X, ALU.max,
                                      negate=True).then_inc(dve_max, 1)
                if n >= 4 and n % 2 == 0:
                    b = n // 2 - 2
                    f = b % 2
                    dve.wait_ge(pe_out, U * b + U)
                    for u in range(U):
                        last = dve.max(top[:, u, :], ps_a[:, H * (HD + 1) + 8 * u:H * (HD + 1) + 8 * u + 8])
                    link(last)
                    dve.tensor_tensor(top_d[:, :, :], top[:, :, 0:2], top[:, :, 0:1].to_broadcast([P, U, 2]),
                                      ALU.subtract).then_inc(dve_gate, 1)
                    dve.wait_ge(act_gate, b + 1)
                    link(dve.tensor_reduce(top_s[:, 0, :], top_e[:, :, :], AX.X, ALU.add))
                    link(dve.reciprocal(top_s[:, 0, :], top_s[:, 0, :]))
                    link(dve.tensor_tensor(top_w[:, :, :], top_e[:, :, :],
                                           top_s[:, 0, :].unsqueeze(2).to_broadcast([P, U, 2]), ALU.mult))
                    link(dve.tensor_reduce(top_s[:, 1, :], top_w[:, :, :], AX.X, ALU.add))
                    for u in range(U):
                        link(dve.scalar_tensor_tensor(moe[:, f, u, :], ps_turn_hi[:, u, :], top_s[:, 1, u:u + 1],
                                                      x1[:, (U * b + u) % 4, :], ALU.mult, ALU.add))
                    if b >= 2:
                        dve.wait_ge(stored[f], 16 * (b // 2))
                    for u in range(U):
                        dve.tensor_tensor(y_out[:, f, u, :], moe[:, f, u, :], ps_turn_lo[:, u, :],
                                          ALU.add).then_inc(dve_out, 1)
                if 2 <= n < NT + 2:
                    m, q = n - 2, n % 2
                    dve.wait_ge(pe_z, m + 1)
                    link(dve.scalar_tensor_tensor(z_tok[:, q, :], ps_b[:, 0:D], y_scale[:, q, 1:2], w_scale_bc[:, :],
                                                  ALU.mult, ALU.mult))
                    if m == 0:
                        dve.wait_ge(pool_xb, B)
                    dve.tensor_tensor(x1[:, m % 4, :], z_tok[:, q, :], x_bias[:, m, :], ALU.add).then_inc(dve_x1, 1)
                if 1 <= n <= NT:
                    m, q = n - 1, (n - 1) % 2
                    dve.wait_ge(pe_pv, m + 1)
                    o_ps = ps_a[:, 0:H * (HD + 1)].rearrange("p (h d) -> p h d", h=H)
                    link(dve.reciprocal(rden[:, q, :], o_ps[:, :, HD]))
                    if m >= 2:
                        dve.wait_ge(pe_oT, m - 1)
                    dve.tensor_tensor(o_tok[:, q, :].rearrange("p (h d) -> p h d", h=H), o_ps[:, :, 0:HD],
                                      rden[:, q, :].unsqueeze(2).to_broadcast([P, H, HD]), ALU.mult).then_inc(dve_o, 1)
                    dve.wait_ge(pe_y, m + 1)
                    link(dve.tensor_reduce(y_scale[:, q, 0:1], ps_b[:, 0:D], AX.X, ALU.max, apply_absolute_value=True))
                    link(dve.tensor_scalar(y_scale[:, q, 1:2], y_scale[:, q, 0:1], 1.0 / QMAX, 1e-12,
                                           ALU.mult, ALU.max))
                    link(dve.reciprocal(y_scale[:, q, 2:3], y_scale[:, q, 1:2]))
                    if m >= 2:
                        dve.wait_ge(pe_yT, m - 1)
                    link(dve.tensor_scalar(y_round[:, q, :], ps_b[:, 0:D], y_scale[:, q, 2:3], MAGIC,
                                           ALU.mult, ALU.add))
                    dve.tensor_scalar(y_round[:, q, :], y_round[:, q, :], MAGIC + QMAX, MAGIC - QMAX - 1,
                                      ALU.min, ALU.max).then_inc(dve_yround, 1)

        @block.tensor
        def _(pe):
            def mm(out_, lhsT, rhs, start=True, stop=True):
                return nc.tensor.matmul(out_, lhsT, rhs, start=start, stop=stop)

            def turn(out_, in_, rows=P):
                return nc.tensor.transpose(out_, in_, cst[0:rows, C_IDENT:C_IDENT + rows])

            pe.wait_ge(consts_in, 32)
            pe.wait_ge(wqkv_in, 48)
            for c in range(DC):
                for m in range(4):
                    last = turn(ps_scores[:, c, m * P:(m + 1) * P], w_qkv[:, m, c * P:(c + 1) * P])
                last.then_inc(pe_wqkv, 1)
            for b in range(B):
                pe.wait_ge(x_in[b], 16)
                if b >= 2:
                    pe.wait_ge(act_xT, b - 1)
                for c in range(DC):
                    for u in range(U):
                        last = turn(ps_scores[:, 2 + b % 2, (c * U + u) * P:(c * U + u + 1) * P],
                                    x_tok[:, U * b + u, c * P:(c + 1) * P])
                last.then_inc(pe_xT, 1)
            pe.wait_ge(act_wqkv, 2 * DC)
            for b in range(B):
                pe.wait_ge(act_xT, b + 1)
                if b >= 2:
                    pe.wait_ge(act_kv, 2 * (b - 1))
                for u in range(U):
                    for c in range(DC):
                        last = mm(bank[b % 2][:, u * D:(u + 1) * D], xT[:, c, U * b + u, :], wT_qkv[:, c, D:2 * D],
                                  start=(c == 0), stop=(c == DC - 1))
                last.then_inc(pe_kv, 1)
            pe.wait_ge(dve_rows, 3)
            for k in range(3):
                last = mm(ps_turn[:, k, :], abe[:, k:k + 1].to_broadcast([P, P]), ident)
            last.then_inc(pe_rows, 1)
            for c in range(KC):
                last = mm(ps_turn[:, 4, c * B:(c + 1) * B], in_row[:, c * P:(c + 1) * P], v_diag[:, :])
            last.then_inc(pe_rows, 1)
            for b in range(B):
                if b >= 2:
                    pe.wait_ge(act_q, b - 1)
                for u in range(U):
                    for c in range(DC):
                        last = mm(ps_scores[:, b % 2, u * D:(u + 1) * D], xT[:, c, U * b + u, :], wT_qkv[:, c, 0:D],
                                  start=(c == 0), stop=(c == DC - 1))
                last.then_inc(pe_q, 1)
            pe.wait_ge(act_q, B)
            for k, (name, w) in enumerate((("wo", w_o), ("wi", w_round), ("w1", w_1), ("wu", w_u), ("wd", w_d))):
                pe.wait_ge(weights_in[name], 16)
                if name == "wi":
                    pe.wait_ge(dve_wround, 1)
                for c in range(DC):
                    for m in range(DC):
                        where = bank[1][:, :] if name == "wd" else ps_scores[:, k, :]
                        last = turn(where[:, (c * DC + m) * P:(c * DC + m + 1) * P], w[:, m, c * P:(c + 1) * P])
                last.then_inc(pe_wT, 1)
            pe.wait_ge(weights_in["lora_b"], 32)
            pe.wait_ge(weights_in["wg"], 16)
            pe.wait_ge(dve_rid, 1)
            for c in range(DC):
                last = turn(ps_turn[:, c, :], b_all[:, c, :])
            last.then_inc(pe_wT, 1)
            for c in range(DC):
                last = turn(ps_turn[:, 4, c * N_EXP:(c + 1) * N_EXP], w_g[:, c * P:(c + 1) * P], rows=N_EXP)
            last.then_inc(pe_wT, 1)
            for m in range(DC):
                last = mm(ps_a[:, m * P:(m + 1) * P], w_scale[:, m:m + 1].to_broadcast([P, P]), ident)
            last.then_inc(pe_wT, 1)
            pe.wait_ge(act_wT, N_WT)
            for b in range(B):
                pe.wait_ge(pool_sel, b + 1)
                for c in range(DC):
                    last = mm(ps_scores[:, b, c * D:(c + 1) * D], a_sel[:, b, c * P:(c + 1) * P], bT[:, :])
                last.then_inc(pe_wT, 1)
            pe.wait_ge(dve_bc, 1)
            for b in range(B):
                pe.wait_ge(dve_q, b // 2 + 1)
                if b >= 2:
                    pe.wait_ge(act_qT, b - 1)
                for u in range(U):
                    for i in range(GS):
                        last = turn(bank[b % 2][:, (i * U + u) * P:(i * U + u + 1) * P], q_rot[:, U * b + u, i * P:(i + 1) * P])
                last.then_inc(pe_qT, 1)
            pe.wait_ge(act_qT, B)
            pe.wait_ge(dve_eff, B)

            def keys(b):
                pe.wait_ge(kv_in[b], 16 * KC)
                for c in range(KC):
                    last = turn(ps_a[:, c * P:(c + 1) * P], kv[:, b, c, 0:P])
                last.then_inc(pe_kT, 1)

            keys(0)
            for n in range(NT + 4):
                r = n % 2
                if n < NT:
                    b, u = n // U, n % U
                    pe.wait_ge(act_kT, b + 1)
                    if n >= 1:
                        pe.wait_ge(dve_fold, n)
                    for i in range(GS):
                        for g in range(G):
                            last = mm(ps_scores[:, g, i * 2 * P:(i + 1) * 2 * P],
                                      qT[g * HD:(g + 1) * HD, b, i, u * P:(u + 1) * P],
                                      kT[g * HD:(g + 1) * HD, b, u * P:(u + 2) * P])
                    last.then_inc(pe_scores, 1)
                if n >= 4 and n % 2 == 0:
                    b = n // 2 - 2
                    f = b % 2
                    pe.wait_ge(act_u, b + 1)
                    if n <= NT:
                        pe.wait_ge(act_pT, n)
                    pe.wait_ge(act_kT, min(n // 2 + 1, B))
                    for u in range(U):
                        tok = slice(u * P, (u + 1) * P)
                        for c in range(DC):
                            mm(ps_turn_lo[:, u, :], rT[:, f, c, tok], wT_d[:, c, :], start=(c == 0), stop=(c == DC - 1))
                        for c in range(DC):
                            mm(ps_turn_hi[:, u, :], hT[:, f, c, tok], w_e[:, c, :], start=(c == 0), stop=(c == DC - 1))
                        for c in range(DC):
                            last = mm(ps_a[:, H * (HD + 1) + 8 * u:H * (HD + 1) + 8 * u + 8], hT[:, f, c, tok],
                                      wT_g[:, c, :], start=(c == 0), stop=(c == DC - 1))
                        last.then_inc(pe_out, 1)
                if 2 <= n < NT + 2:
                    m, q = n - 2, n % 2
                    pe.wait_ge(act_yT, m + 1)
                    for c in range(DC):
                        last = mm(ps_b[:, 0:D], yT[:, q, c, :], wT_i[:, c, :], start=(c == 0), stop=(c == DC - 1))
                    last.then_inc(pe_z, 1)
                if 1 <= n <= NT:
                    m, q = n - 1, (n - 1) % 2
                    b, u = m // U, m % U
                    pe.wait_ge(pool_v, (KC + 1) * (b + 1))
                    pe.wait_ge(dve_pT, m + 1)
                    pe.wait_ge(pool_pT, m + 1)
                    pe.wait_ge(act_kT, min((n - 1) // 2 + 2, B))
                    if n >= 4 and n % 2 == 0:
                        pe.wait_ge(dve_gate, n // 2 - 1)
                    for h in range(H):
                        o_ps = ps_a[:, h * (HD + 1):(h + 1) * (HD + 1)]
                        mm(o_ps, pT_old[:, q, h, :], v_aug[:, b, u, h // GS, :], stop=False)
                        last = mm(o_ps, pT_new[:, q, h, :], v_aug[:, b, u + 1, h // GS, :], start=False)
                    last.then_inc(pe_pv, 1)
                if 2 <= n < NT + 2:
                    m = n - 2
                    pe.wait_ge(dve_x1, m + 1)
                    for c in range(DC):
                        last = turn(ps_b[:, c * P:(c + 1) * P], x1[:, m % 4, c * P:(c + 1) * P])
                    last.then_inc(pe_x1T, 1)
                if 1 <= n <= NT:
                    m, q = n - 1, (n - 1) % 2
                    pe.wait_ge(dve_o, m + 1)
                    for c in range(DC):
                        last = turn(ps_a[:, c * P:(c + 1) * P], o_tok[:, q, c * P:(c + 1) * P])
                    last.then_inc(pe_oT, 1)
                if 3 <= n < NT + 3 and n % 2 == 1:
                    b = (n - 3) // 2
                    pe.wait_ge(act_x1T, U * b + U)
                    if n <= NT:
                        pe.wait_ge(act_pT, n)
                    for m in range(DC):
                        for c in range(DC):
                            last = mm(ps_turn_lo[:, m, :], w_eff[:, b, c, m * P:(m + 1) * P], x1T[:, b % 2, c, :],
                                      start=(c == 0), stop=(c == DC - 1))
                    last.then_inc(pe_h, 1)
                if 1 <= n <= NT:
                    m, q = n - 1, (n - 1) % 2
                    pe.wait_ge(act_oT, m + 1)
                    if m >= 1:
                        pe.wait_ge(act_x1T, m)
                    for c in range(DC):
                        last = mm(ps_b[:, 0:D], oT[:, q, c, :], wT_o[:, c, :], start=(c == 0), stop=(c == DC - 1))
                    last.then_inc(pe_y, 1)
                if 3 <= n < NT + 3 and n % 2 == 1:
                    b = (n - 3) // 2
                    pe.wait_ge(act_h, b + 1)
                    for m in range(DC):
                        for c in range(DC):
                            last = mm(ps_turn_hi[:, m, :], wT_u[:, c, m * P:(m + 1) * P], hT[:, b % 2, c, :],
                                      start=(c == 0), stop=(c == DC - 1))
                    last.then_inc(pe_u, 1)
                if n < NT:
                    pe.wait_ge(act_exp, n + 1)
                    if n >= 4 and n % 2 == 0:
                        pe.wait_ge(dve_out, U * (n // 2 - 1))
                    if n >= 3 and n % 2 == 1:
                        pe.wait_ge(act_u, (n - 3) // 2 + 1)
                    for h in range(H):
                        last = turn(ps_turn[:, h, :], probs[:, r, h, :])
                    last.then_inc(pe_pT, 1)
                if 1 <= n <= NT:
                    m, q = n - 1, (n - 1) % 2
                    pe.wait_ge(dve_yround, m + 1)
                    for c in range(DC):
                        last = turn(ps_b[:, D + c * P:D + (c + 1) * P], y_round[:, q, c * P:(c + 1) * P])
                    last.then_inc(pe_yT, 1)
                if n < NT and n % 2 == 0 and n // 2 + 1 < B:
                    pe.wait_ge(act_kT, n // 2 + 1)
                    keys(n // 2 + 1)


def constants():
    import numpy as np
    c = np.zeros((P, NCONST), np.float32)
    p = np.arange(P)
    c[:, C_IDENT:C_IDENT + P] = np.eye(P)
    c[:, C_OLD:C_OLD + P] = p[None, :] > p[:, None]
    c[:, C_OLD_T:C_OLD_T + P] = p[:, None] > p[None, :]
    c[:, C_NEW_T:C_NEW_T + P] = p[:, None] <= p[None, :]
    c[:, C_BMASK:C_BMASK + B] = p[:, None] // RB == np.arange(B)[None, :]
    c[:, C_JKEY:C_JKEY + KC] = p[:, None] + P * np.arange(KC)[None, :]
    c[:, C_FALL:C_FALL + B] = NEW + HR * np.arange(B)[None, :]
    half = np.arange(HALF, dtype=np.float32) / np.float32(HALF)
    c[:, C_INV:C_INV + HALF] = np.float32(1.0) / np.power(np.float32(10000.0), half)
    c[:, C_POS:C_POS + U] = p[:, None] + P * np.arange(U)[None, :]
    c[:, C_ROW16] = BLOCK * (p % RB)
    c[:, C_ROWS] = p % RB - W0
    c[:, C_TOFF] = T * (p // RB) - WINDOW + 1
    c[:, C_ROWS_H] = p % HB - W0
    c[:, C_ADAPT] = p // RANK
    c[:, C_IOTA:] = np.arange(KC * P)[None, :]
    return c


_INS = ["x", "itok_Bx257_0_4111", "itok_B_37_3939", "itok_B_0_6", "L0_cond_Wq", "L0_cond_Wk", "L0_cond_Wv",
        "L0_cond_Wo", "L0_cond_q_norm_scale", "L0_cond_k_norm_scale", "L0_cond_k_blocks", "L0_cond_v_blocks",
        "L0_ffn_weight", "L0_ffn_bias", "L1_cond_W", "L1_cond_A", "L1_cond_Bm", "L1_cond_scalings",
        "L1_ffn_W_up", "L1_ffn_W_down", "L1_ffn_W_gate", "L1_ffn_W_expert"]


def kernel(**inputs):
    import numpy as np
    import concourse.bacc as bacc
    from concourse.bass_utils import run_bass_kernel_spmd

    nc = bacc.Bacc("TRN2", target_bir_lowering=False, num_devices=1)
    arrays, args = {}, []
    for name, a in [(n, inputs[n]) for n in _INS] + [("consts", constants())]:
        a = np.ascontiguousarray(a)
        arrays[f"in_{name}"] = a
        args.append(nc.dram_tensor(f"in_{name}", a.shape, mybir.dt.from_np(a.dtype), kind="ExternalInput").ap())
    args.append(nc.dram_tensor("out_x", (B, T, D), F32, kind="ExternalOutput").ap())
    build(nc, *args)
    r = run_bass_kernel_spmd(nc, [arrays], core_ids=[0])
    return r.results[0]["out_x"]
```

```python
from contextlib import ExitStack

import concourse.bass as bass
from concourse import mybir

F32 = mybir.dt.float32
BF16 = mybir.dt.bfloat16
I32 = mybir.dt.int32
U32 = mybir.dt.uint32
ALU = mybir.AluOpType
ACT = mybir.ActivationFunctionType
AX = mybir.AxisListType

P = 128
B, T, D = 4, 256, 256
U = T // P
NT = B * U
DC = D // P
H, G, HD = 8, 4, 32
GS = H // G
HALF = HD // 2
BLOCK, WINDOW = 16, 128
NBLK = 257
S_ALL = NBLK * BLOCK
KC = (WINDOW + T) // P
RB = 32
W0 = WINDOW // BLOCK
NW = T // BLOCK + 1
HB = WINDOW // BLOCK + 1
HR = HB * BLOCK
NEW = B * T
N_ADAPT, RANK = 8, 16
N_EXP = 8
EPS = 1e-6
SCALE = 256.0 ** -0.5
QMAX = 127.0
MAGIC = 1.5 * 2.0 ** 23
TWO_PI_HI = 6.28125
TWO_PI_MID = 0.0019340515136718750
TWO_PI_LO = 1.2556659146170633e-06
INV_TWO_PI = 0.15915494309189535
PI = 3.1415925
OUTSIDE = -1e38

C_IDENT = 0
C_OLD = C_IDENT + P
C_OLD_T = C_OLD + P
C_NEW_T = C_OLD_T + P
C_BMASK = C_NEW_T + P
C_JKEY = C_BMASK + B
C_FALL = C_JKEY + KC
C_INV = C_FALL + B
C_POS = C_INV + HALF
C_ROW16 = C_POS + U
C_ROWS = C_ROW16 + 1
C_TOFF = C_ROWS + 1
C_ROWS_H = C_TOFF + 1
C_ADAPT = C_ROWS_H + 1
NCONST = C_ADAPT + 1

W_Q, W_K, W_V = 0, D, D + G * HD
W_QKV = W_V + G * HD
W_O, W_1, W_UP, W_DOWN, W_EXP, W_GATE = (k * D for k in range(6))
W_REST = W_GATE + N_EXP

I_LEN, I_ADAPT, NINT = NBLK, NBLK + 1, NBLK + 2
F_QS, F_KS, NFLOAT = D, D + HD, D + 2 * HD
L_A, L_B, L_S, NLORA = 0, D, 2 * D, 2 * D + 1


def build(nc, x, x_turned, k_blocks, v_blocks, w_qkv_in, w_rest_in, w_int, lora, ints, floats, consts, out):
    with ExitStack() as ctx:
        def sb(name, shape, dt=F32):
            return ctx.enter_context(nc.sbuf_tensor(name, shape, dt))

        def sem(name):
            return ctx.enter_context(nc.semaphore(name))

        def dram_view(t, pattern, offset=0):
            return bass.AP(t.tensor, offset, pattern)

        kv_rows = nc.dram_tensor("kv_rows", [NEW + B * HR, 2 * P], F32, kind="Internal").ap()

        ps_scores = ctx.enter_context(nc.psum_tensor("ps_scores", [P, G, GS * 2 * P], F32))
        ps_turn = ctx.enter_context(nc.psum_tensor("ps_turn", [P, 2, 512], F32))
        ps_a = ctx.enter_context(nc.psum_tensor("ps_a", [P, 512], F32))
        ps_b = ctx.enter_context(nc.psum_tensor("ps_b", [P, 512], F32))

        cst = sb("cst", [P, NCONST])
        ident = cst[:, C_IDENT:C_IDENT + P]
        iota = sb("iota", [P, KC * P])
        ones = sb("ones", [P, P], BF16)
        x_tok = sb("x_tok", [P, NT, D])
        xT = sb("xT", [P, DC, B, T])
        w_qkv = sb("w_qkv", [P, DC, W_QKV])
        w_rest = sb("w_rest", [P, DC, W_REST])
        w_i = sb("w_i", [P, DC, D])
        lora_sb = sb("lora_sb", [P, NLORA])
        row_bc = sb("row_bc", [P, NFLOAT])
        bias_bc = row_bc[:, 0:D]
        tab_h = sb("tab_h", [P, NINT], I32)
        tab_r = sb("tab_r", [P, NINT], I32)
        ints_bc = sb("ints_bc", [P, B, 2], I32)

        wT_i = sb("wT_i", [P, DC, D], BF16)
        a_sel = sb("a_sel", [P, B, D])
        w_eff = sb("w_eff", [P, B, DC, D])
        w_max = sb("w_max", [P, DC])
        w_inv = sb("w_inv", [P, DC])
        w_scale = sb("w_scale", [P, DC])
        w_scale_bc = sb("w_scale_bc", [P, D])
        sel = sb("sel", [P, B])
        x_bias = x_tok

        k_raw = sb("k_raw", [P, NT, P])
        k_sq = sb("k_sq", [P, NT, P])
        q_raw = sb("q_raw", [P, NT, D])
        q_sq = sb("q_sq", [P, NT, D])
        q_rot = q_sq
        kv_new = sb("kv_new", [P, NT, 2 * P])
        len_f = sb("len_f", [P, B])
        pos = sb("pos", [P, B, U])
        ang = sb("ang", [P, 2, NT * HALF])
        turns = sb("turns", [P, 2, NT * HALF])
        part = sb("part", [P, 2, NT * HALF])
        trig = sb("trig", [P, 2, NT, HALF])
        cos_k, sin_k = sb("cos_k", [P, NT, HD]), sb("sin_k", [P, NT, HD])
        cos_q, sin_q = sb("cos_q", [P, NT, HD]), sb("sin_q", [P, NT, HD])
        qk_scale = sb("qk_scale", [P, 2, HD])
        var = sb("var", [P, NT * (G + H)])
        std = sb("std", [P, NT * (G + H)])
        rstd = sb("rstd", [P, NT * (G + H)])
        newton = sb("newton", [P, NT * (G + H)])
        rot_a = sb("rot_a", [P, 4, D])
        rot_b = sb("rot_b", [P, 4, D])

        slot = sb("slot", [P, 4])
        slot_i = sb("slot_i", [P, 4], I32)
        picked = sb("picked", [P, NBLK])
        blk_h = sb("blk_h", [P, 1])
        idx_h = sb("idx_h", [P, 1], I32)
        row = sb("row", [P, 12])
        (R_LEN, R_SLOT, R_BLK, R_U, R_U15, R_V, R_JMIN, R_JMAX, R_LO, R_HI) = range(10)
        abe = sb("abe", [P, 3])
        j_row = sb("j_row", [P, KC * P])
        in_row = sb("in_row", [P, KC * P])
        v_diag = sb("v_diag", [P, B])
        abe_bc = sb("abe_bc", [P, 3, B * NW])
        j_min, j_max, low = sb("j_min", [P, B]), sb("j_max", [P, B]), sb("low", [P, B])
        low_i = sb("low_i", [P, B], I32)
        j_key = sb("j_key", [P, KC, B])
        rid = sb("rid", [P, KC * B])
        m_ge = sb("m_ge", [P, KC * B, B * NW])
        m_le = sb("m_le", [P, KC * B, B * NW])
        cand = sb("cand", [P, KC * B, B * NW])
        win = sb("win", [P, KC, B])
        idx_f = sb("idx_f", [P, KC, B])
        fall = sb("fall", [P, 3, B])
        idx = sb("idx", [P, KC, B], I32)
        penalty = sb("penalty", [P, B, U, P], BF16)

        def view(t, pattern, **dims):
            return t[:, :, :].rearrange("p a b -> p (a b)").rearrange(pattern.replace("(", "p (", 1), **dims)

        kv = sb("kv", [P, B, KC, 2 * P])
        kT = sb("kT", [P, 2, KC * P])
        qT = sb("qT", [P, 2, GS, T])
        turned = sb("turned", [P, 2, 2 * H * P])
        pT_old, pT_new = (turned[:, k, :].rearrange("p (r h t) -> p r h t", r=2, h=H) for k in range(2))
        probs = sb("probs", [P, 2, H, P])
        folded = sb("folded", [P, 2, H, P])
        old_k = folded[0:B * HB, :, :, :].rearrange("s r h t -> s (r h t)")
        old_v = probs[0:B * HB, :, :, :].rearrange("s r h t -> s (r h t)")
        old_rows = turned[0:B * HB, :, :].rearrange("s k (o c) -> s (k o) c", c=2 * P)
        neg_max = sb("neg_max", [P, 2, H])
        den = sb("den", [P, 2, H])
        rden = sb("rden", [P, 2, H])

        y_round, z_tok = (kv_new[:, 2 * k:2 * k + 2, :] for k in range(2))
        oT = kv_new[:, 6:8, :].rearrange("p r (c t) -> p r c t", c=DC)
        y_scale = sb("y_scale", [P, 2, 3])
        yT = sb("yT", [P, 2, DC, P], BF16)
        x1 = xT[:, 0, :, :]
        y_out = xT[:, 1, :, :].rearrange("p b t -> p (b t)").rearrange("p (r u d) -> p r u d", r=2, u=U)
        x1T = view(k_raw, "(r c t) -> p r c t", r=2, c=DC)
        hT = view(k_sq, "(r c t) -> p r c t", r=2, c=DC)
        rT = view(rot_a, "(r c t) -> p r c t", r=2, c=DC)
        moe = sb("moe", [P, 2, U, D])
        top = sb("top", [P, U, 8])
        top_d = sb("top_d", [P, U, 2])
        top_e = sb("top_e", [P, U, 2])
        top_w = sb("top_w", [P, U, 2])
        top_s = sb("top_s", [P, U, 3])

        consts_in, tab_h_in, tab_r_in, ints_in = sem("consts_in"), sem("tab_h_in"), sem("tab_r_in"), sem("ints_in")
        row_in, wqkv_in, lora_in, wi_in = sem("row_in"), sem("wqkv_in"), sem("lora_in"), sem("wi_in")
        wrest_in = [sem(f"wrest_in{k}") for k in range(2)]
        xT_in = [sem(f"xT_in{b}") for b in range(B)]
        x_in = sem("x_in")
        old_in, old_out, new_out = sem("old_in"), sem("old_out"), sem("new_out")
        kv_in = [sem(f"kv_in{b}") for b in range(B)]
        stored = [sem(f"stored{k}") for k in range(2)]

        pool_iota, pool_ang, act_trig = sem("pool_iota"), sem("pool_ang"), sem("act_trig")
        pe_kv, act_kv, pe_q, act_q = sem("pe_kv"), sem("act_kv"), sem("pe_q"), sem("act_q")
        dve_var, act_std = sem("dve_var"), sem("act_std")
        dve_k, dve_q = sem("dve_k"), sem("dve_q")
        dve_idx_h, act_old = sem("dve_idx_h"), sem("act_old")
        dve_rows, pe_rows, dve_rid, pool_cand, dve_idx = (
            sem("dve_rows"), sem("pe_rows"), sem("dve_rid"), sem("pool_cand"), sem("dve_idx"))
        dve_lim, pool_pen = sem("dve_lim"), sem("pool_pen")
        dve_sel, pool_sel, pe_eff, act_eff, pool_eff = (
            sem("dve_sel"), sem("pool_sel"), sem("pe_eff"), sem("act_eff"), sem("pool_eff"))
        dve_wscale, dve_wround, pe_wi, act_wi = sem("dve_wscale"), sem("dve_wround"), sem("pe_wi"), sem("act_wi")
        pool_xb = sem("pool_xb")
        pe_qT, act_qT, pe_kT, act_kT = sem("pe_qT"), sem("act_qT"), sem("pe_kT"), sem("act_kT")
        pe_scores, act_fold, dve_fold, dve_max = sem("pe_scores"), sem("act_fold"), sem("dve_fold"), sem("dve_max")
        act_exp, dve_probs, pe_pT, dve_pT = sem("act_exp"), sem("dve_probs"), sem("pe_pT"), sem("dve_pT")
        pe_pv, act_oT, pe_y = sem("pe_pv"), sem("act_oT"), sem("pe_y")
        dve_yround, pe_yT, act_yT, pe_z, dve_x1 = (
            sem("dve_yround"), sem("pe_yT"), sem("act_yT"), sem("pe_z"), sem("dve_x1"))
        pe_x1T, act_x1T, pe_h, act_h, pe_u, act_u = (
            sem("pe_x1T"), sem("act_x1T"), sem("pe_h"), sem("act_h"), sem("pe_u"), sem("act_u"))
        pe_out, dve_gate, act_gate, dve_out = sem("pe_out"), sem("dve_gate"), sem("act_gate"), sem("dve_out")
        pool_chain, dve_chain = sem("pool_chain"), sem("dve_chain")

        q_bank = [ps_a[:, :], ps_b[:, :], ps_scores[:, 0, :], ps_scores[:, 1, :]]
        eff_bank = [ps_scores[:, 2, :], ps_scores[:, 3, :], ps_a[:, :], ps_b[:, :]]

        block = ctx.enter_context(nc.Block())

        @block.sync
        def _(sp):
            sp.dma_start(tab_h[0:B * HB, :], dram_view(ints, [[NINT, B], [0, HB], [1, NINT]])).then_inc(tab_h_in, 16)
            sp.dma_start(ints_bc[:, :, :], dram_view(ints, [[0, P], [NINT, B], [1, 2]], I_LEN)).then_inc(ints_in, 16)
            sp.dma_start(cst[:, :], consts).then_inc(consts_in, 16)
            for b in range(B):
                sp.dma_start(xT[:, :, b, :], x_turned[b].rearrange("(c p) t -> p c t", p=P)).then_inc(xT_in[b], 16)
            sp.dma_start(row_bc[:, :], dram_view(floats, [[0, P], [1, NFLOAT]])).then_inc(row_in, 16)
            sp.dma_start(w_i[:, :, :], w_int.rearrange("(c p) d -> p c d", p=P)).then_inc(wi_in, 16)
            sp.dma_start(x_tok[:, :, :], x.rearrange("b (u p) d -> p (b u) d", p=P)).then_inc(x_in, 16)
            rest = w_rest_in.rearrange("(c p) d -> p c d", p=P)
            for k, (a, z) in enumerate(((0, 2 * D), (2 * D, W_REST))):
                sp.dma_start(w_rest[:, :, a:z], rest[:, :, a:z]).then_inc(wrest_in[k], 16)
            for half in range(2):
                sp.wait_ge(dve_k, half + 1)
                sp.wait_ge(act_kv, 4 * half + 4)
                n0 = 2 * U * half
                sp.dma_start(kv_rows[n0 * P:(n0 + 2 * U) * P, :].rearrange("(n p) c -> p n c", p=P),
                             kv_new[:, n0:n0 + 2 * U, :]).then_inc(new_out, 16)
            for b in range(B):
                sp.wait_ge(dve_out, U * b + U)
                sp.dma_start(out[b].rearrange("(u p) d -> p u d", p=P), y_out[:, b % 2, :, :]
                             ).then_inc(stored[b % 2], 16)
            for k in range(2):
                sp.wait_ge(stored[k], 16 * (B // 2))

        @block.gpsimd
        def _(pool):
            chain = [0]

            def link(ins):
                chain[0] += 1
                ins.then_inc(pool_chain, 1)
                pool.wait_ge(pool_chain, chain[0])

            pool.iota(iota[:, :], [[1, KC * P]], base=0, channel_multiplier=0,
                      allow_small_or_imprecise_dtypes=True).then_inc(pool_iota, 1)
            link(pool.memset(ones[:, :], 1.0))
            pool.wait_ge(ints_in, 16)
            pool.wait_ge(consts_in, 16)
            link(pool.tensor_copy(len_f[:, :], ints_bc[:, :, 0]))
            link(pool.tensor_tensor(pos[:, :, :], len_f[:, :].unsqueeze(2).to_broadcast([P, B, U]),
                                    cst[:, C_POS:C_POS + U].unsqueeze(1).to_broadcast([P, B, U]), ALU.add))
            pos_n = pos[:, :, :].rearrange("p b u -> p (b u)").unsqueeze(2).to_broadcast([P, NT, HALF])
            inv_n = cst[:, C_INV:C_INV + HALF].unsqueeze(1).to_broadcast([P, NT, HALF])
            for k in range(2):
                last = pool.tensor_tensor(ang[:, k, :].rearrange("p (n i) -> p n i", n=NT), pos_n, inv_n, ALU.mult)
            link(last)
            pool.tensor_scalar(turns[:, 0, :], ang[:, 0, :], INV_TWO_PI, 0.0, ALU.mult, ALU.add)
            link(pool.tensor_scalar(turns[:, 1, :], ang[:, 1, :], INV_TWO_PI, 0.25, ALU.mult, ALU.add))
            link(pool.tensor_scalar(turns[:, :, :], turns[:, :, :], MAGIC, None, ALU.add))
            link(pool.tensor_scalar(turns[:, :, :], turns[:, :, :], MAGIC, None, ALU.subtract))
            for share in (TWO_PI_HI, TWO_PI_MID, TWO_PI_LO):
                link(pool.tensor_scalar(part[:, :, :], turns[:, :, :], share, None, ALU.mult))
                link(pool.tensor_tensor(ang[:, :, :], ang[:, :, :], part[:, :, :], ALU.subtract))
            link(pool.tensor_scalar(ang[:, 1, :], ang[:, 1, :], 0.5 * 3.141592653589793, None, ALU.add))
            pool.tensor_scalar(ang[:, :, :], ang[:, :, :], PI, -PI, ALU.min, ALU.max).then_inc(pool_ang, 1)
            pool.wait_ge(dve_idx_h, 1)
            for dst, cache in ((old_k, k_blocks), (old_v, v_blocks)):
                pool.indirect_dma_start(out=dst, out_offset=None, in_=cache.rearrange("n g o d -> n (g o d)"),
                                        in_offset=bass.IndirectOffsetOnAxis(ap=idx_h[0:B * HB, 0:1], axis=0)
                                        ).then_inc(old_in, 16)
            pool.wait_ge(dve_lim, 1)
            for b in range(B):
                pool.tensor_scalar(penalty[:, b, 0, :], iota[:, 0:P], j_min[:, b:b + 1], OUTSIDE,
                                   ALU.is_lt, ALU.mult).then_inc(pool_pen, 1)
                pool.tensor_scalar(penalty[:, b, 1, :], iota[:, (KC - 1) * P:], j_max[:, b:b + 1], OUTSIDE,
                                   ALU.is_gt, ALU.mult).then_inc(pool_pen, 1)
            pool.wait_ge(dve_sel, 1)
            for b in range(B):
                pool.tensor_scalar(a_sel[:, b, :], lora_sb[:, L_A:L_A + D], sel[:, b:b + 1], None,
                                   ALU.mult).then_inc(pool_sel, 1)
            pool.wait_ge(act_old, 2)
            pool.dma_start(kv_rows[NEW:, :].rearrange("(s o) c -> s (o c)", o=BLOCK),
                           old_rows[:, :, :].rearrange("s o c -> s (o c)")).then_inc(old_out, 16)
            pool.wait_ge(dve_rid, 1)
            pool.tensor_tensor(cand[:, :, :], rid[:, :].unsqueeze(2).to_broadcast([P, KC * B, B * NW]),
                               abe_bc[:, 2, :].unsqueeze(1).to_broadcast([P, KC * B, B * NW]),
                               ALU.add).then_inc(pool_cand, 1)
            pool.wait_ge(dve_idx, 1)
            pool.wait_ge(new_out, 32)
            pool.wait_ge(old_out, 16)
            for b in range(B):
                for c in range(KC):
                    pool.indirect_dma_start(out=kv[:, b, c, :], out_offset=None, in_=kv_rows[:, :],
                                            in_offset=bass.IndirectOffsetOnAxis(ap=idx[:, c, b:b + 1], axis=0)
                                            ).then_inc(kv_in[b], 16)
            for b in range(B):
                pool.wait_ge(act_eff, b + 1)
                pool.wait_ge(wrest_in[0], 16)
                pool.tensor_tensor(w_eff[:, b, :, :], w_eff[:, b, :, :], w_rest[:, :, W_1:W_1 + D],
                                   ALU.add).then_inc(pool_eff, 1)
                if b == 0:
                    pool.wait_ge(x_in, 16)
                    pool.wait_ge(row_in, 16)
                    pool.tensor_tensor(x_bias[:, :, :], x_tok[:, :, :],
                                       bias_bc.unsqueeze(1).to_broadcast([P, NT, D]), ALU.add).then_inc(pool_xb, 1)

        @block.scalar
        def _(act):
            act.dma_start(w_qkv[:, :, :], w_qkv_in.rearrange("(c p) d -> p c d", p=P)).then_inc(wqkv_in, 16)
            act.dma_start(tab_r[:, :], dram_view(ints, [[NINT, B], [0, RB], [1, NINT]])).then_inc(tab_r_in, 16)
            act.dma_start(lora_sb[:, :], lora).then_inc(lora_in, 16)

            def kv_copies(b):
                act.wait_ge(pe_kv, b + 1)
                kv_ps = ps_scores[:, b, :].rearrange("p (u c) -> p u c", u=U)
                tiles = slice(U * b, U * b + U)
                nc.scalar.activation(k_sq[:, tiles, :], kv_ps[:, :, 0:P], ACT.Square)
                nc.scalar.copy(k_raw[:, tiles, :], kv_ps[:, :, 0:P]).then_inc(act_kv, 1)
                nc.scalar.copy(kv_new[:, tiles, P:2 * P], kv_ps[:, :, P:2 * P]).then_inc(act_kv, 1)

            def q_copies(b):
                act.wait_ge(pe_q, b + 1)
                q_ps = q_bank[b].rearrange("p (u c) -> p u c", u=U)
                tiles = slice(U * b, U * b + U)
                nc.scalar.activation(q_sq[:, tiles, :], q_ps, ACT.Square)
                nc.scalar.copy(q_raw[:, tiles, :], q_ps).then_inc(act_q, 1)

            for b in range(B):
                kv_copies(b)
            act.wait_ge(pool_ang, 1)
            nc.scalar.activation(trig[:, :, :, :].rearrange("p k n i -> p k (n i)"), ang[:, :, :],
                                 ACT.Sin).then_inc(act_trig, 1)
            act.wait_ge(dve_var, 1)
            nc.scalar.activation(std[:, 0:NT * G], var[:, 0:NT * G], ACT.Sqrt).then_inc(act_std, 1)
            act.wait_ge(old_in, 32)
            for k, old in enumerate((old_k, old_v)):
                nc.scalar.copy(old_rows[:, :, k * P:(k + 1) * P].rearrange("s o (g d) -> s o g d", g=G),
                               old.rearrange("s (g o d) -> s o g d", g=G, o=BLOCK)).then_inc(act_old, 1)
            for b in range(B):
                q_copies(b)
            act.wait_ge(dve_var, 2)
            nc.scalar.activation(std[:, NT * G:], var[:, NT * G:], ACT.Sqrt).then_inc(act_std, 1)
            for b in range(B):
                act.wait_ge(pe_eff, b + 1)
                nc.scalar.copy(w_eff[:, b, :, :].rearrange("p c d -> p (c d)"), eff_bank[b]).then_inc(act_eff, 1)

            def queries(b):
                act.wait_ge(pe_qT, b + 1)
                if b >= 2:
                    act.wait_ge(pe_scores, U * (b - 1))
                nc.scalar.copy(qT[:, b % 2, :, :].rearrange("p i t -> p (i t)"), ps_scores[:, 2, :]).then_inc(act_qT, 1)

            def keys(b):
                act.wait_ge(pe_kT, b + 1)
                nc.scalar.copy(kT[:, b % 2, :], ps_scores[:, 3, 0:KC * P]).then_inc(act_kT, 1)

            def int_weight():
                act.wait_ge(pe_wi, 1)
                nc.scalar.activation(wT_i[:, :, :].rearrange("p c d -> p (c d)"), ps_turn[:, 0, :], ACT.Copy,
                                     bias=-MAGIC).then_inc(act_wi, 1)
                nc.scalar.copy(w_scale_bc[:, :], ps_turn[:, 1, 0:D]).then_inc(act_wi, 1)

            queries(0)
            int_weight()
            keys(0)
            for n in range(NT + 4):
                r = n % 2
                if n < NT:
                    act.wait_ge(pe_scores, n + 1)
                    if n >= 2:
                        act.wait_ge(act_exp, H * (n - 1))
                    nc.scalar.copy(folded[:, r, :, :],
                                   ps_scores[:, :, :].rearrange("p g (i k) -> p (g i) k", i=GS)[:, :, P:2 * P]
                                   ).then_inc(act_fold, 1)
                if 2 <= n < NT + 2:
                    m, q = n - 2, n % 2
                    act.wait_ge(pe_yT, m + 1)
                    if m >= 2:
                        act.wait_ge(pe_z, m - 1)
                    nc.scalar.activation(yT[:, q, :, :].rearrange("p c t -> p (c t)"), ps_b[:, 0:D], ACT.Copy,
                                         bias=-MAGIC).then_inc(act_yT, 1)

                def gate(u):
                    b = n // 2 - 2
                    act.wait_ge(dve_gate, U * b + u + 1)
                    nc.scalar.activation(top_e[:, u, :], top_d[:, u, :], ACT.Exp,
                                         accum_out=top_s[:, u, 0:1]).then_inc(act_gate, 1)

                if n >= 4 and n % 2 == 0:
                    gate(0)
                if n < NT:
                    act.wait_ge(dve_max, n + 1)
                    if n >= 2:
                        act.wait_ge(pe_pT, n - 1)
                        act.wait_ge(dve_probs, n - 1)
                    for h in range(H):
                        nc.scalar.activation(probs[:, r, h, :], folded[:, r, h, :], ACT.Exp,
                                             bias=neg_max[:, r, h:h + 1],
                                             accum_out=den[:, r, h:h + 1]).then_inc(act_exp, 1)
                if 1 <= n <= NT:
                    m, q = n - 1, (n - 1) % 2
                    act.wait_ge(pe_pv, m + 1)
                    if m >= 2:
                        act.wait_ge(pe_y, m - 1)
                    nc.scalar.copy(oT[:, q, :, :].rearrange("p c t -> p (c t)"), ps_a[:, 0:D]).then_inc(act_oT, 1)
                if 2 <= n < NT + 2:
                    m = n - 2
                    act.wait_ge(pe_x1T, m + 1)
                    u, f = m % 2, (m // 2) % 2
                    if m >= 4:
                        act.wait_ge(pe_h, m // 2 - 1)
                    nc.scalar.copy(x1T[:, f, :, u * P:(u + 1) * P],
                                   ps_b[:, 0:D].rearrange("p (c t) -> p c t", c=DC)).then_inc(act_x1T, 1)
                if n >= 4 and n % 2 == 0:
                    gate(1)
                if 3 <= n < NT + 3 and n % 2 == 1:
                    b = (n - 3) // 2
                    act.wait_ge(pe_h, b + 1)
                    if b >= 2:
                        act.wait_ge(pe_out, U * (b - 1))
                    nc.scalar.copy(hT[:, b % 2, :, :].rearrange("p c t -> p (c t)"), ps_scores[:, 0, :]
                                   ).then_inc(act_h, 1)
                    act.wait_ge(pe_u, b + 1)
                    nc.scalar.activation(rT[:, b % 2, :, :].rearrange("p c t -> p (c t)"), ps_scores[:, 1, :],
                                         ACT.Relu).then_inc(act_u, 1)
                if n < NT and n % 2 == 0 and n // 2 + 1 < B:
                    queries(n // 2 + 1)
                    keys(n // 2 + 1)

        @block.vector
        def _(dve):
            chain = [0]

            def link(ins):
                chain[0] += 1
                ins.then_inc(dve_chain, 1)
                dve.wait_ge(dve_chain, chain[0])

            hb = slice(0, B * HB)
            dve.wait_ge(tab_h_in, 16)
            link(dve.tensor_scalar(slot_i[hb, 0:1], tab_h[hb, I_LEN:I_LEN + 1], 4, None, ALU.logical_shift_right))
            dve.wait_ge(consts_in, 16)
            link(dve.tensor_scalar(slot[hb, 0:1], slot_i[hb, 0:1], cst[hb, C_ROWS_H:C_ROWS_H + 1], None, ALU.add))
            dve.wait_ge(pool_iota, 1)
            link(dve.scalar_tensor_tensor(picked[hb, :], iota[hb, 0:NBLK], slot[hb, 0:1], tab_h[hb, 0:NBLK],
                                          ALU.is_equal, ALU.mult, accum_out=blk_h[hb, :]))
            dve.tensor_copy(idx_h[hb, :], blk_h[hb, :]).then_inc(dve_idx_h, 1)

            dve.wait_ge(ints_in, 16)
            dve.tensor_scalar(j_min[:, :], ints_bc[:, :, 0], -1.0, float(WINDOW), ALU.mult, ALU.add)
            dve.tensor_scalar(j_max[:, :], ints_bc[:, :, 0], -1.0, float(S_ALL - 1 + WINDOW), ALU.mult,
                              ALU.add).then_inc(dve_lim, 1)
            dve.wait_ge(lora_in, 16)
            dve.tensor_scalar(sel[:, :], ints_bc[:, :, 1], cst[:, C_ADAPT:C_ADAPT + 1], lora_sb[:, L_S:L_S + 1],
                              ALU.is_equal, ALU.mult).then_inc(dve_sel, 1)

            def col(k):
                return row[:, k:k + 1]

            dve.wait_ge(tab_r_in, 16)
            len_r = tab_r[:, I_LEN:I_LEN + 1]
            dve.tensor_scalar(slot_i[:, 1:2], len_r, 4, None, ALU.logical_shift_right)
            dve.tensor_scalar(slot_i[:, 2:3], len_r, 15, None, ALU.bitwise_and)
            link(dve.tensor_copy(col(R_LEN), len_r))
            link(dve.tensor_scalar(col(R_SLOT), slot_i[:, 1:2], cst[:, C_ROWS:C_ROWS + 1], None, ALU.add))
            dve.scalar_tensor_tensor(picked[:, :], iota[:, 0:NBLK], col(R_SLOT), tab_r[:, 0:NBLK],
                                     ALU.is_equal, ALU.mult, accum_out=col(R_BLK))
            dve.tensor_scalar(col(R_U), slot_i[:, 2:3], -1.0, cst[:, C_ROW16:C_ROW16 + 1], ALU.mult, ALU.add)
            dve.tensor_scalar(col(R_JMIN), col(R_LEN), -1.0, float(WINDOW), ALU.mult, ALU.add)
            link(dve.tensor_scalar(col(R_JMAX), col(R_LEN), -1.0, float(S_ALL - 1 + WINDOW), ALU.mult, ALU.add))
            dve.scalar_tensor_tensor(col(R_V), col(R_BLK), float(BLOCK), col(R_U), ALU.mult, ALU.subtract)
            dve.tensor_scalar(col(R_LO), col(R_U), float(WINDOW), None, ALU.max)
            link(dve.tensor_scalar(col(R_U15), col(R_U), BLOCK - 1.0, None, ALU.add))
            link(dve.tensor_scalar(col(R_HI), col(R_U15), float(KC * P - 1), col(R_JMAX), ALU.min, ALU.min))
            dve.tensor_tensor(abe[:, 0:1], col(R_V), col(R_LO), ALU.add)
            dve.tensor_tensor(abe[:, 1:2], col(R_V), col(R_HI), ALU.add)
            dve.tensor_tensor(abe[:, 2:3], cst[:, C_TOFF:C_TOFF + 1], col(R_V), ALU.subtract).then_inc(dve_rows, 1)
            dve.tensor_scalar(v_diag[:, :], cst[:, C_BMASK:C_BMASK + B], col(R_V), None, ALU.mult).then_inc(dve_rows, 1)
            link(dve.tensor_scalar(j_row[:, :], iota[:, :], col(R_JMIN), col(R_JMAX), ALU.max, ALU.min))
            link(dve.tensor_scalar(in_row[:, :], j_row[:, :], col(R_U), None, ALU.is_ge))
            dve.scalar_tensor_tensor(in_row[:, :], j_row[:, :], col(R_U15), in_row[:, :],
                                     ALU.is_le, ALU.mult).then_inc(dve_rows, 1)
            link(dve.tensor_scalar(low_i[:, :], ints_bc[:, :, 0], 15, None, ALU.bitwise_and))
            dve.tensor_copy(low[:, :], low_i[:, :])
            j_own = cst[:, C_JKEY:C_JKEY + KC].unsqueeze(2).to_broadcast([P, KC, B])
            link(dve.tensor_tensor(j_key[:, :, :], j_own, j_min[:, :].unsqueeze(1).to_broadcast([P, KC, B]), ALU.max))
            link(dve.tensor_tensor(j_key[:, :, :], j_key[:, :, :],
                                   j_max[:, :].unsqueeze(1).to_broadcast([P, KC, B]), ALU.min))
            dve.wait_ge(row_in, 16)
            link(dve.tensor_scalar(qk_scale[:, :, :].rearrange("p k d -> p (k d)"), row_bc[:, F_QS:NFLOAT], 1.0, None,
                                   ALU.add))
            link(dve.tensor_scalar(qk_scale[:, 0, :], qk_scale[:, 0, :], SCALE, None, ALU.mult))

            def tables_of(which, cos_t, sin_t):
                for h in range(2):
                    sc = qk_scale[:, which, h * HALF:(h + 1) * HALF].unsqueeze(1).to_broadcast([P, NT, HALF])
                    other = slice((1 - h) * HALF, (2 - h) * HALF)
                    dve.tensor_tensor(cos_t[:, :, h * HALF:(h + 1) * HALF], trig[:, 1, :, :], sc, ALU.mult)
                    last = dve.tensor_tensor(sin_t[:, :, other], trig[:, 0, :, :], sc, ALU.mult)
                link(last)
                link(dve.tensor_scalar(sin_t[:, :, 0:HALF], sin_t[:, :, 0:HALF], -1.0, None, ALU.mult))

            def variance(sq, seg):
                link(dve.tensor_reduce(var[:, seg], sq[:, :, :].rearrange("p n (h d) -> p (n h) d", d=HD),
                                       AX.X, ALU.add))
                dve.tensor_scalar(var[:, seg], var[:, seg], 1.0 / HD, EPS, ALU.mult, ALU.add).then_inc(dve_var, 1)

            def inverse(seg, done):
                dve.wait_ge(dve_var, done)
                dve.wait_ge(act_std, done)
                link(dve.reciprocal(rstd[:, seg], std[:, seg]))
                link(dve.tensor_tensor(newton[:, seg], rstd[:, seg], rstd[:, seg], ALU.mult))
                link(dve.tensor_tensor(newton[:, seg], newton[:, seg], var[:, seg], ALU.mult))
                link(dve.tensor_scalar(newton[:, seg], newton[:, seg], -0.5, 1.5, ALU.mult, ALU.add))
                link(dve.tensor_tensor(rstd[:, seg], rstd[:, seg], newton[:, seg], ALU.mult))

            def rope(raw, heads, seg0, cos_t, sin_t, n0, nt, dst, signal, count):
                size = nt * heads * HD
                rs = rstd[:, seg0 + n0 * heads:seg0 + (n0 + nt) * heads].unsqueeze(2).to_broadcast([P, nt * heads, HD])
                a2, b2 = (t[:, :, :].rearrange("p n c -> p (n c)")[:, 0:size] for t in (rot_a, rot_b))
                a4, b4 = (t.rearrange("p (n h d) -> p n h d", n=nt, d=HD) for t in (a2, b2))
                link(dve.tensor_tensor(a2.rearrange("p (m d) -> p m d", d=HD),
                                       raw[:, n0:n0 + nt, :].rearrange("p n (h d) -> p (n h) d", d=HD), rs, ALU.mult))
                for h in range(2):
                    here, there = slice(h * HALF, (h + 1) * HALF), slice((1 - h) * HALF, (2 - h) * HALF)
                    sn = sin_t[:, n0:n0 + nt, here].unsqueeze(2).to_broadcast([P, nt, heads, HALF])
                    last = dve.tensor_tensor(b4[:, :, :, here], a4[:, :, :, there], sn, ALU.mult)
                link(last)
                cs = cos_t[:, n0:n0 + nt, :].unsqueeze(2).to_broadcast([P, nt, heads, HD])
                link(dve.tensor_tensor(a4, a4, cs, ALU.mult))
                dve.tensor_tensor(dst[:, n0:n0 + nt, 0:heads * HD].rearrange("p n (h d) -> p n h d", d=HD), a4, b4,
                                  ALU.add).then_inc(signal, 1)
                dve.wait_ge(signal, count)

            k_seg, q_seg = slice(0, NT * G), slice(NT * G, NT * (G + H))
            dve.wait_ge(act_kv, 2 * B)
            variance(k_sq, k_seg)
            dve.wait_ge(act_trig, 1)
            tables_of(1, cos_k, sin_k)
            inverse(k_seg, 1)
            for half in range(2):
                rope(k_raw, G, 0, cos_k, sin_k, 2 * U * half, 2 * U, kv_new, dve_k, half + 1)

            dve.wait_ge(pe_rows, 2)
            dve.tensor_copy(abe_bc[:, :, :].rearrange("p k (b w) -> p k b w", b=B),
                            ps_turn[:, 0, 0:3 * P].rearrange("p (k b w) -> p k b w", k=3, b=B)[:, :, :, W0:W0 + NW])
            dve.tensor_tensor(rid[:, :], ps_turn[:, 1, 0:KC * B], j_key[:, :, :].rearrange("p c b -> p (c b)"),
                              ALU.add).then_inc(dve_rid, 1)
            dve.wait_ge(dve_rid, 1)
            rid_w = rid[:, :].unsqueeze(2).to_broadcast([P, KC * B, B * NW])
            dve.tensor_tensor(m_ge[:, :, :], rid_w, abe_bc[:, 0, :].unsqueeze(1).to_broadcast([P, KC * B, B * NW]),
                              ALU.is_ge)
            link(dve.tensor_tensor(m_le[:, :, :], rid_w,
                                   abe_bc[:, 1, :].unsqueeze(1).to_broadcast([P, KC * B, B * NW]), ALU.is_le))
            link(dve.tensor_tensor(m_ge[:, :, :], m_ge[:, :, :], m_le[:, :, :], ALU.mult))
            dve.wait_ge(pool_cand, 1)
            link(dve.tensor_tensor(m_ge[:, :, :], m_ge[:, :, :], cand[:, :, :], ALU.mult))
            link(dve.tensor_reduce(win[:, :, :].rearrange("p c b -> p (c b)"), m_ge[:, :, :], AX.X, ALU.max))
            dve.tensor_scalar(idx_f[:, :, :], win[:, :, :], -1.0, None, ALU.add)
            dve.tensor_scalar(fall[:, 1, :], win[:, 0, :], 0.0, None, ALU.is_gt)
            link(dve.tensor_tensor(fall[:, 0, :], j_key[:, 0, :], low[:, :], ALU.add))
            link(dve.tensor_tensor(fall[:, 0, :], fall[:, 0, :], cst[:, C_FALL:C_FALL + B], ALU.add))
            link(dve.tensor_tensor(fall[:, 2, :], idx_f[:, 0, :], fall[:, 0, :], ALU.subtract))
            link(dve.tensor_tensor(fall[:, 2, :], fall[:, 2, :], fall[:, 1, :], ALU.mult))
            link(dve.tensor_tensor(idx_f[:, 0, :], fall[:, 2, :], fall[:, 0, :], ALU.add))
            dve.tensor_copy(idx[:, :, :], idx_f[:, :, :]).then_inc(dve_idx, 1)

            tables_of(0, cos_q, sin_q)
            dve.wait_ge(act_q, B)
            variance(q_sq, q_seg)
            inverse(q_seg, 2)

            def rope_q(b):
                rope(q_raw, H, NT * G, cos_q, sin_q, U * b, U, q_rot, dve_q, b + 1)

            rope_q(0)
            dve.wait_ge(wi_in, 16)
            link(dve.tensor_reduce(w_max[:, :], w_i[:, :, :], AX.X, ALU.max, apply_absolute_value=True))
            dve.tensor_scalar(w_scale[:, :], w_max[:, :], 1e-8, 1.0 / QMAX, ALU.max, ALU.mult).then_inc(dve_wscale, 1)
            dve.wait_ge(dve_wscale, 1)
            link(dve.reciprocal(w_inv[:, :], w_scale[:, :]))
            for c in range(DC):
                last = dve.tensor_scalar(w_i[:, c, :], w_i[:, c, :], w_inv[:, c:c + 1], MAGIC, ALU.mult, ALU.add)
            link(last)
            dve.tensor_scalar(w_i[:, :, :], w_i[:, :, :], MAGIC + QMAX, MAGIC - QMAX - 1,
                              ALU.min, ALU.max).then_inc(dve_wround, 1)
            rope_q(1)

            for n in range(NT + 4):
                r = n % 2
                even = n % 2 == 0
                b = n // 2 - 2
                f = b % 2

                def gate_in(u, logits):
                    dve.wait_ge(pe_out, U * b + u + 1)
                    link(dve.max(top[:, u, :], logits))
                    dve.tensor_tensor(top_d[:, u, :], top[:, u, 0:2], top[:, u, 0:1].to_broadcast([P, 2]),
                                      ALU.subtract).then_inc(dve_gate, 1)

                def gate_out(u, expert, shared):
                    dve.wait_ge(act_gate, U * b + u + 1)
                    link(dve.reciprocal(top_s[:, u, 1:2], top_s[:, u, 0:1]))
                    link(dve.tensor_scalar(top_w[:, u, :], top_e[:, u, :], top_s[:, u, 1:2], None, ALU.mult, ALU.add,
                                           accum_out=top_s[:, u, 2:3]))
                    link(dve.scalar_tensor_tensor(moe[:, f, u, :], expert, top_s[:, u, 2:3],
                                                  x1[:, (U * b + u) % 4, :], ALU.mult, ALU.add))
                    if b >= 2:
                        dve.wait_ge(stored[f], 16 * (b // 2))
                    dve.tensor_tensor(y_out[:, f, u, :], moe[:, f, u, :], shared, ALU.add).then_inc(dve_out, 1)

                if 1 <= n <= NT:
                    m, q = n - 1, (n - 1) % 2
                    dve.wait_ge(pe_pT, m + 1)
                    if m >= 2:
                        dve.wait_ge(pe_pv, m - 1)
                    for dst, mask in ((pT_old, C_OLD_T), (pT_new, C_NEW_T)):
                        dve.tensor_tensor(dst[:, q, :, :], ps_turn[:, :, :].rearrange("p k (h t) -> p (k h) t", t=P),
                                          cst[:, mask:mask + P].unsqueeze(1).to_broadcast([P, H, P]),
                                          ALU.mult).then_inc(dve_pT, 1)
                if n < NT:
                    dve.wait_ge(act_fold, n + 1)
                    dve.copy_predicated(folded[:, r, :, :],
                                        cst[:, C_OLD:C_OLD + P].bitcast(U32).unsqueeze(1).to_broadcast([P, H, P]),
                                        ps_scores[:, :, :].rearrange("p g (i k) -> p (g i) k", i=GS)[:, :, 0:P]
                                        ).then_inc(dve_fold, 1)
                    dve.wait_ge(dve_fold, n + 1)
                    if n >= 2:
                        dve.wait_ge(act_exp, H * (n - 1))
                    dve.tensor_reduce(neg_max[:, r, :], folded[:, r, :, :], AX.X, ALU.max,
                                      negate=True).then_inc(dve_max, 1)
                if n >= 4 and even:
                    gate_in(0, ps_turn[:, 0, D:D + N_EXP])
                if 2 <= n < NT + 2:
                    m, q = n - 2, n % 2
                    dve.wait_ge(pe_z, m + 1)
                    if m == 0:
                        dve.wait_ge(act_wi, 2)
                        dve.wait_ge(pool_xb, 1)
                    link(dve.scalar_tensor_tensor(z_tok[:, q, :], ps_b[:, 0:D], y_scale[:, q, 1:2], w_scale_bc[:, :],
                                                  ALU.mult, ALU.mult))
                    dve.tensor_tensor(x1[:, m % 4, :], z_tok[:, q, :], x_bias[:, m, :], ALU.add).then_inc(dve_x1, 1)
                if n >= 4 and even:
                    gate_out(0, ps_turn[:, 0, 0:D], ps_turn[:, 1, 0:D])
                if not even and n // 2 + 2 < B:
                    rope_q(n // 2 + 2)
                if n < NT:
                    dve.wait_ge(act_exp, H * (n + 1))
                    link(dve.reciprocal(rden[:, r, :], den[:, r, :]))
                    dve.tensor_tensor(probs[:, r, :, :], probs[:, r, :, :],
                                      rden[:, r, :].unsqueeze(2).to_broadcast([P, H, P]),
                                      ALU.mult).then_inc(dve_probs, 1)
                if n >= 4 and even:
                    gate_in(1, ps_scores[:, 0, D:D + N_EXP])
                    gate_out(1, ps_scores[:, 0, 0:D], ps_scores[:, 1, 0:D])
                if 1 <= n <= NT:
                    m, q = n - 1, (n - 1) % 2
                    dve.wait_ge(pe_y, m + 1)
                    link(dve.tensor_reduce(y_scale[:, q, 0:1], ps_a[:, 0:D], AX.X, ALU.max, apply_absolute_value=True))
                    link(dve.tensor_scalar(y_scale[:, q, 1:2], y_scale[:, q, 0:1], 1.0 / QMAX, 1e-12,
                                           ALU.mult, ALU.max))
                    link(dve.reciprocal(y_scale[:, q, 2:3], y_scale[:, q, 1:2]))
                    if m >= 2:
                        dve.wait_ge(pe_yT, m - 1)
                    link(dve.tensor_scalar(y_round[:, q, :], ps_a[:, 0:D], y_scale[:, q, 2:3], MAGIC,
                                           ALU.mult, ALU.add))
                    dve.tensor_scalar(y_round[:, q, :], y_round[:, q, :], MAGIC + QMAX, MAGIC - QMAX - 1,
                                      ALU.min, ALU.max).then_inc(dve_yround, 1)

        @block.tensor
        def _(pe):
            def mm(out_, lhsT, rhs, start=True, stop=True):
                return nc.tensor.matmul(out_, lhsT, rhs, start=start, stop=stop)

            def turn(out_, in_):
                return nc.tensor.transpose(out_, in_, ident)

            pe.wait_ge(wqkv_in, 16)
            for b in range(B):
                pe.wait_ge(xT_in[b], 16)
                for u in range(U):
                    for c in range(DC):
                        last = mm(ps_scores[:, b, u * D:(u + 1) * D], xT[:, c, b, u * P:(u + 1) * P],
                                  w_qkv[:, c, W_K:], start=(c == 0), stop=(c == DC - 1))
                last.then_inc(pe_kv, 1)
            pe.wait_ge(consts_in, 16)
            pe.wait_ge(dve_rows, 3)
            for k in range(3):
                last = mm(ps_turn[:, 0, k * P:(k + 1) * P], abe[:, k:k + 1].to_broadcast([P, P]), ident)
            last.then_inc(pe_rows, 1)
            for c in range(KC):
                last = mm(ps_turn[:, 1, c * B:(c + 1) * B], in_row[:, c * P:(c + 1) * P], v_diag[:, :])
            last.then_inc(pe_rows, 1)
            for b in range(B):
                if b >= 2:
                    pe.wait_ge(act_kv, 2 * (b - 1))
                for u in range(U):
                    for c in range(DC):
                        last = mm(q_bank[b][:, u * D:(u + 1) * D], xT[:, c, b, u * P:(u + 1) * P],
                                  w_qkv[:, c, W_Q:W_Q + D], start=(c == 0), stop=(c == DC - 1))
                last.then_inc(pe_q, 1)
            for b in range(B):
                pe.wait_ge(pool_sel, b + 1)
                if b < 2:
                    pe.wait_ge(act_kv, 2 * (b + 3))
                else:
                    pe.wait_ge(act_q, b - 1)
                for c in range(DC):
                    last = mm(eff_bank[b][:, c * D:(c + 1) * D], a_sel[:, b, c * P:(c + 1) * P],
                              lora_sb[:, L_B:L_B + D])
                last.then_inc(pe_eff, 1)

            def queries(b):
                pe.wait_ge(dve_q, b + 1)
                for u in range(U):
                    for i in range(GS):
                        last = turn(ps_scores[:, 2, (i * U + u) * P:(i * U + u + 1) * P],
                                    q_rot[:, U * b + u, i * P:(i + 1) * P])
                last.then_inc(pe_qT, 1)

            def keys(b):
                pe.wait_ge(kv_in[b], 16 * KC)
                for c in range(KC):
                    last = turn(ps_scores[:, 3, c * P:(c + 1) * P], kv[:, b, c, 0:P])
                last.then_inc(pe_kT, 1)

            pe.wait_ge(act_eff, 2)
            queries(0)
            pe.wait_ge(dve_wround, 1)
            pe.wait_ge(dve_rid, 1)
            for c in range(DC):
                for m in range(DC):
                    last = turn(ps_turn[:, 0, (c * DC + m) * P:(c * DC + m + 1) * P], w_i[:, m, c * P:(c + 1) * P])
            for m in range(DC):
                last = mm(ps_turn[:, 1, m * P:(m + 1) * P], w_scale[:, m:m + 1].to_broadcast([P, P]), ident)
            last.then_inc(pe_wi, 1)
            keys(0)
            pe.wait_ge(pool_pen, 2 * B)
            pe.wait_ge(act_q, B)

            def expert_and_gate(u, where_e, where_s, f):
                tok = slice(u * P, (u + 1) * P)
                for c in range(DC):
                    mm(where_s, rT[:, f, c, tok], w_rest[:, c, W_DOWN:W_DOWN + D], start=(c == 0), stop=(c == DC - 1))
                for c in range(DC):
                    last = mm(where_e, hT[:, f, c, tok], w_rest[:, c, W_EXP:W_GATE + N_EXP],
                              start=(c == 0), stop=(c == DC - 1))
                last.then_inc(pe_out, 1)

            for n in range(NT + 4):
                r = n % 2
                even = n % 2 == 0
                if n < NT:
                    b, u = n // U, n % U
                    pe.wait_ge(act_qT, min(b + 1 + u, B))
                    pe.wait_ge(act_kT, min(b + 1 + u, B))
                    if n >= 1:
                        pe.wait_ge(dve_fold, n)
                    if n >= 5 and not even:
                        pe.wait_ge(dve_out, U * (n // 2 - 1))
                    if n >= 4 and even:
                        pe.wait_ge(act_u, n // 2 - 1)
                    for i in range(GS):
                        for g in range(G):
                            mm(ps_scores[:, g, i * 2 * P:(i + 1) * 2 * P],
                               qT[g * HD:(g + 1) * HD, b % 2, i, u * P:(u + 1) * P],
                               kT[g * HD:(g + 1) * HD, b % 2, u * P:(u + 2) * P], stop=False)
                        for g in range(G):
                            where = ps_scores[:, g, (2 * i + u) * P:(2 * i + u + 1) * P]
                            last = mm(where, ones[g * HD:g * HD + 1, :], penalty[g * HD:g * HD + 1, b, u, :],
                                      start=False)
                    last.then_inc(pe_scores, 1)
                if 2 <= n < NT + 2:
                    m, q = n - 2, n % 2
                    pe.wait_ge(dve_yround, m + 1)
                    if m >= 1:
                        pe.wait_ge(act_x1T, m)
                    for c in range(DC):
                        last = turn(ps_b[:, c * P:(c + 1) * P], y_round[:, q, c * P:(c + 1) * P])
                    last.then_inc(pe_yT, 1)
                if n >= 4 and even:
                    b = n // 2 - 2
                    pe.wait_ge(act_u, b + 1)
                    if n <= NT:
                        pe.wait_ge(dve_pT, 2 * n)
                    expert_and_gate(0, ps_turn[:, 0, 0:D + N_EXP], ps_turn[:, 1, 0:D], b % 2)
                if 2 <= n < NT + 2:
                    m, q = n - 2, n % 2
                    pe.wait_ge(act_yT, m + 1)
                    if m == 0:
                        pe.wait_ge(act_wi, 1)
                    for c in range(DC):
                        last = mm(ps_b[:, 0:D], yT[:, q, c, :], wT_i[:, c, :], start=(c == 0), stop=(c == DC - 1))
                    last.then_inc(pe_z, 1)
                if 1 <= n <= NT:
                    m, q = n - 1, (n - 1) % 2
                    b, u = m // U, m % U
                    if m >= 1:
                        pe.wait_ge(dve_yround, m)
                    for k, pT in enumerate((pT_old, pT_new)):
                        pe.wait_ge(dve_pT, 2 * m + k + 1)
                        for g in range(G):
                            last = mm(ps_a[g * HD:(g + 1) * HD, 0:GS * P],
                                      kv[:, b, u + k, P + g * HD:P + (g + 1) * HD],
                                      pT[:, q, g * GS:(g + 1) * GS, :].rearrange("p i t -> p (i t)"),
                                      start=(k == 0), stop=(k == 1))
                    last.then_inc(pe_pv, 1)
                if 2 <= n < NT + 2:
                    m = n - 2
                    pe.wait_ge(dve_x1, m + 1)
                    for c in range(DC):
                        last = turn(ps_b[:, c * P:(c + 1) * P], x1[:, m % 4, c * P:(c + 1) * P])
                    last.then_inc(pe_x1T, 1)
                if n >= 4 and even:
                    b = n // 2 - 2
                    if n < NT:
                        pe.wait_ge(dve_fold, n + 1)
                    expert_and_gate(1, ps_scores[:, 0, 0:D + N_EXP], ps_scores[:, 1, 0:D], b % 2)
                if 1 <= n <= NT:
                    m, q = n - 1, (n - 1) % 2
                    pe.wait_ge(act_oT, m + 1)
                    if m == 0:
                        pe.wait_ge(wrest_in[0], 16)
                    for c in range(DC):
                        last = mm(ps_a[:, 0:D], oT[:, q, c, :], w_rest[:, c, W_O:W_O + D],
                                  start=(c == 0), stop=(c == DC - 1))
                    last.then_inc(pe_y, 1)
                if 3 <= n < NT + 3 and not even:
                    b = (n - 3) // 2
                    pe.wait_ge(act_x1T, U * b + U)
                    pe.wait_ge(pool_eff, b + 1)
                    if n < NT:
                        pe.wait_ge(dve_fold, n + 1)
                    else:
                        pe.wait_ge(dve_out, U * (b - 1))
                    for m in range(DC):
                        for c in range(DC):
                            last = mm(ps_scores[:, 0, m * T:(m + 1) * T], w_eff[:, b, c, m * P:(m + 1) * P],
                                      x1T[:, b % 2, c, :], start=(c == 0), stop=(c == DC - 1))
                    last.then_inc(pe_h, 1)
                if n < NT and even and n // 2 + 1 < B:
                    pe.wait_ge(dve_fold, n + 1)
                    queries(n // 2 + 1)
                    keys(n // 2 + 1)
                if n < NT:
                    pe.wait_ge(dve_probs, n + 1)
                    if n == 0:
                        pe.wait_ge(act_wi, 2)
                    if n >= 4 and even:
                        pe.wait_ge(dve_out, U * (n // 2 - 2) + 1)
                    for h in range(H):
                        last = turn(ps_turn[:, h // 4, (h % 4) * P:(h % 4 + 1) * P], probs[:, r, h, :])
                    last.then_inc(pe_pT, 1)
                if 3 <= n < NT + 3 and not even:
                    b = (n - 3) // 2
                    pe.wait_ge(act_h, b + 1)
                    pe.wait_ge(wrest_in[1], 16)
                    for m in range(DC):
                        for c in range(DC):
                            last = mm(ps_scores[:, 1, m * T:(m + 1) * T],
                                      w_rest[:, c, W_UP + m * P:W_UP + (m + 1) * P],
                                      hT[:, b % 2, c, :], start=(c == 0), stop=(c == DC - 1))
                    last.then_inc(pe_u, 1)


def constants():
    import numpy as np
    c = np.zeros((P, NCONST), np.float32)
    p = np.arange(P)
    c[:, C_IDENT:C_IDENT + P] = np.eye(P)
    c[:, C_OLD:C_OLD + P] = p[None, :] > p[:, None]
    c[:, C_OLD_T:C_OLD_T + P] = p[:, None] > p[None, :]
    c[:, C_NEW_T:C_NEW_T + P] = p[:, None] <= p[None, :]
    c[:, C_BMASK:C_BMASK + B] = p[:, None] // RB == np.arange(B)[None, :]
    c[:, C_JKEY:C_JKEY + KC] = p[:, None] + P * np.arange(KC)[None, :]
    c[:, C_FALL:C_FALL + B] = NEW + HR * np.arange(B)[None, :]
    half = np.arange(HALF, dtype=np.float32) / np.float32(HALF)
    c[:, C_INV:C_INV + HALF] = np.float32(1.0) / np.power(np.float32(10000.0), half)
    c[:, C_POS:C_POS + U] = p[:, None] + P * np.arange(U)[None, :]
    c[:, C_ROW16] = BLOCK * (p % RB)
    c[:, C_ROWS] = p % RB - W0
    c[:, C_TOFF] = T * (p // RB) - WINDOW + 1
    c[:, C_ROWS_H] = p % HB - W0
    c[:, C_ADAPT] = p // RANK
    return c


def layouts(i):
    import numpy as np
    i = {k: np.asarray(v) for k, v in i.items()}
    wq = i["L0_cond_Wq"].reshape(G, GS, HD, D).transpose(1, 0, 2, 3).reshape(D, D)
    wo = i["L0_cond_Wo"].reshape(D, G, GS, HD).transpose(0, 2, 1, 3).reshape(D, D)
    return {
        "x": i["x"],
        "x_turned": i["x"].transpose(0, 2, 1),
        "k_blocks": i["L0_cond_k_blocks"],
        "v_blocks": i["L0_cond_v_blocks"],
        "w_qkv": np.concatenate([wq.T, i["L0_cond_Wk"].T, i["L0_cond_Wv"].T], 1),
        "w_rest": np.concatenate([wo.T, i["L1_cond_W"].T, i["L1_ffn_W_up"].T, i["L1_ffn_W_down"].T,
                                  i["L1_ffn_W_expert"], i["L1_ffn_W_gate"].T], 1),
        "w_int": i["L0_ffn_weight"],
        "lora": np.concatenate([i["L1_cond_A"].reshape(N_ADAPT * RANK, D),
                                i["L1_cond_Bm"].transpose(0, 2, 1).reshape(N_ADAPT * RANK, D),
                                np.repeat(i["L1_cond_scalings"], RANK)[:, None]], 1),
        "ints": np.concatenate([i["itok_Bx257_0_4111"], i["itok_B_37_3939"][:, None], i["itok_B_0_6"][:, None]], 1),
        "floats": np.concatenate([i["L0_ffn_bias"], i["L0_cond_q_norm_scale"], i["L0_cond_k_norm_scale"]]),
        "consts": constants(),
    }


def kernel(**inputs):
    import numpy as np
    import concourse.bacc as bacc
    from concourse.bass_utils import run_bass_kernel_spmd

    nc = bacc.Bacc("TRN2", target_bir_lowering=False, num_devices=1)
    arrays, args = {}, []
    for name, a in layouts(inputs).items():
        a = np.ascontiguousarray(a)
        arrays[f"in_{name}"] = a
        args.append(nc.dram_tensor(f"in_{name}", a.shape, mybir.dt.from_np(a.dtype), kind="ExternalInput").ap())
    args.append(nc.dram_tensor("out_x", (B, T, D), F32, kind="ExternalOutput").ap())
    build(nc, *args)
    r = run_bass_kernel_spmd(nc, [arrays], core_ids=[0])
    return r.results[0]["out_x"]
```

```python
from contextlib import ExitStack

import concourse.bass as bass
from concourse import mybir

F32 = mybir.dt.float32
BF16 = mybir.dt.bfloat16
I32 = mybir.dt.int32
U32 = mybir.dt.uint32
ALU = mybir.AluOpType
ACT = mybir.ActivationFunctionType
AX = mybir.AxisListType

P = 128
B, T, D = 4, 256, 256
U = T // P
NT = B * U
DC = D // P
H, G, HD = 8, 4, 32
GS = H // G
HALF = HD // 2
BLOCK, WINDOW = 16, 128
NBLK = 257
S_ALL = NBLK * BLOCK
KC = (WINDOW + T) // P
RB = 32
W0 = WINDOW // BLOCK
NW = T // BLOCK + 1
HB = WINDOW // BLOCK + 1
HR = HB * BLOCK
NEW = B * T
N_ADAPT, RANK = 8, 16
N_EXP = 8
EPS = 1e-6
SCALE = 256.0 ** -0.5
QMAX = 127.0
MAGIC = 1.5 * 2.0 ** 23
TWO_PI_HI = 6.28125
TWO_PI_MID = 0.0019340515136718750
TWO_PI_LO = 1.2556659146170633e-06
INV_TWO_PI = 0.15915494309189535
PI = 3.1415925
OUTSIDE = -1e38

C_SMALL = 64
C_IDENT = C_SMALL
C_OLD = C_IDENT + P
C_OLD_T = C_OLD + P
C_NEW_T = C_OLD_T + P
NCONST = C_NEW_T + P
C_BMASK = 0
C_JKEY = C_BMASK + B
C_FALL = C_JKEY + KC
C_INV = C_FALL + B
C_POS = C_INV + HALF
C_ROW16 = C_POS + U
C_ROWS = C_ROW16 + 1
C_TOFF = C_ROWS + 1
C_ROWS_H = C_TOFF + 1
C_ADAPT = C_ROWS_H + 1

W_Q, W_K, W_V = 0, D, D + G * HD
W_QKV = W_V + G * HD
W_O, W_1, W_UP, W_DOWN, W_EXP, W_GATE = (k * D for k in range(6))
W_REST = W_GATE + N_EXP

I_LEN, I_ADAPT, NINT = NBLK, NBLK + 1, NBLK + 2
F_QS, F_KS, NFLOAT = D, D + HD, D + 2 * HD
L_A, L_B, L_S, NLORA = 0, D, 2 * D, 2 * D + 1


def build(nc, x, x_turned, k_blocks, v_blocks, w_qkv_in, w_rest_in, w_int, lora, ints, floats, consts, out):
    with ExitStack() as ctx:
        def sb(name, shape, dt=F32):
            return ctx.enter_context(nc.sbuf_tensor(name, shape, dt))

        def sem(name):
            return ctx.enter_context(nc.semaphore(name))

        def dram_view(t, pattern, offset=0):
            return bass.AP(t.tensor, offset, pattern)

        kv_rows = nc.dram_tensor("kv_rows", [NEW + B * HR, 2 * P], F32, kind="Internal").ap()

        ps_scores = ctx.enter_context(nc.psum_tensor("ps_scores", [P, G, GS * 2 * P], F32))
        ps_turn = ctx.enter_context(nc.psum_tensor("ps_turn", [P, 2, 512], F32))
        ps_a = ctx.enter_context(nc.psum_tensor("ps_a", [P, 512], F32))
        ps_b = ctx.enter_context(nc.psum_tensor("ps_b", [P, 512], F32))

        cst = sb("cst", [P, NCONST])
        ident = cst[:, C_IDENT:C_IDENT + P]
        iota = sb("iota", [P, KC * P])
        ones = sb("ones", [P, P], BF16)
        x_tok = sb("x_tok", [P, NT, D])
        xT = sb("xT", [P, DC, B, T])
        w_qkv = sb("w_qkv", [P, DC, W_QKV])
        w_rest = sb("w_rest", [P, DC, W_REST])
        w_i = sb("w_i", [P, DC, D])
        lora_sb = sb("lora_sb", [P, NLORA])
        row_bc = sb("row_bc", [P, NFLOAT])
        bias_bc = row_bc[:, 0:D]
        tab_h = sb("tab_h", [P, NINT], I32)
        tab_r = sb("tab_r", [P, NINT], I32)
        ints_bc = sb("ints_bc", [P, B, 2], I32)

        wT_i = sb("wT_i", [P, DC, D], BF16)
        a_sel = sb("a_sel", [P, B, D])
        w_eff = sb("w_eff", [P, B, DC, D])
        w_max = sb("w_max", [P, DC])
        w_inv = sb("w_inv", [P, DC])
        w_scale = sb("w_scale", [P, DC])
        w_scale_bc = sb("w_scale_bc", [P, D])
        sel = sb("sel", [P, B])
        x_bias = x_tok

        k_raw = sb("k_raw", [P, NT, P])
        k_sq = sb("k_sq", [P, NT, P])
        q_raw = sb("q_raw", [P, NT, D])
        q_sq = sb("q_sq", [P, NT, D])
        q_rot = q_sq
        kv_new = sb("kv_new", [P, NT, 2 * P])
        len_f = sb("len_f", [P, B])
        pos = sb("pos", [P, B, U])
        ang = sb("ang", [P, 2, NT * HALF])
        whole = sb("whole", [P, 2, NT * HALF])
        turns = sb("turns", [P, 3, 2, NT * HALF])
        trig = sb("trig", [P, 2, NT, HALF])
        cos_k, sin_k = sb("cos_k", [P, NT, HD]), sb("sin_k", [P, NT, HD])
        cos_q, sin_q = sb("cos_q", [P, NT, HD]), sb("sin_q", [P, NT, HD])
        qk_scale = sb("qk_scale", [P, 2, HD])
        var = sb("var", [P, NT * (G + H)])
        std = sb("std", [P, NT * (G + H)])
        rstd = sb("rstd", [P, NT * (G + H)])
        newton = sb("newton", [P, NT * (G + H)])
        rot_a = sb("rot_a", [P, 4, D])
        rot_b = sb("rot_b", [P, 4, D])

        slot = sb("slot", [P, 4])
        slot_i = sb("slot_i", [P, 4], I32)
        picked = sb("picked", [P, NBLK])
        blk_h = sb("blk_h", [P, 1])
        idx_h = sb("idx_h", [P, 1], I32)
        row = sb("row", [P, 12])
        (R_LEN, R_SLOT, R_BLK, R_U, R_U15, R_V, R_JMIN, R_JMAX, R_LO, R_HI) = range(10)
        abe = sb("abe", [P, 3])
        j_row = sb("j_row", [P, KC * P])
        in_row = sb("in_row", [P, KC * P])
        v_diag = sb("v_diag", [P, B])
        abe_bc = sb("abe_bc", [P, 3, B * NW])
        j_min, j_max, low = sb("j_min", [P, B]), sb("j_max", [P, B]), sb("low", [P, B])
        low_i = sb("low_i", [P, B], I32)
        j_key = sb("j_key", [P, KC, B])
        rid = sb("rid", [P, KC * B])
        m_ge = sb("m_ge", [P, KC * B, B * NW], BF16)
        m_le = sb("m_le", [P, KC * B, B * NW], BF16)
        cand = sb("cand", [P, KC * B, B * NW])
        win = sb("win", [P, KC, B])
        idx_f = sb("idx_f", [P, KC, B])
        fall = sb("fall", [P, 3, B])
        idx = sb("idx", [P, KC, B], I32)
        penalty = sb("penalty", [P, B, U, P], BF16)

        def view(t, pattern, **dims):
            return t[:, :, :].rearrange("p a b -> p (a b)").rearrange(pattern.replace("(", "p (", 1), **dims)

        kv = sb("kv", [P, B, KC, 2 * P])
        kT = sb("kT", [P, 2, G, KC * P])
        qT = sb("qT", [P, 2, GS, T])
        turned = sb("turned", [P, 2, 2 * H * P])
        pT_old, pT_new = (turned[:, k, :].rearrange("p (r h t) -> p r h t", r=2, h=H) for k in range(2))
        pT_all = sb("pT_all", [P, H, P])
        probs = sb("probs", [P, 2, H, P])
        folded = sb("folded", [P, 2, H, P])
        old_k = folded[0:B * HB, :, :, :].rearrange("s r h t -> s (r h t)")
        old_v = probs[0:B * HB, :, :, :].rearrange("s r h t -> s (r h t)")
        old_rows = turned[0:B * HB, :, :].rearrange("s k (o c) -> s (k o) c", c=2 * P)
        exp_ahead = sb("exp_ahead", [P, 1])
        neg_max = sb("neg_max", [P, 2, H])
        den = sb("den", [P, 2, H])
        rden = sb("rden", [P, 2, H])

        y_round, z_tok = (kv_new[:, 2 * k:2 * k + 2, :] for k in range(2))
        oT = kv_new[:, 6:8, :].rearrange("p r (c t) -> p r c t", c=DC)
        y_scale = sb("y_scale", [P, 2, 3])
        yT = sb("yT", [P, 2, DC, P], BF16)
        x1 = xT[:, 0, :, :]
        y_out = xT[:, 1, :, :].rearrange("p b t -> p (b t)").rearrange("p (r u d) -> p r u d", r=2, u=U)
        x1T = view(k_raw, "(r c t) -> p r c t", r=2, c=DC)
        hT = view(k_sq, "(r c t) -> p r c t", r=2, c=DC)
        rT = view(rot_a, "(r c t) -> p r c t", r=2, c=DC)
        moe = sb("moe", [P, 2, U, D])
        top = sb("top", [P, U, 8])
        top_d = sb("top_d", [P, U, 2])
        top_e = sb("top_e", [P, U, 2])
        top_w = sb("top_w", [P, U, 2])
        top_s = sb("top_s", [P, U, 3])

        consts_in, masks_in, ints_in = sem("consts_in"), sem("masks_in"), sem("ints_in")
        tab_h_in, tab_r_in = sem("tab_h_in"), sem("tab_r_in")
        row_in, wqkv_in, lora_in, wi_in = sem("row_in"), sem("wqkv_in"), sem("lora_in"), sem("wi_in")
        wrest_in = [sem(f"wrest_in{k}") for k in range(2)]
        xT_in = [sem(f"xT_in{b}") for b in range(B)]
        x_in = sem("x_in")
        old_in, old_out, new_out = sem("old_in"), sem("old_out"), sem("new_out")
        kv_in = [sem(f"kv_in{b}") for b in range(B)]
        stored = [sem(f"stored{k}") for k in range(2)]

        pool_iota, pool_ang, act_turns, act_trig = sem("pool_iota"), sem("pool_ang"), sem("act_turns"), sem("act_trig")
        pe_kv, act_kv, pe_q, act_q = sem("pe_kv"), sem("act_kv"), sem("pe_q"), sem("act_q")
        dve_var, act_std = sem("dve_var"), sem("act_std")
        dve_qks, pool_tab_k, pool_tab_q, pool_rot = (
            sem("dve_qks"), sem("pool_tab_k"), sem("pool_tab_q"), sem("pool_rot"))
        dve_k, dve_q, pool_q = sem("dve_k"), sem("dve_q"), sem("pool_q")
        dve_idx_h, act_old = sem("dve_idx_h"), sem("act_old")
        dve_rows, pe_rows, dve_rid, pool_cand, dve_idx = (
            sem("dve_rows"), sem("pe_rows"), sem("dve_rid"), sem("pool_cand"), sem("dve_idx"))
        pool_zero, pool_ones, dve_lim, dve_pen = sem("pool_zero"), sem("pool_ones"), sem("dve_lim"), sem("dve_pen")
        dve_sel, act_sel, pe_eff, act_eff, pool_eff = (
            sem("dve_sel"), sem("act_sel"), sem("pe_eff"), sem("act_eff"), sem("pool_eff"))
        dve_wscale, dve_wround, pe_wi, act_wi = sem("dve_wscale"), sem("dve_wround"), sem("pe_wi"), sem("act_wi")
        pool_xb = sem("pool_xb")
        pe_qT, act_qT, pe_kT, act_kT = sem("pe_qT"), sem("act_qT"), sem("pe_kT"), sem("act_kT")
        pe_scores, act_fold, dve_fold, dve_max = sem("pe_scores"), sem("act_fold"), sem("dve_fold"), sem("dve_max")
        act_exp, dve_probs, pe_pT = sem("act_exp"), sem("dve_probs"), sem("pe_pT")
        act_pT, dve_pT, pool_pT = sem("act_pT"), sem("dve_pT"), sem("pool_pT")
        pe_pv, act_oT, pe_y = sem("pe_pv"), sem("act_oT"), sem("pe_y")
        dve_yround, pe_yT, act_yT, pe_z, dve_x1 = (
            sem("dve_yround"), sem("pe_yT"), sem("act_yT"), sem("pe_z"), sem("dve_x1"))
        pe_x1T, act_x1T, pe_h, act_h, pe_u, act_u = (
            sem("pe_x1T"), sem("act_x1T"), sem("pe_h"), sem("act_h"), sem("pe_u"), sem("act_u"))
        pe_expert, pe_shared = sem("pe_expert"), sem("pe_shared")
        dve_gate, act_gate, dve_out = sem("dve_gate"), sem("act_gate"), sem("dve_out")
        pool_chain, act_chain, dve_chain = sem("pool_chain"), sem("act_chain"), sem("dve_chain")

        q_bank = [ps_a[:, :], ps_b[:, :], ps_scores[:, 0, :], ps_scores[:, 1, :]]
        eff_bank = [ps_turn[:, 0, :], ps_turn[:, 1, :], ps_a[:, :], ps_b[:, :]]

        kT_bank = [ps_a[:, :] if b == 1 else ps_scores[:, 3, :] for b in range(B)]
        qT_bank = [ps_b[:, :] if b in (1, 2) else ps_scores[:, 2, :] for b in range(B)]
        h_bank = [ps_scores[:, 0, :]] * (B - 1) + [ps_scores[:, 2, :]]
        u_bank = [ps_turn[:, 1, :]] * (B - 1) + [ps_scores[:, 3, :]]

        def new_heads(m):
            return H // 2 if m < 3 or m == NT - 1 else H

        def out_banks(b, u):
            if u == 0:
                return ps_scores[:, 0, :], ps_scores[:, 1, :]
            if b == B - 3:
                return ps_scores[:, 2, :], ps_scores[:, 3, :]
            return ps_turn[:, 0, :], ps_turn[:, 1, :]

        block = ctx.enter_context(nc.Block())

        @block.sync
        def _(sp):
            sp.dma_start(tab_h[0:B * HB, :], dram_view(ints, [[NINT, B], [0, HB], [1, NINT]])).then_inc(tab_h_in, 16)
            sp.dma_start(cst[:, 0:C_SMALL], consts[:, 0:C_SMALL]).then_inc(consts_in, 16)
            sp.dma_start(ints_bc[:, :, :], dram_view(ints, [[0, P], [NINT, B], [1, 2]], I_LEN)).then_inc(ints_in, 16)
            sp.dma_start(xT[:, :, 0, :], x_turned[0].rearrange("(c p) t -> p c t", p=P)).then_inc(xT_in[0], 16)
            sp.dma_start(cst[:, C_SMALL:], consts[:, C_SMALL:]).then_inc(masks_in, 16)
            sp.dma_start(xT[:, :, 1, :], x_turned[1].rearrange("(c p) t -> p c t", p=P)).then_inc(xT_in[1], 16)
            sp.dma_start(lora_sb[:, :], lora).then_inc(lora_in, 16)
            for b in range(2, B):
                sp.dma_start(xT[:, :, b, :], x_turned[b].rearrange("(c p) t -> p c t", p=P)).then_inc(xT_in[b], 16)
            sp.dma_start(row_bc[:, :], dram_view(floats, [[0, P], [1, NFLOAT]])).then_inc(row_in, 16)
            sp.dma_start(w_i[:, :, :], w_int.rearrange("(c p) d -> p c d", p=P)).then_inc(wi_in, 16)
            rest = w_rest_in.rearrange("(c p) d -> p c d", p=P)
            sp.dma_start(w_rest[:, :, 0:W_UP], rest[:, :, 0:W_UP]).then_inc(wrest_in[0], 16)
            sp.wait_ge(old_in, 32)
            sp.dma_start(x_tok[:, :, :], x.rearrange("b (u p) d -> p (b u) d", p=P)).then_inc(x_in, 16)
            sp.wait_ge(act_kv, 2 * B)
            rows = kv_rows[0:NEW, :].rearrange("(n p) c -> p n c", p=P)
            sp.dma_start(rows[:, :, P:], kv_new[:, :, P:]).then_inc(new_out, 16)
            sp.dma_start(w_rest[:, :, W_UP:], rest[:, :, W_UP:]).then_inc(wrest_in[1], 16)
            for b in range(B):
                sp.wait_ge(dve_k, b + 1)
                tiles = slice(U * b, U * b + U)
                sp.dma_start(rows[:, tiles, 0:P], kv_new[:, tiles, 0:P]).then_inc(new_out, 16)
            for b in range(B - 1):
                sp.wait_ge(dve_out, U * b + U)
                sp.dma_start(out[b].rearrange("(u p) d -> p u d", p=P), y_out[:, b % 2, :, :]
                             ).then_inc(stored[b % 2], 16)
            for u in range(U):
                sp.wait_ge(dve_out, U * (B - 1) + u + 1)
                sp.dma_start(out[B - 1, u * P:(u + 1) * P, :], y_out[:, (B - 1) % 2, u, :]
                             ).then_inc(stored[(B - 1) % 2], 16)
            sp.wait_ge(stored[0], 16 * (B // 2))
            sp.wait_ge(stored[1], 16 * (B // 2 - 1 + U))

        @block.gpsimd
        def _(pool):
            chain = [0]

            def link(ins):
                chain[0] += 1
                ins.then_inc(pool_chain, 1)
                pool.wait_ge(pool_chain, chain[0])

            pool.iota(iota[:, :], [[1, KC * P]], base=0, channel_multiplier=0,
                      allow_small_or_imprecise_dtypes=True).then_inc(pool_iota, 1)
            pool.memset(ones[:, :], 1.0).then_inc(pool_ones, 1)
            pool.memset(kT[:, :, :, :], 0.0).then_inc(pool_zero, 1)
            pool.wait_ge(ints_in, 16)
            pool.wait_ge(consts_in, 16)
            link(pool.tensor_copy(len_f[:, :], ints_bc[:, :, 0]))
            link(pool.tensor_tensor(pos[:, :, :], len_f[:, :].unsqueeze(2).to_broadcast([P, B, U]),
                                    cst[:, C_POS:C_POS + U].unsqueeze(1).to_broadcast([P, B, U]), ALU.add))
            pos_n = pos[:, :, :].rearrange("p b u -> p (b u)").unsqueeze(2).to_broadcast([P, NT, HALF])
            inv_n = cst[:, C_INV:C_INV + HALF].unsqueeze(1).to_broadcast([P, NT, HALF])
            for k in range(2):
                last = pool.tensor_tensor(ang[:, k, :].rearrange("p (n i) -> p n i", n=NT), pos_n, inv_n, ALU.mult)
            last.then_inc(pool_ang, 1)
            pool.wait_ge(dve_idx_h, 1)
            for dst, cache in ((old_k, k_blocks), (old_v, v_blocks)):
                pool.indirect_dma_start(out=dst, out_offset=None, in_=cache.rearrange("n g o d -> n (g o d)"),
                                        in_offset=bass.IndirectOffsetOnAxis(ap=idx_h[0:B * HB, 0:1], axis=0)
                                        ).then_inc(old_in, 16)
            pool.wait_ge(pool_ang, 1)
            for k in range(3):
                pool.wait_ge(act_turns, k + 1)
                link(pool.tensor_tensor(ang[:, :, :], ang[:, :, :], turns[:, k, :, :], ALU.subtract))
            link(pool.tensor_scalar(ang[:, 1, :], ang[:, 1, :], 0.5 * 3.141592653589793, None, ALU.add))
            pool.tensor_scalar(ang[:, :, :], ang[:, :, :], PI, -PI, ALU.min, ALU.max).then_inc(pool_ang, 1)
            pool.wait_ge(dve_rid, 1)
            pool.tensor_tensor(cand[:, :, :], rid[:, :].unsqueeze(2).to_broadcast([P, KC * B, B * NW]),
                               abe_bc[:, 2, :].unsqueeze(1).to_broadcast([P, KC * B, B * NW]),
                               ALU.add).then_inc(pool_cand, 1)
            pool.wait_ge(act_trig, 1)
            pool.wait_ge(dve_qks, 1)
            for which, cos_t, sin_t, signal in ((1, cos_k, sin_k, pool_tab_k), (0, cos_q, sin_q, pool_tab_q)):
                for h in range(2):
                    sc = qk_scale[:, which, h * HALF:(h + 1) * HALF].unsqueeze(1).to_broadcast([P, NT, HALF])
                    other = slice((1 - h) * HALF, (2 - h) * HALF)
                    pool.tensor_tensor(cos_t[:, :, h * HALF:(h + 1) * HALF], trig[:, 1, :, :], sc, ALU.mult)
                    last = pool.tensor_tensor(sin_t[:, :, other], trig[:, 0, :, :], sc, ALU.mult)
                link(last)
                pool.tensor_scalar(sin_t[:, :, 0:HALF], sin_t[:, :, 0:HALF], -1.0, None, ALU.mult).then_inc(signal, 1)
                if which == 1:
                    pool.wait_ge(act_kv, 2 * B)
                    pool.tensor_tensor(rot_a[:, :, :].rearrange("p n c -> p (n c)").rearrange(
                                           "p (n g d) -> p n g d", n=NT, d=HD),
                                       k_raw[:, :, :].rearrange("p n (g d) -> p n g d", d=HD),
                                       cos_k[:, :, :].unsqueeze(2).to_broadcast([P, NT, G, HD]),
                                       ALU.mult).then_inc(pool_rot, 1)

            def bias(half):
                tiles = slice(half * (NT // 2), (half + 1) * (NT // 2))
                pool.tensor_tensor(x_bias[:, tiles, :], x_tok[:, tiles, :],
                                   bias_bc.unsqueeze(1).to_broadcast([P, NT // 2, D]), ALU.add).then_inc(pool_xb, 1)

            pool.wait_ge(x_in, 16)
            pool.wait_ge(row_in, 16)
            bias(0)
            pool.wait_ge(dve_idx, 1)
            pool.wait_ge(new_out, 16 * (1 + B))
            pool.wait_ge(old_out, 32)
            for b in range(B):
                for c in range(KC):
                    pool.indirect_dma_start(out=kv[:, b, c, :], out_offset=None, in_=kv_rows[:, :],
                                            in_offset=bass.IndirectOffsetOnAxis(ap=idx[:, c, b:b + 1], axis=0)
                                            ).then_inc(kv_in[b], 16)

            def rotate_scale_q(b):
                tiles, at = slice(U * b, U * b + U), b % 2 * U * D
                pool.wait_ge(dve_q, b - 1)
                r4 = q_raw[:, tiles, :].rearrange("p n (h d) -> p n h d", d=HD)
                a2, b2 = (t[:, :, :].rearrange("p n c -> p (n c)")[:, at:at + U * D] for t in (rot_a, rot_b))
                a4, b4 = (t.rearrange("p (n h d) -> p n h d", n=U, d=HD) for t in (a2, b2))
                for h in range(2):
                    here, there = slice(h * HALF, (h + 1) * HALF), slice((1 - h) * HALF, (2 - h) * HALF)
                    pool.tensor_tensor(b4[:, :, :, here], r4[:, :, :, there],
                                       sin_q[:, tiles, here].unsqueeze(2).to_broadcast([P, U, H, HALF]), ALU.mult)
                link(pool.tensor_tensor(a4, r4, cos_q[:, tiles, :].unsqueeze(2).to_broadcast([P, U, H, HD]),
                                        ALU.mult))
                link(pool.tensor_tensor(a2, a2, b2, ALU.add))
                seg = slice(NT * G + U * b * H, NT * G + U * (b + 1) * H)
                rs = rstd[:, seg].unsqueeze(2).to_broadcast([P, U * H, HD])
                pool.tensor_tensor(q_rot[:, tiles, :].rearrange("p n (h d) -> p (n h) d", d=HD),
                                   a2.rearrange("p (m d) -> p m d", d=HD), rs, ALU.mult).then_inc(pool_q, 1)

            pool.wait_ge(dve_q, 2)
            rotate_scale_q(2)
            for m in range(NT):
                q = m % 2
                pool.wait_ge(act_pT, m + 1)
                if m >= 2:
                    pool.wait_ge(pe_pv, m - 1)
                heads = new_heads(m)
                pool.tensor_tensor(pT_new[:, q, 0:heads, :], pT_all[:, 0:heads, :],
                                   cst[:, C_NEW_T:C_NEW_T + P].unsqueeze(1).to_broadcast([P, heads, P]),
                                   ALU.mult).then_inc(pool_pT, 1)
                if m == 0:
                    rotate_scale_q(3)
                if m == 2:
                    bias(1)
                if 1 <= m <= B:
                    pool.wait_ge(act_eff, m)
                    pool.wait_ge(wrest_in[0], 16)
                    pool.tensor_tensor(w_eff[:, m - 1, :, :], w_eff[:, m - 1, :, :], w_rest[:, :, W_1:W_1 + D],
                                       ALU.add).then_inc(pool_eff, 1)

        @block.scalar
        def _(act):
            act.dma_start(tab_r[:, :], dram_view(ints, [[NINT, B], [0, RB], [1, NINT]])).then_inc(tab_r_in, 16)
            act.dma_start(w_qkv[:, :, :], w_qkv_in.rearrange("(c p) d -> p c d", p=P)).then_inc(wqkv_in, 16)
            chain = [0]

            def link(ins):
                chain[0] += 1
                ins.then_inc(act_chain, 1)
                act.wait_ge(act_chain, chain[0])

            act.wait_ge(pool_ang, 1)
            nc.scalar.activation(whole[:, 0, :], ang[:, 0, :], ACT.Copy, scale=INV_TWO_PI)
            link(nc.scalar.activation(whole[:, 1, :], ang[:, 1, :], ACT.Copy, scale=INV_TWO_PI, bias=0.25))
            link(nc.scalar.activation(whole[:, :, :], whole[:, :, :], ACT.Copy, bias=MAGIC))
            link(nc.scalar.activation(whole[:, :, :], whole[:, :, :], ACT.Copy, bias=-MAGIC))
            for k, share in enumerate((TWO_PI_HI, TWO_PI_MID, TWO_PI_LO)):
                nc.scalar.activation(turns[:, k, :, :], whole[:, :, :], ACT.Copy, scale=share).then_inc(act_turns, 1)

            def kv_copies(b):
                act.wait_ge(pe_kv, b + 1)
                kv_ps = ps_scores[:, b, :].rearrange("p (u c) -> p u c", u=U)
                tiles = slice(U * b, U * b + U)
                nc.scalar.activation(k_sq[:, tiles, :], kv_ps[:, :, 0:P], ACT.Square)
                nc.scalar.copy(k_raw[:, tiles, :], kv_ps[:, :, 0:P]).then_inc(act_kv, 1)
                nc.scalar.copy(kv_new[:, tiles, P:2 * P], kv_ps[:, :, P:2 * P]).then_inc(act_kv, 1)

            def q_copies(b):
                act.wait_ge(pe_q, b + 1)
                q_ps = q_bank[b].rearrange("p (u c) -> p u c", u=U)
                tiles = slice(U * b, U * b + U)
                nc.scalar.activation(q_sq[:, tiles, :], q_ps, ACT.Square)
                nc.scalar.copy(q_raw[:, tiles, :], q_ps).then_inc(act_q, 1)

            def queries(b):
                act.wait_ge(pe_qT, b + 1)
                if b >= 2:
                    act.wait_ge(pe_scores, 2 * U * (b - 1))
                nc.scalar.copy(qT[:, b % 2, :, :].rearrange("p i t -> p (i t)"), qT_bank[b]).then_inc(act_qT, 1)

            def keys(b, groups=range(G)):
                act.wait_ge(pe_kT, b + 1)
                if b == 0:
                    act.wait_ge(pool_zero, 1)
                for g in groups:
                    rows = slice(g * HD, (g + 1) * HD)
                    nc.scalar.copy(kT[rows, b % 2, g, :], kT_bank[b][rows, 0:KC * P]).then_inc(act_kT, 1)

            kv_copies(0)
            act.wait_ge(dve_sel, 1)
            for b in range(B):
                nc.scalar.mul(a_sel[:, b, :], lora_sb[:, L_A:L_A + D], sel[:, b:b + 1]).then_inc(act_sel, 1)
            kv_copies(1)
            act.wait_ge(pool_ang, 2)
            nc.scalar.activation(trig[:, :, :, :].rearrange("p k n i -> p k (n i)"), ang[:, :, :],
                                 ACT.Sin).then_inc(act_trig, 1)
            kv_copies(2)
            kv_copies(3)

            def old_part(k, old):
                nc.scalar.copy(old_rows[:, :, k * P:(k + 1) * P].rearrange("s o (g d) -> s o g d", g=G),
                               old.rearrange("s (g o d) -> s o g d", g=G, o=BLOCK)).then_inc(act_old, 1)
                act.wait_ge(act_old, k + 1)
                act.dma_start(kv_rows[NEW:, k * P:(k + 1) * P].rearrange("(s o) c -> s o c", o=BLOCK),
                              old_rows[:, :, k * P:(k + 1) * P]).then_inc(old_out, 16)

            act.wait_ge(old_in, 32)
            old_part(0, old_k)
            act.wait_ge(dve_var, 1)
            nc.scalar.activation(std[:, 0:NT * G], var[:, 0:NT * G], ACT.Sqrt).then_inc(act_std, 1)
            old_part(1, old_v)
            q_copies(0)
            act.wait_ge(dve_var, 2)
            nc.scalar.activation(std[:, NT * G:NT * G + U * H], var[:, NT * G:NT * G + U * H],
                                 ACT.Sqrt).then_inc(act_std, 1)
            for b in range(1, B):
                q_copies(b)

            def adapter_part(b):
                act.wait_ge(pe_eff, b + 1)
                nc.scalar.copy(w_eff[:, b, :, :].rearrange("p c d -> p (c d)"), eff_bank[b]).then_inc(act_eff, 1)

            adapter_part(0)
            adapter_part(1)
            queries(0)
            act.wait_ge(dve_var, 3)
            nc.scalar.activation(std[:, NT * G + U * H:], var[:, NT * G + U * H:], ACT.Sqrt).then_inc(act_std, 1)
            nc.scalar.activation(exp_ahead[:, :], cst[:, 0:1], ACT.Exp)

            def int_weight():
                act.wait_ge(pe_wi, 1)
                nc.scalar.activation(wT_i[:, :, :].rearrange("p c d -> p (c d)"), ps_b[:, :], ACT.Copy,
                                     bias=-MAGIC).then_inc(act_wi, 1)
                nc.scalar.copy(w_scale_bc[:, :], ps_a[:, 0:D]).then_inc(act_wi, 1)

            keys(0)
            adapter_part(2)
            adapter_part(3)

            def fold(n, k):
                act.wait_ge(pe_scores, 2 * n + k + 1)
                if n >= 2:
                    act.wait_ge(act_exp, H * (n - 1))
                nc.scalar.copy(folded[:, n % 2, 4 * k:4 * k + 4, :],
                               ps_scores[:, 2 * k:2 * k + 2, :].rearrange(
                                   "p g (i k) -> p (g i) k", i=GS)[:, :, P:2 * P]).then_inc(act_fold, 1)

            def exps(n, first, end):
                act.wait_ge(dve_max, n + 1)
                if n >= 2:
                    act.wait_ge(pe_pT, n - 1)
                    act.wait_ge(dve_probs, n - 1)
                for h in range(first, end):
                    nc.scalar.activation(probs[:, n % 2, h, :], folded[:, n % 2, h, :], ACT.Exp,
                                         bias=neg_max[:, n % 2, h:h + 1],
                                         accum_out=den[:, n % 2, h:h + 1]).then_inc(act_exp, 1)

            def turned_probs(m):
                act.wait_ge(pe_pT, m + 1)
                if m >= 1:
                    act.wait_ge(dve_pT, m)
                    act.wait_ge(pool_pT, m)
                nc.scalar.copy(pT_all[:, :, :].rearrange("p h t -> p (h t)"),
                               ps_turn[:, :, :].rearrange("p k t -> p (k t)")).then_inc(act_pT, 1)

            def attended(m):
                act.wait_ge(pe_pv, m + 1)
                if m >= 2:
                    act.wait_ge(pe_y, m - 1)
                nc.scalar.copy(oT[:, m % 2, :, :].rearrange("p c t -> p (c t)"), ps_a[:, 0:D]).then_inc(act_oT, 1)

            def turned_rounded(m):
                act.wait_ge(pe_yT, m + 1)
                if m >= 2:
                    act.wait_ge(pe_z, m - 1)
                nc.scalar.activation(yT[:, m % 2, :, :].rearrange("p c t -> p (c t)"), ps_b[:, 0:D], ACT.Copy,
                                     bias=-MAGIC).then_inc(act_yT, 1)

            def turned_x1(m):
                act.wait_ge(pe_x1T, m + 1)
                u, f = m % 2, (m // 2) % 2
                if m >= 4:
                    act.wait_ge(pe_h, m // 2 - 1)
                nc.scalar.copy(x1T[:, f, :, u * P:(u + 1) * P],
                               ps_b[:, 0:D].rearrange("p (c t) -> p c t", c=DC)).then_inc(act_x1T, 1)

            def adapted(b):
                act.wait_ge(pe_h, b + 1)
                if b >= 2:
                    act.wait_ge(pe_shared, U * (b - 1))
                nc.scalar.copy(hT[:, b % 2, :, :].rearrange("p c t -> p (c t)"), h_bank[b]).then_inc(act_h, 1)

            def up(b):
                act.wait_ge(pe_u, b + 1)
                if b == 0:
                    act.wait_ge(pool_q, B - 2)
                nc.scalar.activation(rT[:, b % 2, :, :].rearrange("p c t -> p (c t)"), u_bank[b],
                                     ACT.Relu).then_inc(act_u, 1)

            def gate(b, u):
                act.wait_ge(dve_gate, U * b + u + 1)
                nc.scalar.activation(top_e[:, u, :], top_d[:, u, :], ACT.Exp,
                                     accum_out=top_s[:, u, 0:1]).then_inc(act_gate, 1)

            fold(0, 0)
            fold(0, 1)
            queries(1)
            keys(1)
            exps(0, 0, H // 2)
            fold(1, 0)
            exps(0, H // 2, H)
            fold(1, 1)
            fold(2, 0)
            turned_probs(0)
            exps(1, 0, H // 2)
            fold(2, 1)
            int_weight()
            exps(1, H // 2, H)
            fold(3, 0)
            attended(0)
            queries(2)
            turned_probs(1)
            exps(2, 0, H // 2)
            fold(3, 1)
            exps(2, H // 2, H)
            keys(2)
            turned_rounded(0)
            exps(3, 0, H // 2)
            attended(1)
            exps(3, H // 2, H)
            turned_probs(2)
            fold(4, 0)
            turned_x1(0)
            fold(4, 1)
            turned_rounded(1)
            turned_probs(3)
            attended(2)
            turned_x1(1)
            exps(4, 0, H // 2)
            for n in range(4, NT):
                b = n // U
                if n > 4:
                    fold(n, 0)
                    fold(n, 1)
                    turned_probs(n - 1)
                if n % 2 == 0:
                    adapted(b - 2)
                turned_rounded(n - 2)
                if n > 4:
                    exps(n, 0, H // 2)
                if n % 2 == 0:
                    if b < B - 1:
                        queries(b + 1)
                    up(b - 2)
                    turned_x1(n - 2)
                    exps(n, H // 2, H)
                    attended(n - 1)
                elif b < B - 1:
                    keys(b + 1, range(G // 2))
                    gate(b - 2, 0)
                    keys(b + 1, range(G // 2, G))
                    turned_x1(n - 2)
                    exps(n, H // 2, H)
                    attended(n - 1)
                    gate(b - 2, 1)
                else:
                    exps(n, H // 2, H // 2 + 2)
                    gate(b - 2, 0)
                    exps(n, H // 2 + 2, H)
                    turned_x1(n - 2)
                    attended(n - 1)
                    gate(b - 2, 1)
            turned_probs(NT - 1)
            adapted(B - 2)
            turned_rounded(NT - 2)
            attended(NT - 1)
            turned_x1(NT - 2)
            up(B - 2)
            turned_rounded(NT - 1)
            gate(B - 2, 0)
            turned_x1(NT - 1)
            adapted(B - 1)
            gate(B - 2, 1)
            up(B - 1)
            gate(B - 1, 0)
            gate(B - 1, 1)

        @block.vector
        def _(dve):
            chain = [0]

            def link(ins):
                chain[0] += 1
                ins.then_inc(dve_chain, 1)
                dve.wait_ge(dve_chain, chain[0])

            hb = slice(0, B * HB)
            dve.wait_ge(tab_h_in, 16)
            link(dve.tensor_scalar(slot_i[hb, 0:1], tab_h[hb, I_LEN:I_LEN + 1], 4, None, ALU.logical_shift_right))
            dve.wait_ge(consts_in, 16)
            link(dve.tensor_scalar(slot[hb, 0:1], slot_i[hb, 0:1], cst[hb, C_ROWS_H:C_ROWS_H + 1], None, ALU.add))
            dve.wait_ge(pool_iota, 1)
            link(dve.scalar_tensor_tensor(picked[hb, :], iota[hb, 0:NBLK], slot[hb, 0:1], tab_h[hb, 0:NBLK],
                                          ALU.is_equal, ALU.mult, accum_out=blk_h[hb, :]))
            dve.tensor_copy(idx_h[hb, :], blk_h[hb, :]).then_inc(dve_idx_h, 1)

            dve.wait_ge(ints_in, 16)
            dve.tensor_scalar(j_min[:, :], ints_bc[:, :, 0], -1.0, float(WINDOW), ALU.mult, ALU.add)
            dve.tensor_scalar(j_max[:, :], ints_bc[:, :, 0], -1.0, float(S_ALL - 1 + WINDOW), ALU.mult,
                              ALU.add).then_inc(dve_lim, 1)
            dve.wait_ge(dve_lim, 1)

            def col(k):
                return row[:, k:k + 1]

            dve.wait_ge(tab_r_in, 16)
            len_r = tab_r[:, I_LEN:I_LEN + 1]
            dve.tensor_scalar(slot_i[:, 1:2], len_r, 4, None, ALU.logical_shift_right)
            dve.tensor_scalar(slot_i[:, 2:3], len_r, 15, None, ALU.bitwise_and)
            link(dve.tensor_copy(col(R_LEN), len_r))
            link(dve.tensor_scalar(col(R_SLOT), slot_i[:, 1:2], cst[:, C_ROWS:C_ROWS + 1], None, ALU.add))
            dve.scalar_tensor_tensor(picked[:, :], iota[:, 0:NBLK], col(R_SLOT), tab_r[:, 0:NBLK],
                                     ALU.is_equal, ALU.mult, accum_out=col(R_BLK))
            dve.tensor_scalar(col(R_U), slot_i[:, 2:3], -1.0, cst[:, C_ROW16:C_ROW16 + 1], ALU.mult, ALU.add)
            dve.tensor_scalar(col(R_JMIN), col(R_LEN), -1.0, float(WINDOW), ALU.mult, ALU.add)
            link(dve.tensor_scalar(col(R_JMAX), col(R_LEN), -1.0, float(S_ALL - 1 + WINDOW), ALU.mult, ALU.add))
            dve.scalar_tensor_tensor(col(R_V), col(R_BLK), float(BLOCK), col(R_U), ALU.mult, ALU.subtract)
            dve.tensor_scalar(col(R_LO), col(R_U), float(WINDOW), None, ALU.max)
            link(dve.tensor_scalar(col(R_U15), col(R_U), BLOCK - 1.0, None, ALU.add))
            link(dve.tensor_scalar(col(R_HI), col(R_U15), float(KC * P - 1), col(R_JMAX), ALU.min, ALU.min))
            dve.tensor_tensor(abe[:, 0:1], col(R_V), col(R_LO), ALU.add)
            dve.tensor_tensor(abe[:, 1:2], col(R_V), col(R_HI), ALU.add)
            dve.tensor_tensor(abe[:, 2:3], cst[:, C_TOFF:C_TOFF + 1], col(R_V), ALU.subtract).then_inc(dve_rows, 1)
            dve.tensor_scalar(v_diag[:, :], cst[:, C_BMASK:C_BMASK + B], col(R_V), None, ALU.mult).then_inc(dve_rows, 1)
            link(dve.tensor_scalar(j_row[:, :], iota[:, :], col(R_JMIN), col(R_JMAX), ALU.max, ALU.min))
            link(dve.tensor_scalar(in_row[:, :], j_row[:, :], col(R_U), None, ALU.is_ge))
            dve.scalar_tensor_tensor(in_row[:, :], j_row[:, :], col(R_U15), in_row[:, :],
                                     ALU.is_le, ALU.mult).then_inc(dve_rows, 1)
            link(dve.tensor_scalar(low_i[:, :], ints_bc[:, :, 0], 15, None, ALU.bitwise_and))
            dve.tensor_copy(low[:, :], low_i[:, :])
            j_own = cst[:, C_JKEY:C_JKEY + KC].unsqueeze(2).to_broadcast([P, KC, B])
            link(dve.tensor_tensor(j_key[:, :, :], j_own, j_min[:, :].unsqueeze(1).to_broadcast([P, KC, B]), ALU.max))
            link(dve.tensor_tensor(j_key[:, :, :], j_key[:, :, :],
                                   j_max[:, :].unsqueeze(1).to_broadcast([P, KC, B]), ALU.min))
            dve.wait_ge(row_in, 16)
            link(dve.tensor_scalar(qk_scale[:, :, :].rearrange("p k d -> p (k d)"), row_bc[:, F_QS:NFLOAT], 1.0, None,
                                   ALU.add))
            dve.tensor_scalar(qk_scale[:, 0, :], qk_scale[:, 0, :], SCALE, None, ALU.mult).then_inc(dve_qks, 1)

            dve.wait_ge(lora_in, 16)
            dve.tensor_scalar(sel[:, :], ints_bc[:, :, 1], cst[:, C_ADAPT:C_ADAPT + 1], lora_sb[:, L_S:L_S + 1],
                              ALU.is_equal, ALU.mult).then_inc(dve_sel, 1)

            dve.wait_ge(pe_rows, 2)
            dve.tensor_copy(abe_bc[:, :, :].rearrange("p k (b w) -> p k b w", b=B),
                            ps_turn[:, 0, 0:3 * P].rearrange("p (k b w) -> p k b w", k=3, b=B)[:, :, :, W0:W0 + NW])
            dve.tensor_tensor(rid[:, :], ps_turn[:, 1, 0:KC * B], j_key[:, :, :].rearrange("p c b -> p (c b)"),
                              ALU.add).then_inc(dve_rid, 1)
            dve.wait_ge(dve_rid, 1)
            rid_w = rid[:, :].unsqueeze(2).to_broadcast([P, KC * B, B * NW])
            dve.tensor_tensor(m_ge[:, :, :], rid_w, abe_bc[:, 0, :].unsqueeze(1).to_broadcast([P, KC * B, B * NW]),
                              ALU.is_ge)
            link(dve.tensor_tensor(m_le[:, :, :], rid_w,
                                   abe_bc[:, 1, :].unsqueeze(1).to_broadcast([P, KC * B, B * NW]), ALU.is_le))
            link(dve.tensor_tensor(m_ge[:, :, :], m_ge[:, :, :], m_le[:, :, :], ALU.mult))
            dve.wait_ge(pool_cand, 1)
            link(dve.tensor_tensor(cand[:, :, :], m_ge[:, :, :], cand[:, :, :], ALU.mult))
            link(dve.tensor_reduce(win[:, :, :].rearrange("p c b -> p (c b)"), cand[:, :, :], AX.X, ALU.max))
            dve.tensor_scalar(idx_f[:, :, :], win[:, :, :], -1.0, None, ALU.add)
            dve.tensor_scalar(fall[:, 1, :], win[:, 0, :], 0.0, None, ALU.is_gt)
            link(dve.tensor_tensor(fall[:, 0, :], j_key[:, 0, :], low[:, :], ALU.add))
            link(dve.tensor_tensor(fall[:, 0, :], fall[:, 0, :], cst[:, C_FALL:C_FALL + B], ALU.add))
            link(dve.tensor_tensor(fall[:, 2, :], idx_f[:, 0, :], fall[:, 0, :], ALU.subtract))
            link(dve.tensor_tensor(fall[:, 2, :], fall[:, 2, :], fall[:, 1, :], ALU.mult))
            link(dve.tensor_tensor(idx_f[:, 0, :], fall[:, 2, :], fall[:, 0, :], ALU.add))
            dve.tensor_copy(idx[:, :, :], idx_f[:, :, :]).then_inc(dve_idx, 1)

            def variance(sq, tiles, seg):
                link(dve.tensor_reduce(var[:, seg], sq[:, tiles, :].rearrange("p n (h d) -> p (n h) d", d=HD),
                                       AX.X, ALU.add))
                dve.tensor_scalar(var[:, seg], var[:, seg], 1.0 / HD, EPS, ALU.mult, ALU.add).then_inc(dve_var, 1)

            def inverse(seg, done):
                dve.wait_ge(dve_var, done)
                dve.wait_ge(act_std, done)
                link(dve.reciprocal(rstd[:, seg], std[:, seg]))
                link(dve.tensor_tensor(newton[:, seg], rstd[:, seg], rstd[:, seg], ALU.mult))
                link(dve.scalar_tensor_tensor(newton[:, seg], newton[:, seg], -0.5, var[:, seg], ALU.mult, ALU.mult))
                link(dve.scalar_tensor_tensor(rstd[:, seg], newton[:, seg], 1.5, rstd[:, seg], ALU.add, ALU.mult))

            def rotate(raw, heads, cos_t, sin_t, n0, nt, at):
                size = nt * heads * HD
                r4 = raw[:, n0:n0 + nt, :].rearrange("p n (h d) -> p n h d", d=HD)
                a2, b2 = (t[:, :, :].rearrange("p n c -> p (n c)")[:, at:at + size] for t in (rot_a, rot_b))
                a4, b4 = (t.rearrange("p (n h d) -> p n h d", n=nt, d=HD) for t in (a2, b2))
                for h in range(2):
                    here, there = slice(h * HALF, (h + 1) * HALF), slice((1 - h) * HALF, (2 - h) * HALF)
                    sn = sin_t[:, n0:n0 + nt, here].unsqueeze(2).to_broadcast([P, nt, heads, HALF])
                    last = dve.tensor_tensor(b4[:, :, :, here], r4[:, :, :, there], sn, ALU.mult)
                if cos_t is None:
                    link(last)
                    dve.wait_ge(pool_rot, 1)
                else:
                    cs = cos_t[:, n0:n0 + nt, :].unsqueeze(2).to_broadcast([P, nt, heads, HD])
                    link(dve.tensor_tensor(a4, r4, cs, ALU.mult))
                link(dve.tensor_tensor(a2, a2, b2, ALU.add))
                return a2

            def scale(a2, heads, seg0, n0, nt, dst, signal):
                rs = rstd[:, seg0 + n0 * heads:seg0 + (n0 + nt) * heads].unsqueeze(2).to_broadcast([P, nt * heads, HD])
                dve.tensor_tensor(dst[:, n0:n0 + nt, 0:heads * HD].rearrange("p n (h d) -> p n h d", d=HD),
                                  a2.rearrange("p (n h d) -> p n h d", n=nt, d=HD),
                                  rs.rearrange("p (n h) d -> p n h d", n=nt), ALU.mult).then_inc(signal, 1)

            k_seg = slice(0, NT * G)
            q_seg = (slice(NT * G, NT * G + U * H), slice(NT * G + U * H, NT * (G + H)))
            dve.wait_ge(act_kv, 2 * B)
            variance(k_sq, slice(0, NT), k_seg)
            dve.wait_ge(pool_tab_k, 1)
            k_turned = rotate(k_raw, G, None, sin_k, 0, NT, 0)
            inverse(k_seg, 1)
            for b in range(B):
                scale(k_turned[:, b * U * P:(b + 1) * U * P], G, 0, U * b, U, kv_new, dve_k)

            for b in range(B):
                dve.tensor_scalar(penalty[:, b, 0, :], iota[:, 0:P], j_min[:, b:b + 1], OUTSIDE,
                                  ALU.is_lt, ALU.mult).then_inc(dve_pen, 1)
                dve.tensor_scalar(penalty[:, b, 1, :], iota[:, (KC - 1) * P:], j_max[:, b:b + 1], OUTSIDE,
                                  ALU.is_gt, ALU.mult).then_inc(dve_pen, 1)
            dve.wait_ge(act_q, 1)
            variance(q_sq, slice(0, U), q_seg[0])
            dve.wait_ge(pool_tab_q, 1)

            def rotate_q(b):
                dve.wait_ge(dve_k, 2 * b + 2)
                return rotate(q_raw, H, cos_q, sin_q, U * b, U, b % 2 * U * D)

            def scale_q(b, q_turned):
                scale(q_turned, H, NT * G, U * b, U, q_rot, dve_q)

            q_turned = rotate_q(0)
            inverse(q_seg[0], 2)
            scale_q(0, q_turned)
            dve.wait_ge(act_q, B)
            variance(q_sq, slice(U, NT), q_seg[1])

            def int_weight():
                dve.wait_ge(wi_in, 16)
                link(dve.tensor_reduce(w_max[:, :], w_i[:, :, :], AX.X, ALU.max, apply_absolute_value=True))
                dve.tensor_scalar(w_scale[:, :], w_max[:, :], 1e-8, 1.0 / QMAX, ALU.max,
                                  ALU.mult).then_inc(dve_wscale, 1)
                dve.wait_ge(dve_wscale, 1)
                link(dve.reciprocal(w_inv[:, :], w_scale[:, :]))
                for c in range(DC):
                    last = dve.tensor_scalar(w_i[:, c, :], w_i[:, c, :], w_inv[:, c:c + 1], MAGIC, ALU.mult, ALU.add)
                link(last)
                dve.tensor_scalar(w_i[:, :, :], w_i[:, :, :], MAGIC + QMAX, MAGIC - QMAX - 1,
                                  ALU.min, ALU.max).then_inc(dve_wround, 1)

            int_weight()
            inverse(q_seg[1], 3)
            scale_q(1, rotate_q(1))

            def quantise(m):
                q = m % 2
                dve.wait_ge(pe_y, m + 1)
                link(dve.tensor_reduce(y_scale[:, q, 0:1], ps_a[:, 0:D], AX.X, ALU.max, apply_absolute_value=True))
                link(dve.tensor_scalar(y_scale[:, q, 1:2], y_scale[:, q, 0:1], 1.0 / QMAX, 1e-12,
                                       ALU.mult, ALU.max))
                link(dve.reciprocal(y_scale[:, q, 2:3], y_scale[:, q, 1:2]))
                if m >= 2:
                    dve.wait_ge(pe_yT, m - 1)
                link(dve.tensor_scalar(y_round[:, q, :], ps_a[:, 0:D], y_scale[:, q, 2:3], MAGIC,
                                       ALU.mult, ALU.add))
                dve.tensor_scalar(y_round[:, q, :], y_round[:, q, :], MAGIC + QMAX, MAGIC - QMAX - 1,
                                  ALU.min, ALU.max).then_inc(dve_yround, 1)

            def fold(n, k):
                dve.wait_ge(act_fold, 2 * n + k + 1)
                dve.copy_predicated(folded[:, n % 2, 4 * k:4 * k + 4, :],
                                    cst[:, C_OLD:C_OLD + P].bitcast(U32).unsqueeze(1).to_broadcast([P, H // 2, P]),
                                    ps_scores[:, 2 * k:2 * k + 2, :].rearrange(
                                        "p g (i k) -> p (g i) k", i=GS)[:, :, 0:P]).then_inc(dve_fold, 1)

            def maximum(n):
                dve.wait_ge(dve_fold, 2 * n + 2)
                if n >= 2:
                    dve.wait_ge(act_exp, H * (n - 1))
                dve.tensor_reduce(neg_max[:, n % 2, :], folded[:, n % 2, :, :], AX.X, ALU.max,
                                  negate=True).then_inc(dve_max, 1)

            def normalise(m):
                q = m % 2
                dve.wait_ge(act_exp, H * (m + 1))
                link(dve.reciprocal(rden[:, q, :], den[:, q, :]))
                dve.tensor_tensor(probs[:, q, :, :], probs[:, q, :, :],
                                  rden[:, q, :].unsqueeze(2).to_broadcast([P, H, P]), ALU.mult).then_inc(dve_probs, 1)

            def mask_old(m):
                dve.wait_ge(act_pT, m + 1)
                if m >= 2:
                    dve.wait_ge(pe_pv, m - 1)
                last = dve.tensor_tensor(pT_old[:, m % 2, :, :], pT_all[:, :, :],
                                         cst[:, C_OLD_T:C_OLD_T + P].unsqueeze(1).to_broadcast([P, H, P]), ALU.mult)
                heads = new_heads(m)
                if heads < H:
                    last = dve.tensor_tensor(pT_new[:, m % 2, heads:, :], pT_all[:, heads:, :],
                                             cst[:, C_NEW_T:C_NEW_T + P].unsqueeze(1).to_broadcast([P, H - heads, P]),
                                             ALU.mult)
                last.then_inc(dve_pT, 1)

            def residual(m):
                q = m % 2
                dve.wait_ge(pe_z, m + 1)
                if m == 0:
                    dve.wait_ge(act_wi, 2)
                if m % (NT // 2) == 0:
                    dve.wait_ge(pool_xb, m // (NT // 2) + 1)
                link(dve.scalar_tensor_tensor(z_tok[:, q, :], ps_b[:, 0:D], y_scale[:, q, 1:2], w_scale_bc[:, :],
                                              ALU.mult, ALU.mult))
                dve.tensor_tensor(x1[:, m % 4, :], z_tok[:, q, :], x_bias[:, m, :], ALU.add).then_inc(dve_x1, 1)

            def gate_in(b, u):
                dve.wait_ge(pe_expert, U * b + u + 1)
                link(dve.max(top[:, u, :], out_banks(b, u)[0][:, D:D + N_EXP]))
                dve.tensor_tensor(top_d[:, u, :], top[:, u, 0:2], top[:, u, 0:1].to_broadcast([P, 2]),
                                  ALU.subtract).then_inc(dve_gate, 1)

            def gate_out(b, u):
                f = b % 2
                expert, shared = (bank[:, 0:D] for bank in out_banks(b, u))
                dve.wait_ge(act_gate, U * b + u + 1)
                link(dve.reciprocal(top_s[:, u, 1:2], top_s[:, u, 0:1]))
                link(dve.tensor_scalar(top_w[:, u, :], top_e[:, u, :], top_s[:, u, 1:2], None, ALU.mult, ALU.add,
                                       accum_out=top_s[:, u, 2:3]))
                link(dve.scalar_tensor_tensor(moe[:, f, u, :], expert, top_s[:, u, 2:3],
                                              x1[:, (U * b + u) % 4, :], ALU.mult, ALU.add))
                dve.wait_ge(pe_shared, U * b + u + 1)
                if b >= 2:
                    dve.wait_ge(stored[f], 16 * (b // 2))
                dve.tensor_tensor(y_out[:, f, u, :], moe[:, f, u, :], shared, ALU.add).then_inc(dve_out, 1)

            fold(0, 0)
            fold(0, 1)
            maximum(0)
            fold(1, 0)
            normalise(0)
            fold(1, 1)
            maximum(1)
            fold(2, 0)
            mask_old(0)
            fold(2, 1)
            maximum(2)
            normalise(1)
            fold(3, 0)
            mask_old(1)
            fold(3, 1)
            quantise(0)
            maximum(3)
            normalise(2)
            residual(0)
            normalise(3)
            quantise(1)
            fold(4, 0)
            mask_old(2)
            fold(4, 1)
            residual(1)
            maximum(4)
            for n in range(4, NT):
                b = n // U
                if n > 4:
                    normalise(n - 1)
                if n >= 6 and n % 2 == 0:
                    gate_out(b - 3, 1)
                if n > 4:
                    fold(n, 0)
                quantise(n - 2)
                if n > 4:
                    fold(n, 1)
                    maximum(n)
                mask_old(n - 1)
                residual(n - 2)
                if n % 2 == 1:
                    gate_in(b - 2, 0)
                    gate_out(b - 2, 0)
                    gate_in(b - 2, 1)
            normalise(NT - 1)
            quantise(NT - 2)
            mask_old(NT - 1)
            residual(NT - 2)
            gate_out(B - 3, 1)
            quantise(NT - 1)
            gate_in(B - 2, 0)
            residual(NT - 1)
            gate_out(B - 2, 0)
            gate_in(B - 2, 1)
            gate_out(B - 2, 1)
            gate_in(B - 1, 0)
            gate_in(B - 1, 1)
            gate_out(B - 1, 0)
            gate_out(B - 1, 1)

        @block.tensor
        def _(pe):
            def mm(out_, lhsT, rhs, start=True, stop=True):
                return nc.tensor.matmul(out_, lhsT, rhs, start=start, stop=stop)

            def turn(out_, in_):
                return nc.tensor.transpose(out_, in_, ident)

            def keys_values(b):
                pe.wait_ge(xT_in[b], 16)
                for u in range(U):
                    for c in range(DC):
                        last = mm(ps_scores[:, b, u * D:(u + 1) * D], xT[:, c, b, u * P:(u + 1) * P],
                                  w_qkv[:, c, W_K:], start=(c == 0), stop=(c == DC - 1))
                last.then_inc(pe_kv, 1)

            pe.wait_ge(wqkv_in, 16)
            keys_values(0)
            pe.wait_ge(masks_in, 16)
            pe.wait_ge(dve_rows, 3)
            for k in range(3):
                last = mm(ps_turn[:, 0, k * P:(k + 1) * P], abe[:, k:k + 1].to_broadcast([P, P]), ident)
            last.then_inc(pe_rows, 1)
            for c in range(KC):
                last = mm(ps_turn[:, 1, c * B:(c + 1) * B], in_row[:, c * P:(c + 1) * P], v_diag[:, :])
            last.then_inc(pe_rows, 1)
            for b in range(1, B):
                keys_values(b)
            for b in range(B):
                if b >= 2:
                    pe.wait_ge(act_kv, 2 * (b - 1))
                for u in range(U):
                    for c in range(DC):
                        last = mm(q_bank[b][:, u * D:(u + 1) * D], xT[:, c, b, u * P:(u + 1) * P],
                                  w_qkv[:, c, W_Q:W_Q + D], start=(c == 0), stop=(c == DC - 1))
                last.then_inc(pe_q, 1)

            def queries(b):
                if b < 2:
                    pe.wait_ge(dve_q, b + 1)
                else:
                    pe.wait_ge(pool_q, b - 1)
                if b == 1:
                    pe.wait_ge(act_eff, B)
                if b == 2:
                    pe.wait_ge(act_wi, 1)
                for u in range(U):
                    for i in range(GS):
                        last = turn(qT_bank[b][:, (i * U + u) * P:(i * U + u + 1) * P],
                                    q_rot[:, U * b + u, i * P:(i + 1) * P])
                last.then_inc(pe_qT, 1)

            def keys(b):
                pe.wait_ge(kv_in[b], 16 * KC)
                for c in range(KC):
                    last = turn(kT_bank[b][:, c * P:(c + 1) * P], kv[:, b, c, 0:P])
                last.then_inc(pe_kT, 1)

            def adapter(b):
                pe.wait_ge(act_sel, b + 1)
                if b < 2:
                    pe.wait_ge(dve_rid, 1)
                else:
                    pe.wait_ge(act_q, b - 1)
                for c in range(DC):
                    last = mm(eff_bank[b][:, c * D:(c + 1) * D], a_sel[:, b, c * P:(c + 1) * P],
                              lora_sb[:, L_B:L_B + D])
                last.then_inc(pe_eff, 1)

            adapter(0)
            adapter(1)
            pe.wait_ge(act_kv, 2 * B)
            queries(0)
            adapter(2)
            adapter(3)
            keys(0)
            pe.wait_ge(dve_pen, 2 * B)
            pe.wait_ge(pool_ones, 1)
            pe.wait_ge(act_q, B)

            def int_weight():
                pe.wait_ge(dve_wround, 1)
                pe.wait_ge(act_qT, 2)
                pe.wait_ge(act_kT, 2 * G)
                for c in range(DC):
                    for m in range(DC):
                        last = turn(ps_b[:, (c * DC + m) * P:(c * DC + m + 1) * P],
                                    w_i[:, m, c * P:(c + 1) * P])
                for m in range(DC):
                    last = mm(ps_a[:, m * P:(m + 1) * P], w_scale[:, m:m + 1].to_broadcast([P, P]), ident)
                last.then_inc(pe_wi, 1)

            def scores(n, k):
                b, u = n // U, n % U
                pe.wait_ge(act_qT, B if (n, k) == (5, 1) else b + 1)
                if n >= 6 and u == 0:
                    pe.wait_ge(dve_out, U * (b - 3) + 1)
                if n >= 5 and u == 1:
                    pe.wait_ge(act_h, b - 1)
                if n >= 1:
                    pe.wait_ge(dve_fold, 2 * n - 1 + k)
                if k == 1:
                    pe.wait_ge(act_kT, G * (b + 1))
                for g in (2 * k, 2 * k + 1):
                    pe.wait_ge(act_kT, G * b + g + 1)
                    for i in range(GS):
                        mm(ps_scores[:, g, i * 2 * P:(i + 1) * 2 * P], qT[:, b % 2, i, u * P:(u + 1) * P],
                           kT[:, b % 2, g, u * P:(u + 2) * P], stop=False)
                        where = ps_scores[:, g, (2 * i + u) * P:(2 * i + u + 1) * P]
                        last = mm(where, ones[g * HD:g * HD + 1, :], penalty[g * HD:g * HD + 1, b, u, :],
                                  start=False)
                last.then_inc(pe_scores, 1)

            def turn_probs(m):
                pe.wait_ge(dve_probs, m + 1)
                if m == 0:
                    pe.wait_ge(act_eff, B)
                else:
                    pe.wait_ge(act_pT, m)
                if m == 5:
                    pe.wait_ge(dve_out, U)
                if m >= 4 and m % 2 == 0:
                    pe.wait_ge(act_u, m // 2 - 1)
                for h in range(H):
                    last = turn(ps_turn[:, h // 4, (h % 4) * P:(h % 4 + 1) * P], probs[:, m % 2, h, :])
                last.then_inc(pe_pT, 1)

            def attend(m):
                b, u = m // U, m % U
                if m == 0:
                    pe.wait_ge(act_wi, 2)
                else:
                    pe.wait_ge(dve_yround, m)
                for k, (pT, ready) in enumerate(((pT_old, dve_pT), (pT_new, pool_pT))):
                    pe.wait_ge(ready, m + 1)
                    for g in range(G):
                        last = mm(ps_a[g * HD:(g + 1) * HD, 0:GS * P],
                                  kv[:, b, u + k, P + g * HD:P + (g + 1) * HD],
                                  pT[:, m % 2, g * GS:(g + 1) * GS, :].rearrange("p i t -> p (i t)"),
                                  start=(k == 0), stop=(k == 1))
                last.then_inc(pe_pv, 1)

            def output(m):
                pe.wait_ge(act_oT, m + 1)
                if m == 0:
                    pe.wait_ge(wrest_in[0], 16)
                for c in range(DC):
                    last = mm(ps_a[:, 0:D], oT[:, m % 2, c, :], w_rest[:, c, W_O:W_O + D],
                              start=(c == 0), stop=(c == DC - 1))
                last.then_inc(pe_y, 1)

            def turn_rounded(m):
                pe.wait_ge(dve_yround, m + 1)
                if m == 0:
                    pe.wait_ge(act_qT, 3)
                else:
                    pe.wait_ge(act_x1T, m)
                for c in range(DC):
                    last = turn(ps_b[:, c * P:(c + 1) * P], y_round[:, m % 2, c * P:(c + 1) * P])
                last.then_inc(pe_yT, 1)

            def int_product(m):
                pe.wait_ge(act_yT, m + 1)
                for c in range(DC):
                    last = mm(ps_b[:, 0:D], yT[:, m % 2, c, :], wT_i[:, c, :], start=(c == 0), stop=(c == DC - 1))
                last.then_inc(pe_z, 1)

            def turn_x1(m):
                pe.wait_ge(dve_x1, m + 1)
                for c in range(DC):
                    last = turn(ps_b[:, c * P:(c + 1) * P], x1[:, m % 4, c * P:(c + 1) * P])
                last.then_inc(pe_x1T, 1)

            def adapted(b):
                pe.wait_ge(act_x1T, U * b + U)
                pe.wait_ge(pool_eff, b + 1)
                if b < B - 2:
                    pe.wait_ge(dve_fold, 4 * b + 9)
                else:
                    pe.wait_ge(dve_out, U * (B - 3) + b - (B - 3))
                for m in range(DC):
                    for c in range(DC):
                        last = mm(h_bank[b][:, m * T:(m + 1) * T], w_eff[:, b, c, m * P:(m + 1) * P],
                                  x1T[:, b % 2, c, :], start=(c == 0), stop=(c == DC - 1))
                last.then_inc(pe_h, 1)

            def up(b):
                pe.wait_ge(act_h, b + 1)
                pe.wait_ge(wrest_in[1], 16)
                if b < B - 1:
                    pe.wait_ge(act_pT, U * b + 4)
                for m in range(DC):
                    for c in range(DC):
                        last = mm(u_bank[b][:, m * T:(m + 1) * T], w_rest[:, c, W_UP + m * P:W_UP + (m + 1) * P],
                                  hT[:, b % 2, c, :], start=(c == 0), stop=(c == DC - 1))
                last.then_inc(pe_u, 1)

            def expert(b, u):
                pe.wait_ge(wrest_in[1], 16)
                pe.wait_ge(act_h, b + 1)
                n = U * b + 5
                if b == B - 2 and u == 1:
                    pe.wait_ge(act_pT, NT)
                if n < NT:
                    pe.wait_ge(dve_fold, 2 * n + 1 + u)
                    if u == 1 and b < B - 3:
                        pe.wait_ge(act_pT, n)
                elif b == B - 1:
                    pe.wait_ge(dve_out, U * b - 1 + u)
                where, tok = out_banks(b, u)[0], slice(u * P, (u + 1) * P)
                for c in range(DC):
                    last = mm(where[:, 0:D + N_EXP], hT[:, b % 2, c, tok], w_rest[:, c, W_EXP:W_GATE + N_EXP],
                              start=(c == 0), stop=(c == DC - 1))
                last.then_inc(pe_expert, 1)

            def shared(b, u):
                pe.wait_ge(act_u, b + 1)
                where, tok = out_banks(b, u)[1], slice(u * P, (u + 1) * P)
                for c in range(DC):
                    last = mm(where[:, 0:D], rT[:, b % 2, c, tok], w_rest[:, c, W_DOWN:W_DOWN + D],
                              start=(c == 0), stop=(c == DC - 1))
                last.then_inc(pe_shared, 1)

            scores(0, 0)
            scores(0, 1)
            queries(1)
            keys(1)
            scores(1, 0)
            scores(1, 1)
            scores(2, 0)
            turn_probs(0)
            scores(2, 1)
            int_weight()
            scores(3, 0)
            attend(0)
            queries(2)
            turn_probs(1)
            scores(3, 1)
            output(0)
            pe.wait_ge(dve_fold, 8)
            keys(2)
            turn_rounded(0)
            attend(1)
            int_product(0)
            scores(4, 0)
            turn_probs(2)
            output(1)
            turn_x1(0)
            scores(4, 1)
            turn_rounded(1)
            turn_probs(3)
            attend(2)
            int_product(1)
            output(2)
            turn_x1(1)
            for n in range(4, NT):
                b = n // U
                if n > 4:
                    scores(n, 0)
                    output(n - 2)
                    scores(n, 1)
                    turn_probs(n - 1)
                if n % 2 == 0:
                    adapted(b - 2)
                    turn_rounded(n - 2)
                    int_product(n - 2)
                    if b < B - 1:
                        pe.wait_ge(dve_fold, 2 * n + 2)
                        queries(b + 1)
                    up(b - 2)
                else:
                    turn_rounded(n - 2)
                    expert(b - 2, 0)
                    shared(b - 2, 0)
                    int_product(n - 2)
                    if b < B - 1:
                        pe.wait_ge(dve_fold, 2 * n + 2)
                        keys(b + 1)
                    expert(b - 2, 1)
                    shared(b - 2, 1)
                turn_x1(n - 2)
                attend(n - 1)
            output(NT - 2)
            turn_probs(NT - 1)
            adapted(B - 2)
            turn_rounded(NT - 2)
            int_product(NT - 2)
            attend(NT - 1)
            turn_x1(NT - 2)
            output(NT - 1)
            up(B - 2)
            turn_rounded(NT - 1)
            expert(B - 2, 0)
            int_product(NT - 1)
            shared(B - 2, 0)
            turn_x1(NT - 1)
            shared(B - 2, 1)
            adapted(B - 1)
            expert(B - 2, 1)
            up(B - 1)
            expert(B - 1, 0)
            expert(B - 1, 1)
            shared(B - 1, 0)
            shared(B - 1, 1)


def constants():
    import numpy as np
    c = np.zeros((P, NCONST), np.float32)
    p = np.arange(P)
    c[:, C_IDENT:C_IDENT + P] = np.eye(P)
    c[:, C_OLD:C_OLD + P] = p[None, :] > p[:, None]
    c[:, C_OLD_T:C_OLD_T + P] = p[:, None] > p[None, :]
    c[:, C_NEW_T:C_NEW_T + P] = p[:, None] <= p[None, :]
    c[:, C_BMASK:C_BMASK + B] = p[:, None] // RB == np.arange(B)[None, :]
    c[:, C_JKEY:C_JKEY + KC] = p[:, None] + P * np.arange(KC)[None, :]
    c[:, C_FALL:C_FALL + B] = NEW + HR * np.arange(B)[None, :]
    half = np.arange(HALF, dtype=np.float32) / np.float32(HALF)
    c[:, C_INV:C_INV + HALF] = np.float32(1.0) / np.power(np.float32(10000.0), half)
    c[:, C_POS:C_POS + U] = p[:, None] + P * np.arange(U)[None, :]
    c[:, C_ROW16] = BLOCK * (p % RB)
    c[:, C_ROWS] = p % RB - W0
    c[:, C_TOFF] = T * (p // RB) - WINDOW + 1
    c[:, C_ROWS_H] = p % HB - W0
    c[:, C_ADAPT] = p // RANK
    return c


def layouts(i):
    import numpy as np
    i = {k: np.asarray(v) for k, v in i.items()}
    wq = i["L0_cond_Wq"].reshape(G, GS, HD, D).transpose(1, 0, 2, 3).reshape(D, D)
    wo = i["L0_cond_Wo"].reshape(D, G, GS, HD).transpose(0, 2, 1, 3).reshape(D, D)
    return {
        "x": i["x"],
        "x_turned": i["x"].transpose(0, 2, 1),
        "k_blocks": i["L0_cond_k_blocks"],
        "v_blocks": i["L0_cond_v_blocks"],
        "w_qkv": np.concatenate([wq.T, i["L0_cond_Wk"].T, i["L0_cond_Wv"].T], 1),
        "w_rest": np.concatenate([wo.T, i["L1_cond_W"].T, i["L1_ffn_W_up"].T, i["L1_ffn_W_down"].T,
                                  i["L1_ffn_W_expert"], i["L1_ffn_W_gate"].T], 1),
        "w_int": i["L0_ffn_weight"],
        "lora": np.concatenate([i["L1_cond_A"].reshape(N_ADAPT * RANK, D),
                                i["L1_cond_Bm"].transpose(0, 2, 1).reshape(N_ADAPT * RANK, D),
                                np.repeat(i["L1_cond_scalings"], RANK)[:, None]], 1),
        "ints": np.concatenate([i["itok_Bx257_0_4111"], i["itok_B_37_3939"][:, None], i["itok_B_0_6"][:, None]], 1),
        "floats": np.concatenate([i["L0_ffn_bias"], i["L0_cond_q_norm_scale"], i["L0_cond_k_norm_scale"]]),
        "consts": constants(),
    }


def kernel(**inputs):
    import numpy as np
    import concourse.bacc as bacc
    from concourse.bass_utils import run_bass_kernel_spmd

    nc = bacc.Bacc("TRN2", target_bir_lowering=False, num_devices=1)
    arrays, args = {}, []
    for name, a in layouts(inputs).items():
        a = np.ascontiguousarray(a)
        arrays[f"in_{name}"] = a
        args.append(nc.dram_tensor(f"in_{name}", a.shape, mybir.dt.from_np(a.dtype), kind="ExternalInput").ap())
    args.append(nc.dram_tensor("out_x", (B, T, D), F32, kind="ExternalOutput").ap())
    build(nc, *args)
    r = run_bass_kernel_spmd(nc, [arrays], core_ids=[0])
    return r.results[0]["out_x"]
```
